# Optimizing a Trainium2 kernel written in Bass

```python
import numpy as np
import jax
import jax.numpy as jnp

def _softmax(x, axis=-1):
    return jax.nn.softmax(x, axis=axis)

def _gelu(x):
    return jax.nn.gelu(x, approximate=True)

def _silu(x):
    return jax.nn.silu(x)

def _sigmoid(x):
    return jax.nn.sigmoid(x)

def _layernorm(x, axis=-1, eps=1e-05):
    m = jnp.mean(x, axis=axis, keepdims=True)
    v = jnp.var(x, axis=axis, keepdims=True)
    return (x - m) / jnp.sqrt(v + eps)

def _scatter_add(tgt, idx, src, axis=0):
    return tgt.at[idx].add(src)

def _segment_sum(src, seg, n):
    return jax.ops.segment_sum(src, seg, n)
kernel_name = 'mk_early_fusion_d1_tok_img1024_r4_4a9458'

def setup_inputs(seed: int=0):
    np.random.seed(seed)
    _w = jnp.asarray

    def _rec_inputs():
        import jax
        import jax.numpy as jnp
        _rk = jax.random.key(seed)
        x = -0.000222058 + 0.999998 * jax.random.normal(jax.random.fold_in(_rk, 1), (64, 3, 64, 64), jnp.float32)
        txt = 0.000354947 + 1.41246 * jax.random.normal(jax.random.fold_in(_rk, 2), (64, 128, 256), jnp.float32)
        return (x, txt)
    x, txt = _rec_inputs()

    def _L0_tok_setup():
        import jax, jax.numpy as jnp
        import numpy as np
        IMG, PS, C, OUT = (64, 16, 3, 256)
        NP = IMG // PS
        IN_FEAT = C * PS * PS
        key = jax.random.key(seed)
        k1, k2, k3, k4 = jax.random.split(key, 4)
        x = jax.random.normal(k1, (128, C, IMG, IMG), dtype=jnp.float32)
        W = jax.random.normal(k2, (OUT, IN_FEAT), dtype=jnp.float32) / np.sqrt(IN_FEAT)
        b = jax.random.normal(k3, (OUT,), dtype=jnp.float32) * 0.01
        pos_emb = jax.random.normal(k4, (NP * NP, OUT), dtype=jnp.float32)
        return {'x': x, 'W': W, 'b': b, 'pos_emb': pos_emb}
    _L0_tok_all = _L0_tok_setup()
    _L0_tok_in = {k: v for k, v in _L0_tok_all.items() if k in ('W', 'b', 'pos_emb')}
    del _L0_tok_all

    def _L0_attn_setup():
        import jax, jax.numpy as jnp
        import numpy as np
        B, N, D, H = (8, 256, 256, 16)
        HD = D // H
        SCALE = HD ** (-0.5)
        key = jax.random.key(seed)
        k1, k2, k3, k4, k5 = jax.random.split(key, 5)
        return {'x': jax.random.normal(k1, (B, N, D), dtype=jnp.float32), 'qkv_w': jax.random.normal(k2, (3 * D, D), dtype=jnp.float32) * 0.02, 'qkv_b': jax.random.normal(k3, (3 * D,), dtype=jnp.float32) * 0.02, 'fc_w': jax.random.normal(k4, (D, D), dtype=jnp.float32) * 0.02, 'fc_b': jax.random.normal(k5, (D,), dtype=jnp.float32) * 0.02}
    _L0_attn_all = _L0_attn_setup()
    _L0_attn_in = {k: v for k, v in _L0_attn_all.items() if k in ('qkv_w', 'qkv_b', 'fc_w', 'fc_b')}
    del _L0_attn_all

    def _L0_ffn_setup():
        import jax, jax.numpy as jnp
        import numpy as np
        B, T, C = (2, 512, 256)
        H, D = (16, 64)
        CR = 8
        R = C // CR
        ROPE = D // 2
        NOPE = D - ROPE
        E, K, I, S = (8, 2, 128, 1)
        THETA = 100000.0
        EPS = 1e-05

        def _rmsnorm(x, w):
            rms = jnp.sqrt(jnp.mean(x * x, axis=-1, keepdims=True) + EPS)
            return w * (x / rms)

        def _rope(xh):
            d = xh.shape[-1]
            t = jnp.arange(xh.shape[2], dtype=jnp.float32)
            freqs = 1.0 / THETA ** (jnp.arange(0, d, 2, dtype=jnp.float32) / d)
            ang = jnp.outer(t, freqs)
            cos, sin = (jnp.cos(ang), jnp.sin(ang))
            xr = xh.reshape(xh.shape[:-1] + (d // 2, 2))
            x0, x1 = (xr[..., 0], xr[..., 1])
            rot = jnp.stack([x0 * cos - x1 * sin, x0 * sin + x1 * cos], axis=-1)
            return rot.reshape(xh.shape)

        def _attention(x, Wq, Wkva, Wkvb, Wo):
            b, t, _ = x.shape
            q = (x @ Wq).reshape(b, t, H, D).transpose(0, 2, 1, 3)
            ckv = x @ Wkva
            kv_latent, k_rope = (ckv[:, :, :R], ckv[:, :, R:])
            kv = (kv_latent @ Wkvb).reshape(b, t, H, NOPE).transpose(0, 2, 1, 3)
            k_rope = jnp.broadcast_to(k_rope[:, None, :, :], (b, H, t, ROPE))
            q_nope, q_rope = (q[..., :NOPE], q[..., NOPE:])
            q = jnp.concatenate([q_nope, _rope(q_rope)], axis=-1)
            k = jnp.concatenate([kv, _rope(k_rope)], axis=-1)
            v = jnp.concatenate([kv, jnp.zeros_like(k_rope)], axis=-1)
            att = jnp.einsum('bhqd,bhkd->bhqk', q, k) / jnp.sqrt(jnp.float32(D))
            mask = jnp.tril(jnp.ones((t, t), dtype=bool))
            att = jnp.where(mask, att, jnp.float32(-jnp.inf))
            att = jax.nn.softmax(att, axis=-1)
            y = jnp.einsum('bhqk,bhkd->bhqd', att, v)
            y = y.transpose(0, 2, 1, 3).reshape(b, t, H * D)
            return y @ Wo

        def _experts(x_flat, Wg, Wu, Wd):
            g = jax.nn.silu(jnp.einsum('nc,eci->nei', x_flat, Wg))
            u = jnp.einsum('nc,eci->nei', x_flat, Wu)
            return jnp.einsum('nei,eic->nec', g * u, Wd)

        def _moe(x, Wgate, expert_bias, Wg, Wu, Wd, sWg, sWu, sWd):
            b, t, c = x.shape
            xf = x.reshape(-1, c)
            shared = jnp.mean(_experts(xf, sWg, sWu, sWd), axis=1)
            logits = xf @ Wgate + expert_bias
            probs = jax.nn.softmax(logits, axis=-1)
            topk_p, topk_i = jax.lax.top_k(probs, K)
            topk_p = topk_p / jnp.sum(topk_p, axis=-1, keepdims=True)
            comb = jnp.sum(jax.nn.one_hot(topk_i, E, dtype=xf.dtype) * topk_p[..., None], axis=1)
            routed = jnp.einsum('ne,nec->nc', comb, _experts(xf, Wg, Wu, Wd))
            return (shared + routed).reshape(b, t, c)
        key = jax.random.key(seed)
        ks = jax.random.split(key, 16)
        w = lambda k, shp: jax.random.normal(k, shp, dtype=jnp.float32) * 0.02
        return {'x': jax.random.normal(ks[0], (B, T, C), dtype=jnp.float32), 'w_ln1': jnp.ones((C,), jnp.float32), 'Wq': w(ks[1], (C, H * D)), 'Wkva': w(ks[2], (C, R + ROPE)), 'Wkvb': w(ks[3], (R, H * NOPE)), 'Wo': w(ks[4], (H * D, C)), 'w_ln2': jnp.ones((C,), jnp.float32), 'Wgate': w(ks[5], (C, E)), 'expert_bias': jnp.zeros((E,), jnp.float32), 'Wg': w(ks[6], (E, C, I)), 'Wu': w(ks[7], (E, C, I)), 'Wd': w(ks[8], (E, I, C)), 'sWg': w(ks[9], (S, C, I)), 'sWu': w(ks[10], (S, C, I)), 'sWd': w(ks[11], (S, I, C))}
    _L0_ffn_all = _L0_ffn_setup()
    _L0_ffn_in = {k: v for k, v in _L0_ffn_all.items() if k in ('w_ln1', 'Wq', 'Wkva', 'Wkvb', 'Wo', 'w_ln2', 'Wgate', 'expert_bias', 'Wg', 'Wu', 'Wd', 'sWg', 'sWu', 'sWd')}
    del _L0_ffn_all
    return {'x': x, 'txt': txt, 'L0_tok_W': _L0_tok_in['W'], 'L0_tok_b': _L0_tok_in['b'], 'L0_tok_pos_emb': _L0_tok_in['pos_emb'], 'L0_attn_qkv_w': _L0_attn_in['qkv_w'], 'L0_attn_qkv_b': _L0_attn_in['qkv_b'], 'L0_attn_fc_w': _L0_attn_in['fc_w'], 'L0_attn_fc_b': _L0_attn_in['fc_b'], 'L0_ffn_w_ln1': _L0_ffn_in['w_ln1'], 'L0_ffn_Wq': _L0_ffn_in['Wq'], 'L0_ffn_Wkva': _L0_ffn_in['Wkva'], 'L0_ffn_Wkvb': _L0_ffn_in['Wkvb'], 'L0_ffn_Wo': _L0_ffn_in['Wo'], 'L0_ffn_w_ln2': _L0_ffn_in['w_ln2'], 'L0_ffn_Wgate': _L0_ffn_in['Wgate'], 'L0_ffn_expert_bias': _L0_ffn_in['expert_bias'], 'L0_ffn_Wg': _L0_ffn_in['Wg'], 'L0_ffn_Wu': _L0_ffn_in['Wu'], 'L0_ffn_Wd': _L0_ffn_in['Wd'], 'L0_ffn_sWg': _L0_ffn_in['sWg'], 'L0_ffn_sWu': _L0_ffn_in['sWu'], 'L0_ffn_sWd': _L0_ffn_in['sWd']}

def reference(x, txt, L0_tok_W, L0_tok_b, L0_tok_pos_emb, L0_attn_qkv_w, L0_attn_qkv_b, L0_attn_fc_w, L0_attn_fc_b, L0_ffn_w_ln1, L0_ffn_Wq, L0_ffn_Wkva, L0_ffn_Wkvb, L0_ffn_Wo, L0_ffn_w_ln2, L0_ffn_Wgate, L0_ffn_expert_bias, L0_ffn_Wg, L0_ffn_Wu, L0_ffn_Wd, L0_ffn_sWg, L0_ffn_sWu, L0_ffn_sWd):
    import jax
    import jax.numpy as jnp

    def _L0_tok_ref(x, W, b, pos_emb):
        import jax, jax.numpy as jnp
        import numpy as np
        IMG, PS, C, OUT = (64, 16, 3, 256)
        NP = IMG // PS
        IN_FEAT = C * PS * PS
        B = x.shape[0]
        p = x.reshape(B, C, NP, PS, NP, PS).transpose(0, 1, 2, 4, 3, 5)
        p = p.transpose(0, 2, 3, 1, 4, 5)
        p = p.reshape(B, NP * NP, IN_FEAT)
        out = jnp.einsum('bnf,of->bno', p, W) + b + pos_emb
        return out

    def _L0_attn_ref(x, qkv_w, qkv_b, fc_w, fc_b):
        import jax, jax.numpy as jnp
        import numpy as np
        B, N, D, H = (8, 256, 256, 16)
        HD = D // H
        SCALE = HD ** (-0.5)
        b, n, d = x.shape
        qkv = (jnp.einsum('bnd,ed->bne', x, qkv_w) + qkv_b).reshape(b, n, H, 3 * HD)
        q, k, v = jnp.split(qkv, 3, axis=-1)
        q = q.transpose(0, 2, 1, 3)
        k = k.transpose(0, 2, 1, 3)
        v = v.transpose(0, 2, 1, 3)
        attn = jax.nn.softmax(jnp.einsum('bhqd,bhkd->bhqk', q, k) * SCALE, axis=-1)
        out = jnp.einsum('bhqk,bhkd->bhqd', attn, v)
        out = out.transpose(0, 2, 1, 3).reshape(b, n, d)
        return jnp.einsum('bnd,ed->bne', out, fc_w) + fc_b + x

    def _L0_ffn_ref(x, w_ln1, Wq, Wkva, Wkvb, Wo, w_ln2, Wgate, expert_bias, Wg, Wu, Wd, sWg, sWu, sWd):
        import jax, jax.numpy as jnp
        import numpy as np
        B, T, C = (2, 512, 256)
        H, D = (16, 64)
        CR = 8
        R = C // CR
        ROPE = D // 2
        NOPE = D - ROPE
        E, K, I, S = (8, 2, 128, 1)
        THETA = 100000.0
        EPS = 1e-05

        def _rmsnorm(x, w):
            rms = jnp.sqrt(jnp.mean(x * x, axis=-1, keepdims=True) + EPS)
            return w * (x / rms)

        def _rope(xh):
            d = xh.shape[-1]
            t = jnp.arange(xh.shape[2], dtype=jnp.float32)
            freqs = 1.0 / THETA ** (jnp.arange(0, d, 2, dtype=jnp.float32) / d)
            ang = jnp.outer(t, freqs)
            cos, sin = (jnp.cos(ang), jnp.sin(ang))
            xr = xh.reshape(xh.shape[:-1] + (d // 2, 2))
            x0, x1 = (xr[..., 0], xr[..., 1])
            rot = jnp.stack([x0 * cos - x1 * sin, x0 * sin + x1 * cos], axis=-1)
            return rot.reshape(xh.shape)

        def _attention(x, Wq, Wkva, Wkvb, Wo):
            b, t, _ = x.shape
            q = (x @ Wq).reshape(b, t, H, D).transpose(0, 2, 1, 3)
            ckv = x @ Wkva
            kv_latent, k_rope = (ckv[:, :, :R], ckv[:, :, R:])
            kv = (kv_latent @ Wkvb).reshape(b, t, H, NOPE).transpose(0, 2, 1, 3)
            k_rope = jnp.broadcast_to(k_rope[:, None, :, :], (b, H, t, ROPE))
            q_nope, q_rope = (q[..., :NOPE], q[..., NOPE:])
            q = jnp.concatenate([q_nope, _rope(q_rope)], axis=-1)
            k = jnp.concatenate([kv, _rope(k_rope)], axis=-1)
            v = jnp.concatenate([kv, jnp.zeros_like(k_rope)], axis=-1)
            att = jnp.einsum('bhqd,bhkd->bhqk', q, k) / jnp.sqrt(jnp.float32(D))
            mask = jnp.tril(jnp.ones((t, t), dtype=bool))
            att = jnp.where(mask, att, jnp.float32(-jnp.inf))
            att = jax.nn.softmax(att, axis=-1)
            y = jnp.einsum('bhqk,bhkd->bhqd', att, v)
            y = y.transpose(0, 2, 1, 3).reshape(b, t, H * D)
            return y @ Wo

        def _experts(x_flat, Wg, Wu, Wd):
            g = jax.nn.silu(jnp.einsum('nc,eci->nei', x_flat, Wg))
            u = jnp.einsum('nc,eci->nei', x_flat, Wu)
            return jnp.einsum('nei,eic->nec', g * u, Wd)

        def _moe(x, Wgate, expert_bias, Wg, Wu, Wd, sWg, sWu, sWd):
            b, t, c = x.shape
            xf = x.reshape(-1, c)
            shared = jnp.mean(_experts(xf, sWg, sWu, sWd), axis=1)
            logits = xf @ Wgate + expert_bias
            probs = jax.nn.softmax(logits, axis=-1)
            topk_p, topk_i = jax.lax.top_k(probs, K)
            topk_p = topk_p / jnp.sum(topk_p, axis=-1, keepdims=True)
            comb = jnp.sum(jax.nn.one_hot(topk_i, E, dtype=xf.dtype) * topk_p[..., None], axis=1)
            routed = jnp.einsum('ne,nec->nc', comb, _experts(xf, Wg, Wu, Wd))
            return (shared + routed).reshape(b, t, c)
        x = x + _attention(_rmsnorm(x, w_ln1), Wq, Wkva, Wkvb, Wo)
        residual = x
        xn = _rmsnorm(x, w_ln2)
        x_out = _moe(xn, Wgate, expert_bias, Wg, Wu, Wd, sWg, sWu, sWd)
        return residual + x_out
    h = _L0_tok_ref(x, L0_tok_W, L0_tok_b, L0_tok_pos_emb)
    h = jnp.concatenate([h, txt], axis=1)
    h = h + _L0_attn_ref(_layernorm(h, axis=-1), L0_attn_qkv_w, L0_attn_qkv_b, L0_attn_fc_w, L0_attn_fc_b)
    h = h + _L0_ffn_ref(_layernorm(h, axis=-1), L0_ffn_w_ln1, L0_ffn_Wq, L0_ffn_Wkva, L0_ffn_Wkvb, L0_ffn_Wo, L0_ffn_w_ln2, L0_ffn_Wgate, L0_ffn_expert_bias, L0_ffn_Wg, L0_ffn_Wu, L0_ffn_Wd, L0_ffn_sWg, L0_ffn_sWu, L0_ffn_sWd)
    return h

_drawn_inputs = setup_inputs


def setup_inputs(seed=0):
    import zlib

    import numpy as np

    out = dict(_drawn_inputs(seed))
    spreads = {'L0_ffn_w_ln1': (1.0, 0.6), 'L0_ffn_w_ln2': (1.0, 0.6), 'L0_ffn_expert_bias': (0.0, 0.8)}
    factors = {'L0_tok_b': 8.0,
     'L0_attn_qkv_w': 8.0,
     'L0_attn_qkv_b': 8.0,
     'L0_attn_fc_w': 8.0,
     'L0_attn_fc_b': 7.014,
     'L0_ffn_Wq': 8.0,
     'L0_ffn_Wkva': 8.0,
     'L0_ffn_Wkvb': 8.0,
     'L0_ffn_Wo': 8.0,
     'L0_ffn_Wgate': 8.0,
     'L0_ffn_Wg': 8.0,
     'L0_ffn_Wu': 8.0,
     'L0_ffn_Wd': 8.0,
     'L0_ffn_sWg': 8.0,
     'L0_ffn_sWu': 8.0,
     'L0_ffn_sWd': 8.0}
    for name, (base, spread) in spreads.items():
        noise = np.random.default_rng([zlib.crc32(name.encode()), seed]).standard_normal(out[name].shape)
        drawn = base * np.exp(spread * noise) if base else spread * noise
        out[name] = jnp.asarray(drawn.astype(out[name].dtype))
    for name, factor in factors.items():
        out[name] = (out[name] * factor).astype(out[name].dtype)
    return out
```

```python
from contextlib import ExitStack

import numpy as np

import concourse.bass as bass
from concourse import mybir

F32 = mybir.dt.float32
F32R = mybir.dt.float32r
BF16 = mybir.dt.bfloat16
ALU = mybir.AluOpType
ACT = mybir.ActivationFunctionType
AX = mybir.AxisListType

P = 128
SEQS, IMG_TOK, TXT_TOK, D = 64, 16, 128, 256
T = IMG_TOK + TXT_TOK
DT = D // P
HEADS, GROUPS, HPG = 16, 4, 4
Q = 32
REM = T - P
PAD_T = P + Q
HD1 = D // HEADS
SPLIT = 6
PARTS = 3
FEAT = 768
KT_EMB = FEAT // P
EPS = 1e-5
NOPE = ROPE = LAT = 32
EXPERTS, ALL_E, TOPK, INNER = 8, 9, 2, 128
NEG = -1.0e30
CHUNK = 512


def need(engine, semaphore, value):
    if isinstance(value, int) and value <= 0:
        return
    engine.wait_ge(semaphore, value)


def in_register(engine, value):
    if isinstance(value, int):
        return value
    register = engine.alloc_register()
    engine.reg_mov(register, value)
    return register


def need_all(engine, *waits):
    waits = [(semaphore, in_register(engine, value)) for semaphore, value in waits]
    for semaphore, value in waits:
        need(engine, semaphore, value)


def spread(ap, axis, n):
    a = ap.unsqueeze(axis)
    shape = list(a.shape)
    shape[axis] = n
    return a.to_broadcast(shape)


def names(ctx, nc, prefix, words):
    return {w: ctx.enter_context(nc.semaphore(f"{prefix}_{w}")) for w in words.split()}


def embed_phase(nc, dram, embedded, seqs):
    tokens = seqs * IMG_TOK
    width = min(CHUNK, tokens)
    chunks = tokens // width
    with ExitStack() as ctx:
        sb = lambda name, shape, dt=F32: ctx.enter_context(nc.sbuf_tensor(name, shape, dt))
        weights = sb("e_weights", [P, KT_EMB, D])
        patches = sb("e_patches", [P, KT_EMB, width])
        bias = sb("e_bias", [P, DT])
        pos = sb("e_pos", [P, DT, IMG_TOK])
        out = [ctx.enter_context(nc.psum_tensor(f"e_out{t}", [P, width], F32)) for t in range(DT)]
        sem = names(ctx, nc, "e", "weights patches product embedded")
        with nc.Block() as block:

            @block.sync
            def _(sp):
                sp.dma_start(weights[:], dram["tok_w"]).then_inc(sem["weights"], 16)
                sp.dma_start(bias[:], dram["tok_b"]).then_inc(sem["weights"], 16)
                sp.dma_start(pos[:], dram["pos"]).then_inc(sem["weights"], 16)
                for c in range(chunks):
                    need(sp, sem["product"], c)
                    sp.dma_start(patches[:], dram["patches"][:, :, c * width:(c + 1) * width]).then_inc(sem["patches"], 16)

            @block.tensor
            def _(pe):
                pe.wait_ge(sem["weights"], 48)
                for c in range(chunks):
                    pe.wait_ge(sem["patches"], 16 * (c + 1))
                    need(pe, sem["embedded"], c)
                    for t in range(DT):
                        for k in range(KT_EMB):
                            mm = pe.matmul(out[t][:], weights[:, k, t * P:(t + 1) * P], patches[:, k, :],
                                           start=(k == 0), stop=(k == KT_EMB - 1))
                    mm.then_inc(sem["product"], 1)

            @block.vector
            def _(dve):
                n = width // IMG_TOK
                for c in range(chunks):
                    dve.wait_ge(sem["product"], c + 1)
                    for t in range(DT):
                        last = dve.scalar_tensor_tensor(
                            out=embedded[:, t, c * width:(c + 1) * width].rearrange("p (s n) -> p s n", n=IMG_TOK),
                            in0=out[t][:].rearrange("p (s n) -> p s n", n=IMG_TOK), scalar=bias[:, t:t + 1],
                            in1=spread(pos[:, t, :], 1, n), op0=ALU.add, op1=ALU.add)
                    last.then_inc(sem["embedded"], 1)


def attn1_phase(nc, dram, embedded, h1_scratch, seqs):
    with ExitStack() as ctx:
        sb = lambda name, shape, dt=F32: ctx.enter_context(nc.sbuf_tensor(name, shape, dt))
        wqk = sb("a_wqk", [P, DT, 4, P])
        bqk = sb("a_bqk", [P, 4])
        wv = sb("a_wv", [P, DT, D])
        bv = sb("a_bv", [P, D])
        bv_rem = sb("a_bv_rem", [P, D])
        fcw = sb("a_fcw", [P, GROUPS, D])
        fcb = sb("a_fcb", [P, DT])
        rem_mask = sb("a_rem_mask", [P, 1])
        ones_avg = sb("a_ones_avg", [P, P])
        ident_f = sb("a_ident_f", [P, P])
        ident = sb("a_ident", [P, P], BF16)
        onehot_f = sb("a_onehot_f", [40, HEADS, P])
        onehot_rem_f = sb("a_onehot_rem_f", [41, HEADS, Q])
        onehot = sb("a_onehot", [40, HEADS, P], BF16)
        onehot_rem = sb("a_onehot_rem", [41, HEADS, Q], BF16)
        nt_rows = sb("a_nt_rows", [40, 2])
        eps = sb("a_eps", [P, 1])
        waited = sb("a_waited", [1, 1])
        x = [sb(f"a_x{i}", [P, DT, T]) for i in range(2)]
        res = [sb(f"a_res{i}", [P, DT, T]) for i in range(2)]
        xs = sb("a_xs", [P, T])
        xc = sb("a_xc", [P, DT, T])
        sq = sb("a_sq", [P, DT, T])
        sqs = sb("a_sqs", [P, T])
        ln_var = sb("a_ln_var", [P, T])
        rstd = sb("a_rstd", [P, T])
        xn = sb("a_xn", [P, DT, T])
        xn_rem = sb("a_xn_rem", [P, DT, P])
        qk = sb("a_qk", [P, 2, 2, T])
        parts = [sb(f"a_part{i}", [P, 2, 2, T], BF16) for i in range(PARTS)]
        rest = sb("a_rest", [P, 2, 2, T])
        stacks = [sb(f"a_stacks{i}", [SPLIT * HD1, 2 * HEADS * T + Q - REM], BF16) for i in range(2)]
        spill = [nc.dram_tensor(f"a_spill{i}", [PARTS, P, GROUPS * T], BF16).ap() for i in range(2)]
        v_main = [sb(f"a_v{i}", [P, HEADS, Q]) for i in range(2)]
        v_rem = [sb(f"a_vrem{i}", [P, GROUPS, P]) for i in range(2)]
        nmax = sb("a_nmax", [P, HEADS + GROUPS])
        nmax_parts = sb("a_nmax_parts", [P, 2, HEADS + GROUPS], BF16)
        nt = sb("a_nt", [41, HPG, T], BF16)
        prob = [sb(f"a_prob{i}", [P, HPG, T]) for i in range(2)]
        prob_rem = [sb(f"a_probrem{i}", [P, T]) for i in range(2)]
        ou = sb("a_ou", [P, GROUPS, T])
        z = sb("a_z", [P, GROUPS, T])
        lnz = sb("a_lnz", [P, GROUPS, T])
        rz = sb("a_rz", [P, GROUPS, T])
        ot = sb("a_ot", [P, GROUPS, T])
        h1 = [sb(f"a_h1{i}", [P, DT, T]) for i in range(2)]
        ps = ctx.enter_context(nc.psum_tensor("a_psum", [P, 8, 512], F32))
        sem = names(ctx, nc, "a", "weights const xload xs mean xc sq sqs var lnv rstd xn xnr res q qk c1 r1 c2 c3 spill stack "
                    "v vout vr vrout s max nm1 nm2 nmt nt st exp pv ou z lnz rz ot fc h1 store")
        EV = sem
        heads = range(HPG)

        def stacked(p, which, h, a, b):
            at = ((h % HPG * 2 + which) * GROUPS + h // HPG) * T
            return stacks[p][:, at + a:at + b]

        def s_banks(g):
            return ps[:, 2 * (g % 2):2 * (g % 2) + 2, :]

        def st_banks(g):
            return ps[:, 2 + 2 * (g % 2):4 + 2 * (g % 2), :]

        def two_heads(banks):
            return banks[:, :, 0:2 * T]

        LOADS = 9
        STACKS = 10

        def load_x(sp, n, q):
            text, patch = n * D, n * IMG_TOK
            need_all(sp, (EV["res"], n - 1), (EV["xload"], 32 * n))
            sp.dma_start(x[q][:, :, IMG_TOK:], dram["txt"][:, bass.ds(text, D)].rearrange("p (t j) -> p t j", t=DT)
                         ).then_inc(EV["xload"], 16)
            sp.dma_start(x[q][:, :, 0:IMG_TOK], embedded[:, :, bass.ds(patch, IMG_TOK)]).then_inc(EV["xload"], 16)

        def stack(sp, n, q):
            for part, made in enumerate(("c1", "c2", "c3")):
                if part == 0:
                    need_all(sp, (EV[made], 2 * n + 2), (EV["stack"], 16 * STACKS * (n - 1)))
                else:
                    sp.wait_ge(EV[made], 2 * n + 2)
                sp.dma_start(spill[q][part], parts[part][:].rearrange("p a b j -> p (a b j)")).then_inc(EV["spill"], 16)
            need_all(sp, (EV["spill"], 16 * PARTS * (n + 1)), (EV["st"], GROUPS * (n - 1)))
            row, plane = GROUPS * T, P * GROUPS * T
            for slot, (a, b) in enumerate(((0, 0), (0, 1), (0, 2), (1, 0), (1, 1), (2, 0))):
                src = spill[q]
                dst = stacks[q][slot * HD1:(slot + 1) * HD1, 0:2 * HEADS * T].rearrange("d (j w c) -> d j w c", w=2, j=HPG)
                if a == b:
                    sp.dma_start(dst.rearrange("d j w c -> d (j w) c"),
                                 bass.AP(tensor=src.tensor, offset=src.offset + a * plane,
                                         ap=[[row, HD1], [HD1 * row, 2 * HPG], [1, row]])).then_inc(EV["stack"], 16)
                else:
                    for w, part in enumerate((a, b)):
                        sp.dma_start(dst[:, :, w, :],
                                     bass.AP(tensor=src.tensor, offset=src.offset + part * plane + w * HD1 * row,
                                             ap=[[row, HD1], [Q * row, HPG], [1, row]])).then_inc(EV["stack"], 16)

        def store_h1(sp, s, p):
            token = s * T
            need_all(sp, (EV["h1"], s + 1), (EV["store"], 16 * (s + 1)))
            sp.dma_start(h1_scratch[:, :, bass.ds(token, T)], h1[p][:]).then_inc(EV["store"], 16)

        def mean(pe, n):
            pe.wait_ge(EV["xs"], n + 1)
            need(pe, EV["nt"], n - 1)
            pe.matmul(ps[:, 7, 0:T], ones_avg[:], xs[:], start=True, stop=True).then_inc(EV["mean"], 1)

        def var(pe, n):
            pe.wait_ge(EV["sqs"], n + 1)
            pe.wait_ge(EV["xc"], n + 1)
            pe.matmul(ps[:, 7, 0:T], ones_avg[:], sqs[:], start=True, stop=True).then_inc(EV["var"], 1)

        def project_qk(pe, n, which):
            if which == 0:
                pe.wait_ge(EV["xn"], n + 1)
                need(pe, EV["max"], GROUPS * (n - 1) + 3)
            for t in range(DT):
                for k in range(DT):
                    mm = pe.matmul(ps[:, which, t * T:(t + 1) * T], wqk[:, k, 2 * which + t, :], xn[:, k, :],
                                   start=(k == 0), stop=(k == DT - 1))
            mm.then_inc(EV["q"], 1)

        def project_v(pe, n):
            pe.wait_ge(EV["qk"], 2 * n + 1)
            for k in range(DT):
                mm = pe.matmul(ps[:, 0, 0:D], xn[:, k, 0:P], wv[:, k, :], start=(k == 0), stop=(k == DT - 1))
            mm.then_inc(EV["v"], 1)

        def project_v_rem(pe, n):
            pe.wait_ge(EV["qk"], 2 * n + 2)
            pe.wait_ge(EV["xnr"], n + 1)
            for k in range(DT):
                mm = pe.matmul(ps[:, 1, 0:D], xn_rem[:, k, :], wv[:, k, :],
                               start=(k == 0), stop=(k == DT - 1))
            mm.then_inc(EV["vr"], 1)

        def scores(pe, s, p, g):
            if g == 0:
                pe.wait_ge(EV["stack"], 16 * STACKS * (s + 1))
                pe.wait_ge(EV["vout"], s + 1)
                pe.wait_ge(EV["vrout"], s + 1)
            elif g == 1:
                need(pe, EV["exp"], GROUPS * (s - 1) + 3)
            else:
                need(pe, EV["max"], GROUPS * s + g - 1)
            b = s_banks(g)
            for j in heads:
                h = HPG * g + j
                pe.matmul(b[:, j // 2, (j % 2) * T:(j % 2 + 1) * T], stacked(p, 0, h, 0, P), stacked(p, 1, h, 0, T),
                          start=True, stop=True)
            for j in heads:
                h = HPG * g + j
                mm = pe.matmul(b[Q * j:Q * j + Q, 0, 2 * T:3 * T], stacked(p, 0, h, P, PAD_T), stacked(p, 1, h, 0, T),
                               start=True, stop=True)
            mm.then_inc(EV["s"], 1)

        def turn_max(pe, s, n_var):
            pe.wait_ge(EV["nm2"], s + 1)
            need(pe, EV["lnv"], n_var)
            pe.matmul(ps[0:40, 7, 0:P], nmax_parts[:].rearrange("p a c -> p (a c)"), ident[:],
                      start=True, stop=True).then_inc(EV["nmt"], 1)

        def scores_t(pe, s, p, g):
            if g == 0:
                pe.wait_ge(EV["nt"], s + 1)
                pe.wait_ge(EV["max"], GROUPS * s + 4)
            else:
                need(pe, EV["exp"], GROUPS * s + g - 1)
            b = st_banks(g)
            for j in heads:
                h = HPG * g + j
                o = b[:, j // 2, (j % 2) * T:(j % 2 + 1) * T]
                pe.matmul(o, stacked(p, 1, h, 0, P), stacked(p, 0, h, 0, T), start=True, stop=False)
                pe.matmul(o, onehot[:, h, :], nt[0:40, j, :], start=False, stop=True)
            for j in heads:
                h = HPG * g + j
                o = b[Q * j:Q * j + Q, 0, 2 * T:3 * T]
                pe.matmul(o, stacked(p, 1, h, P, PAD_T), stacked(p, 0, h, 0, T), start=True, stop=False)
                mm = pe.matmul(o, onehot_rem[:, h, :], nt[:, j, :], start=False, stop=True)
            mm.then_inc(EV["st"], 1)

        def weigh(pe, s, p, g):
            pe.wait_ge(EV["exp"], GROUPS * s + g + 1)
            if g == 0:
                need(pe, EV["h1"], s)
            else:
                pe.wait_ge(EV["ou"], GROUPS * s + g)
            pe.matmul(ps[:, 6, 0:T], v_rem[p][:, g, :], prob_rem[g % 2][:], start=True, stop=False)
            for j in heads:
                mm = pe.matmul(ps[Q * j:Q * j + Q, 6, 0:T], v_main[p][:, HPG * g + j, :], prob[g % 2][:, j, :],
                               start=False, stop=True)
            mm.then_inc(EV["pv"], 1)

        def fc(pe, s):
            pe.wait_ge(EV["ot"], s + 1)
            for t in range(DT):
                for g in range(GROUPS):
                    mm = pe.matmul(ps[:, 6, t * T:(t + 1) * T], fcw[:, g, t * P:(t + 1) * P], ot[:, g, :],
                                   start=(g == 0), stop=(g == GROUPS - 1))
            mm.then_inc(EV["fc"], 1)

        def centre(dve, n, q):
            dve.wait_ge(EV["mean"], n + 1)
            dve.tensor_tensor(xc[:], x[q][:], spread(ps[:, 7, 0:T], 1, DT), ALU.subtract).then_inc(EV["xc"], 1)

        def normalise(dve, n):
            dve.wait_ge(EV["rstd"], n + 1)
            dve.tensor_tensor(xn[:], xc[:], spread(rstd[:], 1, DT), ALU.mult).then_inc(EV["xn"], 1)

        def qk_out(dve, n, which):
            dve.wait_ge(EV["q"], 2 * n + which + 1)
            need(dve, EV["r1"], 2 * (n - 1) + which + 1)
            dve.tensor_tensor(qk[:, which], ps[:, which, 0:2 * T].rearrange("p (t j) -> p t j", t=DT),
                              spread(bqk[:, 2 * which:2 * which + 2], 2, T), ALU.add).then_inc(EV["qk"], 1)

        def v_out(dve, n, q):
            dve.wait_ge(EV["v"], n + 1)
            dve.tensor_tensor(v_main[q][:, :, 0:HD1], ps[:, 0, 0:D].rearrange("p (h d) -> p h d", d=HD1),
                              bv[:].rearrange("p (h d) -> p h d", d=HD1), ALU.add).then_inc(EV["vout"], 1)

        def v_rem_out(dve, n, q):
            dve.wait_ge(EV["vr"], n + 1)
            for j in heads:
                r = slice(Q * j, Q * j + Q)
                last = dve.scalar_tensor_tensor(
                    out=v_rem[q][r, :, Q * j:Q * j + HD1],
                    in0=ps[r, 1, 0:D].rearrange("p (g j d) -> p g j d", g=GROUPS, j=HPG)[:, :, j, :],
                    scalar=rem_mask[r, :],
                    in1=bv_rem[r, :].rearrange("p (g j d) -> p g j d", g=GROUPS, j=HPG)[:, :, j, :],
                    op0=ALU.mult, op1=ALU.add)
            last.then_inc(EV["vrout"], 1)

        def maxima(dve, s, g):
            dve.wait_ge(EV["s"], GROUPS * s + g + 1)
            b = s_banks(g)
            dve.tensor_reduce(nmax[:, HPG * g:HPG * g + HPG].rearrange("p (b j) -> p b j", b=2),
                              two_heads(b).rearrange("p b (j k) -> p b j k", j=2), AX.X, ALU.max, negate=True)
            dve.tensor_reduce(nmax[:, HEADS + g:HEADS + g + 1], b[:, 0, 2 * T:3 * T], AX.X, ALU.max,
                              negate=True).then_inc(EV["max"], 1)

        def split_max(dve, s):
            dve.wait_ge(EV["max"], GROUPS * (s + 1))
            dve.tensor_copy(nmax_parts[:, 0, :], nmax[:]).then_inc(EV["nm1"], 1)
            dve.wait_ge(EV["nm1"], s + 1)
            dve.tensor_tensor(nmax_parts[:, 1, :], nmax[:], nmax_parts[:, 0, :], ALU.subtract).then_inc(EV["nm2"], 1)

        def weighed_out(dve, s, g):
            dve.wait_ge(EV["pv"], GROUPS * s + g + 1)
            dve.tensor_copy(ou[:, g, :], ps[:, 6, 0:T]).then_inc(EV["ou"], 1)

        def sums(dve, s):
            dve.wait_ge(EV["ou"], GROUPS * (s + 1))
            dve.memset(waited[:], 0.0)
            dve.stream_shuffle(z[:], ou[:], [HD1 + i % HD1 for i in range(Q)]).then_inc(EV["z"], 1)

        def residual(dve, s, p):
            dve.wait_ge(EV["fc"], s + 1)
            need(dve, EV["store"], 16 * (s + 1))
            dve.wait_ge(EV["res"], s + 1)
            for t in range(DT):
                last = dve.scalar_tensor_tensor(out=h1[p][:, t, :], in0=ps[:, 6, t * T:(t + 1) * T],
                                                scalar=fcb[:, t:t + 1], in1=res[p][:, t, :], op0=ALU.add, op1=ALU.add)
            last.then_inc(EV["h1"], 1)

        def square(act, n):
            act.wait_ge(EV["xc"], n + 1)
            act.activation(sq[:], xc[:], ACT.Square).then_inc(EV["sq"], 1)

        def inv_std(act, n):
            act.wait_ge(EV["var"], n + 1)
            act.activation(ln_var[:], ps[:, 7, 0:T], ACT.Ln, bias=eps[:]).then_inc(EV["lnv"], 1)
            act.wait_ge(EV["lnv"], n + 1)
            act.activation(rstd[:], ln_var[:], ACT.Exp, scale=-0.5).then_inc(EV["rstd"], 1)

        def repeat_last(act, n):
            act.wait_ge(EV["xn"], n + 1)
            act.activation(xn_rem[:].rearrange("p t (r j) -> p t r j", j=REM), spread(xn[:, :, P:T], 2, P // REM),
                           ACT.Copy).then_inc(EV["xnr"], 1)

        def first_part(act, n, which):
            act.wait_ge(EV["qk"], 2 * n + which + 1)
            need(act, EV["stack"], 16 * STACKS * n)
            act.activation(parts[0][:, which], qk[:, which], ACT.Copy).then_inc(EV["c1"], 1)

        def second_part(act, n, which):
            act.wait_ge(EV["r1"], 2 * n + which + 1)
            act.activation(parts[1][:, which], rest[:, which], ACT.Copy).then_inc(EV["c2"], 1)

        def max_rows(act, s):
            act.wait_ge(EV["nmt"], s + 1)
            act.activation(nt[0:40, :, 0:P], spread(ps[0:40, 7, 0:P], 1, HPG), ACT.Copy, scale=nt_rows[:, 0:1])
            act.activation(nt[0:40, :, P:T], ps[0:40, 7, 0:P].rearrange("p (j q) -> p j q", q=Q)[:, :, 0:REM],
                           ACT.Copy, scale=nt_rows[:, 1:2]).then_inc(EV["nt"], 1)

        def exps(act, s, g):
            act.wait_ge(EV["st"], GROUPS * s + g + 1)
            need(act, EV["pv"], GROUPS * s + g - 1)
            b = st_banks(g)
            act.activation(prob[g % 2][:].rearrange("p (b j) q -> p b (j q)", b=2), two_heads(b), ACT.Exp, scale=HD1 ** -0.5)
            act.activation(prob_rem[g % 2][:], b[:, 0, 2 * T:3 * T], ACT.Exp, scale=HD1 ** -0.5).then_inc(EV["exp"], 1)

        def inv_sums(act, s):
            act.wait_ge(EV["z"], s + 1)
            act.activation(lnz[:], z[:], ACT.Ln).then_inc(EV["lnz"], 1)
            act.wait_ge(EV["lnz"], s + 1)
            act.activation(rz[:], lnz[:], ACT.Exp, scale=-1.0).then_inc(EV["rz"], 1)

        def add_tiles(pool, n, q):
            pool.wait_ge(EV["xload"], 32 * (n + 1))
            need(pool, EV["mean"], n)
            pool.tensor_tensor(xs[:], x[q][:, 0, :], x[q][:, 1, :], ALU.add).then_inc(EV["xs"], 1)

        def add_squares(pool, n):
            pool.wait_ge(EV["sq"], n + 1)
            pool.tensor_tensor(sqs[:], sq[:, 0, :], sq[:, 1, :], ALU.add).then_inc(EV["sqs"], 1)

        def add_norm(pool, n, q):
            pool.wait_ge(EV["xn"], n + 1)
            need(pool, EV["h1"], n - 1)
            pool.tensor_tensor(res[q][:], x[q][:], xn[:], ALU.add).then_inc(EV["res"], 1)

        def rest_one(pool, n, which):
            pool.wait_ge(EV["c1"], 2 * n + which + 1)
            pool.tensor_tensor(rest[:, which], qk[:, which], parts[0][:, which], ALU.subtract).then_inc(EV["r1"], 1)

        def third_part(pool, n, which):
            pool.wait_ge(EV["c2"], 2 * n + which + 1)
            pool.tensor_tensor(parts[2][:, which], rest[:, which], parts[1][:, which], ALU.subtract).then_inc(EV["c3"], 1)

        def divide(pool, s):
            pool.wait_ge(EV["rz"], s + 1)
            if isinstance(s, int):
                need(pool, EV["fc"], s)
            pool.tensor_tensor(ot[:], ou[:], rz[:], ALU.mult).then_inc(EV["ot"], 1)

        def each_step(engine, step):
            step(0, 0, True, False)
            if seqs > 2:
                with engine.Fori(0, (seqs - 2) // 2) as i:
                    step(i * 2 + 1, 1, False, False)
                    step(i * 2 + 2, 0, False, False)
            step(seqs - 1, 1, False, True)

        with nc.Block() as block:

            @block.sync
            def _(sp):
                for dst, name in ((wqk, "wqk"), (bqk, "bqk"), (wv, "wv"), (bv, "bv"), (fcw, "fcw"), (fcb, "fcb"),
                                  (rem_mask, "rem_mask"), (onehot_f, "onehot1"), (onehot_rem_f, "onehot1_rem"), (nt_rows, "nt_rows"), (ident_f, "ident")):
                    sp.dma_start(dst[:], dram[name]).then_inc(sem["weights"], 16)
                load_x(sp, 0, 0)
                stack(sp, 0, 0)

                def step(s, p, first, last):
                    if not last:
                        load_x(sp, s + 1, 1 - p)
                    if not first:
                        store_h1(sp, s - 1, 1 - p)
                    if not last:
                        stack(sp, s + 1, 1 - p)
                each_step(sp, step)
                store_h1(sp, seqs - 1, 1)
                sp.wait_ge(EV["store"], 16 * (seqs + 1))

            @block.tensor
            def _(pe):
                pe.wait_ge(sem["weights"], 176)
                pe.wait_ge(sem["const"], 9)
                mean(pe, 0)
                var(pe, 0)
                project_qk(pe, 0, 0)
                project_qk(pe, 0, 1)
                project_v(pe, 0)
                project_v_rem(pe, 0)

                def step(s, p, first, last):
                    n = s + 1
                    scores(pe, s, p, 0)
                    scores(pe, s, p, 1)
                    if not last:
                        mean(pe, n)
                    scores(pe, s, p, 2)
                    scores(pe, s, p, 3)
                    if not last:
                        var(pe, n)
                    if not first:
                        fc(pe, s - 1)
                    turn_max(pe, s, n + 1 if not last else n)
                    if not last:
                        project_qk(pe, n, 0)
                        project_qk(pe, n, 1)
                    scores_t(pe, s, p, 0)
                    if not last:
                        project_v(pe, n)
                    scores_t(pe, s, p, 1)
                    weigh(pe, s, p, 0)
                    if not last:
                        project_v_rem(pe, n)
                    scores_t(pe, s, p, 2)
                    weigh(pe, s, p, 1)
                    scores_t(pe, s, p, 3)
                    weigh(pe, s, p, 2)
                    weigh(pe, s, p, 3)
                each_step(pe, step)
                fc(pe, seqs - 1)

            @block.vector
            def _(dve):
                dve.memset(ones_avg[:], 1.0 / D).then_inc(sem["const"], 1)
                for i in range(2):
                    dve.memset(v_main[i][:, :, HD1:], 1.0).then_inc(sem["const"], 1)
                dve.memset(eps[:], EPS).then_inc(sem["const"], 1)
                dve.memset(waited[:], 0.0).then_inc(sem["store"], 16)
                for i in range(2):
                    dve.memset(stacks[i][:, 2 * HEADS * T:], 0.0)
                dve.memset(nt[Q:], 1.0)
                dve.memset(nt[0:Q], 0.0).then_inc(sem["const"], 1)
                dve.wait_ge(sem["weights"], 176)
                dve.tensor_copy(ident[:], ident_f[:]).then_inc(sem["const"], 1)
                dve.tensor_copy(onehot[:], onehot_f[:]).then_inc(sem["const"], 1)
                dve.tensor_scalar(bv_rem[:], bv[:], rem_mask[:, 0:1], None, ALU.mult).then_inc(sem["const"], 1)
                dve.wait_ge(sem["const"], 8)
                dve.tensor_copy(onehot_rem[:], onehot_rem_f[:]).then_inc(sem["const"], 1)
                centre(dve, 0, 0)
                normalise(dve, 0)
                qk_out(dve, 0, 0)
                qk_out(dve, 0, 1)
                v_out(dve, 0, 0)
                for i in range(2):
                    dve.memset(v_rem[i][:], 0.0).then_inc(sem["const"], 1)
                dve.wait_ge(sem["const"], 11)
                for i in range(2):
                    for j in heads:
                        r = slice(Q * j, Q * j + Q)
                        last = dve.tensor_copy(v_rem[i][r, :, Q * j + HD1:Q * j + Q],
                                               spread(spread(rem_mask[r, 0], 1, GROUPS), 2, HD1))
                last.then_inc(sem["const"], 1)
                v_rem_out(dve, 0, 0)

                def step(s, p, first, last):
                    n = s + 1
                    if not first:
                        sums(dve, s - 1)
                    maxima(dve, s, 0)
                    maxima(dve, s, 1)
                    if not last:
                        centre(dve, n, 1 - p)
                    maxima(dve, s, 2)
                    maxima(dve, s, 3)
                    split_max(dve, s)
                    if not last:
                        normalise(dve, n)
                    if not first:
                        residual(dve, s - 1, 1 - p)
                    if not last:
                        qk_out(dve, n, 0)
                        qk_out(dve, n, 1)
                        v_out(dve, n, 1 - p)
                    weighed_out(dve, s, 0)
                    if not last:
                        v_rem_out(dve, n, 1 - p)
                    for g in range(1, GROUPS):
                        weighed_out(dve, s, g)
                each_step(dve, step)
                sums(dve, seqs - 1)
                residual(dve, seqs - 1, 1)

            @block.scalar
            def _(act):
                act.preload_act_table_set("natural_log_exp_and_others")
                act.wait_ge(sem["const"], 9)
                square(act, 0)
                inv_std(act, 0)
                repeat_last(act, 0)
                for which in range(2):
                    first_part(act, 0, which)
                    second_part(act, 0, which)

                def step(s, p, first, last):
                    n = s + 1
                    if not first:
                        inv_sums(act, s - 1)
                    if not last:
                        square(act, n)
                        inv_std(act, n)
                        repeat_last(act, n)
                    max_rows(act, s)
                    if not last:
                        first_part(act, n, 0)
                        first_part(act, n, 1)
                    exps(act, s, 0)
                    if not last:
                        second_part(act, n, 0)
                        second_part(act, n, 1)
                    exps(act, s, 1)
                    exps(act, s, 2)
                    exps(act, s, 3)
                each_step(act, step)
                inv_sums(act, seqs - 1)

            @block.gpsimd
            def _(pool):
                add_tiles(pool, 0, 0)
                add_squares(pool, 0)
                add_norm(pool, 0, 0)
                for which in range(2):
                    rest_one(pool, 0, which)
                for which in range(2):
                    third_part(pool, 0, which)

                def step(s, p, first, last):
                    n = s + 1
                    if not last:
                        add_tiles(pool, n, 1 - p)
                    if not first:
                        divide(pool, s - 1)
                    if not last:
                        add_squares(pool, n)
                        add_norm(pool, n, 1 - p)
                        rest_one(pool, n, 0)
                        rest_one(pool, n, 1)
                        third_part(pool, n, 0)
                        third_part(pool, n, 1)
                each_step(pool, step)
                divide(pool, seqs - 1)


def attn2_phase(nc, dram, h1_scratch, x2_scratch, seqs):
    with ExitStack() as ctx:
        sb = lambda name, shape, dt=F32: ctx.enter_context(nc.sbuf_tensor(name, shape, dt))
        RT = HPG + 1
        wqn_t = sb("b_wqn_t", [P, GROUPS, D])
        wkb_t = sb("b_wkb_t", [P, GROUPS, LAT])
        wo_n = sb("b_wo_n", [P, GROUPS, D])
        wq_nope = sb("b_wq_nope", [P, DT, GROUPS, P])
        wo = sb("b_wo", [P, GROUPS, D])
        wq_rope = sb("b_wq_rope", [P, DT, GROUPS, P])
        wkva = sb("b_wkva", [P, DT, P])
        w_ln = sb("b_w_ln", [P, DT])
        rope_cos = sb("b_rope_cos", [P, RT, T])
        rope_sin = sb("b_rope_sin", [P, RT, T])
        ones_avg = sb("b_ones_avg", [P, P])
        ones = sb("b_ones", [P, Q])
        eps = sb("b_eps", [P, 1])
        waited = sb("b_waited", [1, 1])
        masks_f = sb("b_masks_f", [P, 2 * P + T + REM])
        masks = sb("b_masks", [P, 2 * P + T + REM], BF16)
        mask_main, mask_main_t = masks[:, 0:P], masks[:, P:2 * P]
        mask_rem, mask_rem_t = masks[:, 2 * P:2 * P + T], masks[0:REM, 2 * P + T:]
        ident_f = sb("b_ident_f", [P, P])
        ident = sb("b_ident", [P, P], BF16)
        onehot_f = sb("b_onehot_f", [40, HEADS + GROUPS, P])
        onehot = sb("b_onehot", [40, HEADS + GROUPS, P], BF16)
        x = [sb(f"b_x{i}", [P, DT, T]) for i in range(2)]
        xs = sb("b_xs", [P, T])
        xc = sb("b_xc", [P, DT, T])
        sq = sb("b_sq", [P, DT, T])
        sqs = sb("b_sqs", [P, T])
        ln_var = sb("b_ln_var", [P, T])
        rstd = sb("b_rstd", [P, T])
        norm_a = sb("b_norm_a", [P, T])
        norm_b = sb("b_norm_b", [P, T])
        ln_rms = sb("b_ln_rms", [P, T])
        inv_rms = sb("b_inv_rms", [P, T])
        both = sb("b_both", [P, T])
        x1 = [sb(f"b_x1{i}", [P, DT, T]) for i in range(2)]
        xr = sb("b_xr", [P, DT, T])
        nope = [sb(f"b_nope{i}", [P, GROUPS, T], F32R) for i in range(2)]
        raw = sb("b_raw", [P, RT, T])
        swapped = sb("b_swapped", [P, RT, T])
        with_cos = sb("b_with_cos", [P, RT, T])
        with_sin = sb("b_with_sin", [P, RT, T])
        roped = [sb(f"b_roped{i}", [P, RT, T]) for i in range(2)]
        roped_hi = [sb(f"b_roped_hi{i}", [P, RT, T], F32R) for i in range(2)]
        roped_lo = [sb(f"b_roped_lo{i}", [P, RT, T], F32R) for i in range(2)]
        stacks = [sb(f"b_stacks{i}", [P, HEADS * T + Q - REM], F32R) for i in range(2)]
        v_main = [sb(f"b_v{i}", [P, LAT]) for i in range(2)]
        v_rem = [sb(f"b_vrem{i}", [REM, LAT]) for i in range(2)]
        nmax = sb("b_nmax", [P, HEADS + GROUPS])
        nmax_parts = sb("b_nmax_parts", [P, 2, HEADS + GROUPS], BF16)
        nt = sb("b_nt", [40, P], BF16)
        prob = [sb(f"b_prob{i}", [P, HPG, P]) for i in range(2)]
        prob_q = sb("b_prob_q", [P, GROUPS, HPG, REM])
        prob_qq = sb("b_prob_qq", [REM, GROUPS, HPG, REM])
        ouz = sb("b_ouz", [P, 2, GROUPS, T])
        lnz = sb("b_lnz", [P, GROUPS, T])
        rz = sb("b_rz", [P, GROUPS, T])
        ot = sb("b_ot", [P, GROUPS, T])
        x2 = [sb(f"b_x2{i}", [P, DT, T]) for i in range(2)]
        ps = ctx.enter_context(nc.psum_tensor("b_psum", [P, 8, 512], F32))
        sem = names(ctx, nc, "b", "weights const absorb absorbed xload xs mean xc sq sqs var lnv rstd na nb lnr ir both x1 xr "
                    "qn qr qnh qnl raw cos swap sin rope rhi rlo stack v vout "
                    "s max nm1 nm2 nmt nt st exp expr_in expr pv pvr ou oz lnz rz ot wo x2 store")
        EV = sem
        members = range(HPG)

        def place(p, G, m, a, b):
            at = (HPG * G + m) * T
            return stacks[p][:, at + a:at + b]

        def places(p):
            return stacks[p][:, 0:HEADS * T].rearrange("p (h j) -> p h j", j=T)

        def load_x(sp, n, q):
            token = n * T
            need_all(sp, (EV["xc"], n - 1), (EV["xload"], 16 * n))
            sp.dma_start(x[q][:], h1_scratch[:, :, bass.ds(token, T)]).then_inc(EV["xload"], 16)

        def stack(sp, n, q):
            for slot, (made, src) in enumerate((("qnh", nope[0]), ("rhi", roped_hi[q]), ("qnl", nope[1]), ("rlo", roped_lo[q]))):
                if slot == 0:
                    need_all(sp, (EV["expr_in"], n - 1), (EV["st"], GROUPS * (n - 1)), (EV[made], n + 1))
                else:
                    sp.wait_ge(EV[made], n + 1)
                for j in range(HPG):
                    sp.dma_start(stacks[q][Q * slot:Q * slot + Q, j * GROUPS * T:(j + 1) * GROUPS * T].bitcast(F32),
                                 src[Q * j:Q * j + Q, 0:GROUPS, :].rearrange("p g j -> p (g j)").bitcast(F32)).then_inc(EV["stack"], 16)

        def store_x2(sp, s, p):
            token = s * T
            need_all(sp, (EV["x2"], s + 1), (EV["store"], 16 * (s + 1)))
            sp.dma_start(x2_scratch[:, :, bass.ds(token, T)], x2[p][:]).then_inc(EV["store"], 16)

        def mean(pe, n):
            pe.wait_ge(EV["xs"], n + 1)
            need(pe, EV["expr"], n - 1)
            pe.matmul(ps[:, 6, 0:T], ones_avg[:], xs[:], start=True, stop=True).then_inc(EV["mean"], 1)

        def var(pe, n):
            pe.wait_ge(EV["sqs"], n + 1)
            pe.wait_ge(EV["xc"], n + 1)
            pe.matmul(ps[:, 6, 0:T], ones_avg[:], sqs[:], start=True, stop=True).then_inc(EV["var"], 1)

        def project_nope(pe, n):
            pe.wait_ge(EV["xr"], n + 1)
            need(pe, EV["max"], GROUPS * n)
            for g in range(GROUPS):
                for k in range(DT):
                    mm = pe.matmul(ps[:, g // 2, (g % 2) * T:(g % 2 + 1) * T], wq_nope[:, k, g, :], xr[:, k, :],
                                   start=(k == 0), stop=(k == DT - 1))
            mm.then_inc(EV["qn"], 1)

        def project_rope(pe, n):
            for g in range(RT):
                for k in range(DT):
                    w = wq_rope[:, k, g, :] if g < GROUPS else wkva[:, k, :]
                    mm = pe.matmul(ps[:, 2 + g // 3, (g % 3) * T:(g % 3 + 1) * T], w, xr[:, k, :],
                                   start=(k == 0), stop=(k == DT - 1))
            mm.then_inc(EV["qr"], 1)

        def project_v(pe, n):
            pe.wait_ge(EV["qnl"], n + 1)
            for k in range(DT):
                pe.matmul(ps[:, 0, 0:LAT], xr[:, k, 0:P], wkva[:, k, 0:LAT], start=(k == 0), stop=(k == DT - 1))
            for k in range(DT):
                mm = pe.matmul(ps[0:REM, 0, LAT:2 * LAT], xr[:, k, P:T], wkva[:, k, 0:LAT], start=(k == 0), stop=(k == DT - 1))
            mm.then_inc(EV["v"], 1)

        def scores(pe, s, p, G):
            if G == 0:
                pe.wait_ge(EV["stack"], 16 * 16 * (s + 1))
                pe.wait_ge(EV["vout"], s + 1)
                pe.wait_ge(EV["raw"], s + 1)
                pe.wait_ge(EV["qnl"], s + 1)
            else:
                need(pe, EV["max"], GROUPS * s + G - 1)
            b, br = ps[:, G % 2, :], ps[:, 2 + G % 2, 0:T]
            keys = roped[p][:, GROUPS, :]
            pe.matmul(b, ident[:], spread(mask_main, 1, HPG), start=True, stop=False)
            for m in members:
                pe.matmul(b[:, m * P:(m + 1) * P], place(p, G, m, 0, P).bitcast(F32), keys[:, 0:P], start=False, stop=(m == HPG - 1))
            pe.matmul(br, ident[:], mask_rem, start=True, stop=False)
            for m in members:
                mm = pe.matmul(br[Q * m:Q * m + Q], place(p, G, m, P, PAD_T).bitcast(F32), keys, start=False, stop=True)
            mm.then_inc(EV["s"], 1)

        def turn_max(pe, s, n_var):
            pe.wait_ge(EV["nm2"], s + 1)
            need(pe, EV["nb"], n_var)
            pe.matmul(ps[0:40, 6, 0:P], nmax_parts[:].rearrange("p a c -> p (a c)"), ident[:],
                      start=True, stop=True).then_inc(EV["nmt"], 1)

        def scores_t(pe, s, p, G):
            if G == 0:
                pe.wait_ge(EV["nt"], s + 1)
            need(pe, EV["exp"], GROUPS * s + G - 1)
            b = ps[:, 4 + G % 2, :]
            pe.matmul(b, ident[:], spread(mask_main_t, 1, HPG), start=True, stop=False)
            for m in members:
                pe.matmul(b[:, m * P:(m + 1) * P], onehot[:, HPG * G + m, :], nt[:], start=False, stop=False)
            q = places(p)[:, HPG * G:HPG * G + HPG, 0:P]
            pe.matmul(b, roped_hi[p][:, GROUPS, 0:P], q, start=False, stop=False)
            pe.matmul(b, roped_lo[p][:, GROUPS, 0:P], q, start=False, stop=True).then_inc(EV["st"], 1)

        def scores_t_rem(pe, s, p):
            pe.wait_ge(EV["nt"], s + 1)
            b, bb = ps[:, 6, 0:2 * P], ps[0:REM, 6, 2 * P:4 * P]
            q = places(p)[:, :, P:T]
            rem_max = nt[:].rearrange("r (m q) -> r m q", q=Q)[:, :, 0:REM]
            w = HPG * REM
            pe.matmul(b, roped_hi[p][:, GROUPS, 0:P], q, start=True, stop=False)
            pe.matmul(b, roped_lo[p][:, GROUPS, 0:P], q, start=False, stop=False)
            for G in range(GROUPS):
                pe.matmul(b[:, G * w:(G + 1) * w], onehot[:, HEADS + G, :], rem_max, start=False, stop=(G == GROUPS - 1))
            pe.matmul(bb, roped[p][:, GROUPS, P:T], q.bitcast(F32), start=True, stop=False)
            pe.matmul(bb, ident[0:REM, 0:REM], spread(mask_rem_t, 1, HEADS), start=False, stop=False)
            for G in range(GROUPS):
                mm = pe.matmul(bb[:, G * w:(G + 1) * w], onehot[:, HEADS + G, 0:REM], rem_max, start=False, stop=(G == GROUPS - 1))
            mm.then_inc(EV["expr_in"], 1)

        def weigh(pe, s, p, G):
            pe.wait_ge(EV["exp"], GROUPS * s + G + 1)
            if G == 0:
                need(pe, EV["x2"], s)
            else:
                pe.wait_ge(EV["ou"], GROUPS * s + G)
            for m in members:
                pe.matmul(ps[Q * m:Q * m + Q, 7, 0:P], v_main[p][:], prob[G % 2][:, m, :], start=True, stop=True)
            for m in members:
                mm = pe.matmul(ps[Q * m:Q * m + Q, 7, P:2 * P], ones[:], prob[G % 2][:, m, :], start=True, stop=True)
            mm.then_inc(EV["pv"], 1)

        def weigh_rem(pe, s, p):
            pe.wait_ge(EV["expr"], s + 1)
            pe.wait_ge(EV["ou"], GROUPS * (s + 1))
            for m in members:
                for i, (v, vr) in enumerate(((v_main[p][:], v_rem[p][:]), (ones[:], ones[0:REM, :]))):
                    o = ps[Q * m:Q * m + Q, 7, i * HPG * REM:(i + 1) * HPG * REM]
                    pe.matmul(o, v, prob_q[:, :, m, :], start=True, stop=False)
                    mm = pe.matmul(o, vr, prob_qq[:, :, m, :], start=False, stop=True)
            mm.then_inc(EV["pvr"], 1)

        def project_out(pe, s):
            pe.wait_ge(EV["ot"], s + 1)
            pe.wait_ge(EV["oz"], s + 1)
            for t in range(DT):
                for G in range(GROUPS):
                    mm = pe.matmul(ps[:, 7, t * T:(t + 1) * T], wo[:, G, t * P:(t + 1) * P], ot[:, G, :],
                                   start=(G == 0), stop=(G == GROUPS - 1))
            mm.then_inc(EV["wo"], 1)

        def centre(dve, n, q):
            dve.wait_ge(EV["mean"], n + 1)
            dve.tensor_tensor(xc[:], x[q][:], spread(ps[:, 6, 0:T], 1, DT), ALU.subtract).then_inc(EV["xc"], 1)

        def rms_terms(dve, n):
            dve.wait_ge(EV["rstd"], n + 1)
            dve.tensor_tensor(norm_a[:], rstd[:], ps[:, 6, 0:T], ALU.mult).then_inc(EV["na"], 1)
            dve.wait_ge(EV["na"], n + 1)
            dve.tensor_tensor(norm_b[:], norm_a[:], rstd[:], ALU.mult).then_inc(EV["nb"], 1)

        def rms_norm(dve, n):
            dve.wait_ge(EV["ir"], n + 1)
            dve.tensor_tensor(both[:], rstd[:], inv_rms[:], ALU.mult).then_inc(EV["both"], 1)
            dve.wait_ge(EV["both"], n + 1)
            for t in range(DT):
                last = dve.scalar_tensor_tensor(out=xr[:, t, :], in0=xc[:, t, :], scalar=w_ln[:, t:t + 1], in1=both[:],
                                                op0=ALU.mult, op1=ALU.mult)
            last.then_inc(EV["xr"], 1)

        def nope_low(dve, n):
            dve.wait_ge(EV["qnh"], n + 1)
            for c in range(2):
                last = dve.tensor_tensor(nope[1][:, 2 * c:2 * c + 2, :], ps[:, c, 0:2 * T].rearrange("p (g j) -> p g j", g=2),
                                         nope[0][:, 2 * c:2 * c + 2, :].bitcast(F32), ALU.subtract)
            last.then_inc(EV["qnl"], 1)

        def rotate(dve, n, q):
            dve.wait_ge(EV["raw"], n + 1)
            dve.memset(waited[:], 0.0)
            dve.stream_shuffle(swapped[:].rearrange("p a b -> p (a b)"), raw[:].rearrange("p a b -> p (a b)"),
                               [i ^ 1 for i in range(Q)]).then_inc(EV["swap"], 1)
            dve.wait_ge(EV["swap"], n + 1)
            dve.tensor_tensor(with_sin[:], swapped[:], rope_sin[:], ALU.mult).then_inc(EV["sin"], 1)
            dve.wait_ge(EV["sin"], n + 1)
            dve.wait_ge(EV["cos"], n + 1)
            dve.tensor_tensor(roped[q][:], with_sin[:], with_cos[:], ALU.add).then_inc(EV["rope"], 1)

        def v_out(dve, n, q):
            dve.wait_ge(EV["v"], n + 1)
            dve.tensor_copy(v_main[q][:], ps[:, 0, 0:LAT])
            dve.tensor_copy(v_rem[q][:], ps[0:REM, 0, LAT:2 * LAT]).then_inc(EV["vout"], 1)

        def maxima(dve, s, G):
            dve.wait_ge(EV["s"], GROUPS * s + G + 1)
            dve.tensor_reduce(nmax[:, HPG * G:HPG * G + HPG], ps[:, G % 2, :].rearrange("p (m k) -> p m k", m=HPG),
                              AX.X, ALU.max, negate=True)
            dve.tensor_reduce(nmax[:, HEADS + G:HEADS + G + 1], ps[:, 2 + G % 2, 0:T], AX.X, ALU.max,
                              negate=True).then_inc(EV["max"], 1)

        def split_max(dve, s):
            dve.wait_ge(EV["max"], GROUPS * (s + 1))
            dve.tensor_copy(nmax_parts[:, 0, :], nmax[:]).then_inc(EV["nm1"], 1)
            dve.wait_ge(EV["nm1"], s + 1)
            dve.tensor_tensor(nmax_parts[:, 1, :], nmax[:], nmax_parts[:, 0, :], ALU.subtract).then_inc(EV["nm2"], 1)

        def weighed_out(dve, s, G):
            dve.wait_ge(EV["pv"], GROUPS * s + G + 1)
            if G == 0:
                need(dve, EV["ot"], s)
            dve.tensor_copy(ouz[:, :, G, 0:P], ps[:, 7, 0:2 * P].rearrange("p (a q) -> p a q", a=2)).then_inc(EV["ou"], 1)

        def weighed_rem_out(dve, s):
            dve.wait_ge(EV["pvr"], s + 1)
            w = HPG * REM
            for i in range(2):
                last = dve.tensor_copy(ouz[:, i, :, P:T], ps[:, 7, i * w:(i + 1) * w].rearrange("p (g q) -> p g q", q=REM))
            last.then_inc(EV["oz"], 1)

        def residual(dve, s, p):
            dve.wait_ge(EV["wo"], s + 1)
            need(dve, EV["store"], 16 * (s + 1))
            dve.wait_ge(EV["x1"], s + 1)
            dve.tensor_tensor(x2[p][:], ps[:, 7, 0:2 * T].rearrange("p (t j) -> p t j", t=DT), x1[p][:],
                              ALU.add).then_inc(EV["x2"], 1)

        def square(act, n):
            act.wait_ge(EV["xc"], n + 1)
            act.activation(sq[:], xc[:], ACT.Square).then_inc(EV["sq"], 1)

        def inv_std(act, n):
            act.wait_ge(EV["var"], n + 1)
            act.activation(ln_var[:], ps[:, 6, 0:T], ACT.Ln, bias=eps[:]).then_inc(EV["lnv"], 1)
            act.wait_ge(EV["lnv"], n + 1)
            act.activation(rstd[:], ln_var[:], ACT.Exp, scale=-0.5).then_inc(EV["rstd"], 1)

        def inv_mean_square(act, n):
            act.wait_ge(EV["nb"], n + 1)
            act.activation(ln_rms[:], norm_b[:], ACT.Ln, bias=eps[:]).then_inc(EV["lnr"], 1)
            act.wait_ge(EV["lnr"], n + 1)
            act.activation(inv_rms[:], ln_rms[:], ACT.Exp, scale=-0.5).then_inc(EV["ir"], 1)

        def nope_high(act, n):
            act.wait_ge(EV["qn"], n + 1)
            need(act, EV["stack"], 16 * 16 * n)
            for c in range(2):
                last = act.activation(nope[0][:, 2 * c:2 * c + 2, :], ps[:, c, 0:2 * T].rearrange("p (g j) -> p g j", g=2), ACT.Copy)
            last.then_inc(EV["qnh"], 1)

        def rope_raw(act, n):
            act.wait_ge(EV["qr"], n + 1)
            act.activation(raw[:, 0:3, :], ps[:, 2, 0:3 * T].rearrange("p (g j) -> p g j", g=3), ACT.Copy)
            act.activation(raw[:, 3:5, :], ps[:, 3, 0:2 * T].rearrange("p (g j) -> p g j", g=2), ACT.Copy).then_inc(EV["raw"], 1)

        def rope_high(act, n, q):
            act.wait_ge(EV["rope"], n + 1)
            act.activation(roped_hi[q][:], roped[q][:], ACT.Copy).then_inc(EV["rhi"], 1)

        def max_rows(act, s):
            act.wait_ge(EV["nmt"], s + 1)
            act.activation(nt[:], ps[0:40, 6, 0:P], ACT.Copy).then_inc(EV["nt"], 1)

        def exps(act, s, G):
            act.wait_ge(EV["st"], GROUPS * s + G + 1)
            need(act, EV["pv"], GROUPS * s + G - 1)
            act.activation(prob[G % 2][:], ps[:, 4 + G % 2, :].rearrange("p (m q) -> p m q", m=HPG), ACT.Exp,
                           scale=0.125).then_inc(EV["exp"], 1)

        def exps_rem(act, s):
            act.wait_ge(EV["expr_in"], s + 1)
            act.activation(prob_q[:].rearrange("p a b q -> p (a b q)"), ps[:, 6, 0:2 * P], ACT.Exp, scale=0.125)
            act.activation(prob_qq[:].rearrange("p a b q -> p (a b q)"), ps[0:REM, 6, 2 * P:4 * P], ACT.Exp,
                           scale=0.125).then_inc(EV["expr"], 1)

        def inv_sums(act, s):
            act.wait_ge(EV["oz"], s + 1)
            act.activation(lnz[:], ouz[:, 1], ACT.Ln).then_inc(EV["lnz"], 1)
            act.wait_ge(EV["lnz"], s + 1)
            act.activation(rz[:], lnz[:], ACT.Exp, scale=-1.0).then_inc(EV["rz"], 1)

        def add_tiles(pool, n, q):
            pool.wait_ge(EV["xload"], 16 * (n + 1))
            need(pool, EV["mean"], n)
            pool.tensor_tensor(xs[:], x[q][:, 0, :], x[q][:, 1, :], ALU.add).then_inc(EV["xs"], 1)

        def add_squares(pool, n):
            pool.wait_ge(EV["sq"], n + 1)
            pool.tensor_tensor(sqs[:], sq[:, 0, :], sq[:, 1, :], ALU.add).then_inc(EV["sqs"], 1)

        def layer_norm(pool, n, q):
            pool.wait_ge(EV["rstd"], n + 1)
            need(pool, EV["x2"], n - 1)
            pool.tensor_tensor(x1[q][:], xc[:], spread(rstd[:], 1, DT), ALU.mult).then_inc(EV["x1"], 1)

        def times_cos(pool, n):
            pool.wait_ge(EV["raw"], n + 1)
            pool.tensor_tensor(with_cos[:], raw[:], rope_cos[:], ALU.mult).then_inc(EV["cos"], 1)

        def rope_low(pool, n, q):
            pool.wait_ge(EV["rhi"], n + 1)
            pool.tensor_tensor(roped_lo[q][:], roped[q][:], roped_hi[q][:].bitcast(F32), ALU.subtract).then_inc(EV["rlo"], 1)

        def divide(pool, s):
            pool.wait_ge(EV["rz"], s + 1)
            if isinstance(s, int):
                need(pool, EV["wo"], s)
            pool.tensor_tensor(ot[:], ouz[:, 0], rz[:], ALU.mult).then_inc(EV["ot"], 1)

        def each_step(engine, step):
            step(0, 0, True, False)
            if seqs > 2:
                with engine.Fori(0, (seqs - 2) // 2) as i:
                    step(i * 2 + 1, 1, False, False)
                    step(i * 2 + 2, 0, False, False)
            step(seqs - 1, 1, False, True)

        with nc.Block() as block:

            @block.sync
            def _(sp):
                for dst, name in ((wqn_t, "wqn_t"), (wkb_t, "wkb_t"), (wo_n, "wo_n"), (wq_rope, "wq_rope"), (wkva, "wkva"),
                                  (w_ln, "w_ln1"), (rope_cos, "rope_cos"), (rope_sin, "rope_sin"), (masks_f, "masks"),
                                  (ident_f, "ident"), (onehot_f, "onehot2")):
                    sp.dma_start(dst[:], dram[name]).then_inc(sem["weights"], 16)
                load_x(sp, 0, 0)
                stack(sp, 0, 0)

                def step(s, p, first, last):
                    if not last:
                        load_x(sp, s + 1, 1 - p)
                    if not first:
                        store_x2(sp, s - 1, 1 - p)
                    if not last:
                        stack(sp, s + 1, 1 - p)
                each_step(sp, step)
                store_x2(sp, seqs - 1, 1)
                sp.wait_ge(EV["store"], 16 * (seqs + 1))

            @block.tensor
            def _(pe):
                pe.wait_ge(sem["weights"], 176)
                for j in range(HPG):
                    for t in range(DT):
                        for g in range(GROUPS):
                            r = slice(Q * j, Q * j + Q)
                            pe.matmul(ps[:, j, (t * GROUPS + g) * LAT:(t * GROUPS + g + 1) * LAT],
                                      wqn_t[r, g, t * P:(t + 1) * P], wkb_t[r, g, :], start=True, stop=True)
                for j in range(HPG):
                    for g in range(GROUPS):
                        r = slice(Q * j, Q * j + Q)
                        mm = pe.matmul(ps[Q * g:Q * g + Q, 4 + j, 0:D], wkb_t[r, g, :], wo_n[r, g, :], start=True, stop=True)
                mm.then_inc(sem["absorb"], 1)
                pe.wait_ge(sem["absorbed"], 2)
                pe.wait_ge(sem["const"], 6)
                mean(pe, 0)
                var(pe, 0)
                project_nope(pe, 0)
                project_rope(pe, 0)
                project_v(pe, 0)

                def step(s, p, first, last):
                    n = s + 1
                    scores(pe, s, p, 0)
                    scores(pe, s, p, 1)
                    if not last:
                        mean(pe, n)
                    scores(pe, s, p, 2)
                    scores(pe, s, p, 3)
                    if not last:
                        var(pe, n)
                    if not first:
                        project_out(pe, s - 1)
                    turn_max(pe, s, n + 1 if not last else n)
                    if not last:
                        project_nope(pe, n)
                    scores_t(pe, s, p, 0)
                    if not last:
                        project_rope(pe, n)
                    scores_t(pe, s, p, 1)
                    scores_t_rem(pe, s, p)
                    weigh(pe, s, p, 0)
                    if not last:
                        project_v(pe, n)
                    scores_t(pe, s, p, 2)
                    weigh(pe, s, p, 1)
                    scores_t(pe, s, p, 3)
                    weigh(pe, s, p, 2)
                    weigh(pe, s, p, 3)
                    weigh_rem(pe, s, p)
                each_step(pe, step)
                project_out(pe, seqs - 1)

            @block.vector
            def _(dve):
                dve.memset(ones_avg[:], 1.0 / D).then_inc(sem["const"], 1)
                dve.memset(ones[:], 1.0).then_inc(sem["const"], 1)
                dve.memset(eps[:], EPS)
                dve.memset(waited[:], 0.0).then_inc(sem["store"], 16)
                for i in range(2):
                    dve.memset(stacks[i][:, HEADS * T:].bitcast(F32), 0.0)
                dve.wait_ge(sem["weights"], 176)
                dve.tensor_copy(masks[:], masks_f[:]).then_inc(sem["const"], 1)
                dve.tensor_copy(ident[:], ident_f[:]).then_inc(sem["const"], 1)
                dve.tensor_copy(onehot[:], onehot_f[:]).then_inc(sem["const"], 2)
                dve.wait_ge(sem["absorb"], 1)
                for j in range(HPG):
                    last = dve.tensor_copy(wq_nope[:].rearrange("p t g (j r) -> p j (t g) r", j=HPG)[:, j],
                                           ps[:, j, 0:D].rearrange("p (a r) -> p a r", r=LAT))
                last.then_inc(sem["absorbed"], 1)
                dve.tensor_copy(wo[:], ps[:, 4:8, 0:D]).then_inc(sem["absorbed"], 1)
                centre(dve, 0, 0)
                rms_terms(dve, 0)
                rms_norm(dve, 0)
                nope_low(dve, 0)
                rotate(dve, 0, 0)
                v_out(dve, 0, 0)

                def step(s, p, first, last):
                    n = s + 1
                    maxima(dve, s, 0)
                    maxima(dve, s, 1)
                    if not last:
                        centre(dve, n, 1 - p)
                    maxima(dve, s, 2)
                    maxima(dve, s, 3)
                    split_max(dve, s)
                    if not last:
                        rms_terms(dve, n)
                        rms_norm(dve, n)
                    if not first:
                        residual(dve, s - 1, 1 - p)
                    if not last:
                        nope_low(dve, n)
                        rotate(dve, n, 1 - p)
                    weighed_out(dve, s, 0)
                    if not last:
                        v_out(dve, n, 1 - p)
                    for G in range(1, GROUPS):
                        weighed_out(dve, s, G)
                    weighed_rem_out(dve, s)
                each_step(dve, step)
                residual(dve, seqs - 1, 1)

            @block.scalar
            def _(act):
                act.preload_act_table_set("natural_log_exp_and_others")
                act.wait_ge(sem["const"], 6)
                square(act, 0)
                inv_std(act, 0)
                inv_mean_square(act, 0)
                nope_high(act, 0)
                rope_raw(act, 0)
                rope_high(act, 0, 0)

                def step(s, p, first, last):
                    n = s + 1
                    if not first:
                        inv_sums(act, s - 1)
                    if not last:
                        square(act, n)
                        inv_std(act, n)
                        inv_mean_square(act, n)
                    max_rows(act, s)
                    if not last:
                        nope_high(act, n)
                    exps(act, s, 0)
                    if not last:
                        rope_raw(act, n)
                    exps(act, s, 1)
                    exps_rem(act, s)
                    if not last:
                        rope_high(act, n, 1 - p)
                    exps(act, s, 2)
                    exps(act, s, 3)
                each_step(act, step)
                inv_sums(act, seqs - 1)

            @block.gpsimd
            def _(pool):
                add_tiles(pool, 0, 0)
                add_squares(pool, 0)
                layer_norm(pool, 0, 0)
                times_cos(pool, 0)
                rope_low(pool, 0, 0)

                def step(s, p, first, last):
                    n = s + 1
                    if not last:
                        add_tiles(pool, n, 1 - p)
                    if not first:
                        divide(pool, s - 1)
                    if not last:
                        add_squares(pool, n)
                        layer_norm(pool, n, 1 - p)
                        times_cos(pool, n)
                        rope_low(pool, n, 1 - p)
                each_step(pool, step)
                divide(pool, seqs - 1)


def moe_phase(nc, dram, h1_scratch, x2_scratch, out_dram, tokens, width):
    chunks = tokens // width
    tiles = width // P
    with ExitStack() as ctx:
        sb = lambda name, shape, dt=F32: ctx.enter_context(nc.sbuf_tensor(name, shape, dt))
        raw_up = sb("m_raw_up", [P, DT, 2, INNER])
        raw_down = sb("m_raw_down", [P, D])
        up_parts = [sb(f"m_up{i}", [P, ALL_E, DT, 2, INNER], F32R) for i in range(2)]
        down_parts = [sb(f"m_down{i}", [P, ALL_E, D], F32R) for i in range(2)]
        w_gate = sb("m_w_gate", [P, DT, EXPERTS])
        gate_bias = sb("m_gate_bias", [P, EXPERTS])
        order = sb("m_order", [P, EXPERTS])
        w_ln = sb("m_w_ln", [P, DT])
        ident = sb("m_ident", [P, P])
        expert_rows_f = sb("m_expert_rows_f", [2 * EXPERTS, EXPERTS, P])
        expert_rows = sb("m_expert_rows", [2 * EXPERTS, EXPERTS, P], F32R)
        ones_avg = sb("m_ones_avg", [P, P])
        eps = sb("m_eps", [P, 1])
        x2 = [sb(f"m_x2{i}", [P, DT, width]) for i in range(2)]
        both = [sb(f"m_both{i}", [P, DT, width]) for i in range(2)]
        sq = sb("m_sq", [P, DT, width])
        sqs = sb("m_sqs", [P, width])
        ln_sq = sb("m_ln_sq", [P, width])
        rstd = sb("m_rstd", [P, width])
        xn = sb("m_xn", [P, DT, width])
        xn_parts = [[sb(f"m_xn{i}_{k}", [P, DT, width], F32R) for k in range(2)] for i in range(2)]
        small = lambda name, *shape: sb(f"m_{name}", [P, tiles, *shape])
        logit, is_top, rank, first = (small(w, EXPERTS) for w in ("logit", "is_top", "rank", "first"))
        others, is_second, rank2, second = (small(w, EXPERTS) for w in ("others", "is_second", "rank2", "second"))
        share1, share2, comb = (small(w, EXPERTS) for w in ("share1", "share2", "comb"))
        top, best, top2, best2 = (small(w) for w in ("top", "best", "top2", "best2"))
        diff, ratio, total, weight1, weight2 = (small(w) for w in ("diff", "ratio", "total", "weight1", "weight2"))
        comb_parts = sb("m_comb_parts", [P, tiles, 2, EXPERTS], F32R)
        comb_rows = [sb(f"m_comb_rows{i}", [2 * EXPERTS, width], F32R) for i in range(2)]
        silu = [sb(f"m_silu{i}", [P, width]) for i in range(2)]
        gated = sb("m_gated", [P, width])
        hidden = [sb(f"m_hidden{i}", [P, width]) for i in range(2)]
        hidden_parts = [[sb(f"m_hidden{i}_{k}", [P, width], F32R) for k in range(2)] for i in range(2)]
        out = [sb(f"m_out{i}", [P, DT, width]) for i in range(2)]
        y = [ctx.enter_context(nc.psum_tensor(f"m_y{t}", [P, 512], F32)) for t in range(DT)]
        gu = [[ctx.enter_context(nc.psum_tensor(f"m_gu{i}_{w}", [P, 512], F32)) for w in range(2)] for i in range(2)]
        share = ctx.enter_context(nc.psum_tensor("m_share", [P, 512], F32))
        misc = ctx.enter_context(nc.psum_tensor("m_misc", [P, 512], F32))
        sem = names(ctx, nc, "m", "weights raw split_hi split_lo const x2load h1load sq sqs mean lnsq rstd xn xnh xnl logits route diff ratio "
                    "combT rows gu share silu gated hidden hi lo down sum out store")
        ROUTE = 20
        places = range(ALL_E)

        def load_x2(sp, n, q):
            token = n * width
            need_all(sp, (sem["xn"], n - 1), (sem["sum"], n - 1), (sem["x2load"], 16 * n))
            sp.dma_start(x2[q][:], x2_scratch[:, :, bass.ds(token, width)]).then_inc(sem["x2load"], 16)

        def load_h1(sp, n, q):
            token = n * width
            need_all(sp, (sem["out"], n - 1), (sem["h1load"], 16 * n))
            sp.dma_start(both[q][:], h1_scratch[:, :, bass.ds(token, width)]).then_inc(sem["h1load"], 16)

        def store(sp, c, p):
            token = c * width
            need_all(sp, (sem["out"], c + 1), (sem["store"], 16 * (c + 1)))
            sp.dma_start(out_dram[:, :, bass.ds(token, width)], out[p][:]).then_inc(sem["store"], 16)

        def mean_square(pe, n):
            pe.wait_ge(sem["sqs"], n + 1)
            need(pe, sem["rows"], n)
            pe.matmul(misc[:, 0:width], ones_avg[:], sqs[:], start=True, stop=True).then_inc(sem["mean"], 1)

        def logits(pe, n):
            pe.wait_ge(sem["xn"], n + 1)
            pe.wait_ge(sem["lnsq"], n + 1)
            for i in range(tiles):
                for k in range(DT):
                    mm = pe.matmul(misc[:, i * EXPERTS:(i + 1) * EXPERTS], xn[:, k, i * P:(i + 1) * P], w_gate[:, k, :],
                                   start=(k == 0), stop=(k == DT - 1))
            mm.then_inc(sem["logits"], 1)

        def turn_shares(pe, n):
            pe.wait_ge(sem["route"], ROUTE * (n + 1))
            for i in range(tiles):
                mm = pe.matmul(misc[0:2 * EXPERTS, i * P:(i + 1) * P],
                               comb_parts[:, i].rearrange("p a e -> p (a e)").bitcast(F32), ident[:], start=True, stop=True)
            mm.then_inc(sem["combT"], 1)

        def gate_up(pe, c, p, i):
            if i == 0:
                pe.wait_ge(sem["xnh"], c + 1)
                pe.wait_ge(sem["xnl"], c + 1)
            need(pe, sem["hidden"], ALL_E * c + i - 1)
            b = (p + i) % 2
            for w in range(2):
                for j, (a, x) in enumerate(((0, 0), (0, 1), (1, 0))):
                    for k in range(DT):
                        mm = pe.matmul(gu[b][w][:, 0:width], up_parts[a][:, i, k, w, :], xn_parts[p][x][:, k, :],
                                       start=(j == 0 and k == 0), stop=(j == 2 and k == DT - 1))
            mm.then_inc(sem["gu"], 1)

        def spread_share(pe, c, p, i):
            pe.wait_ge(sem["rows"], c + 1)
            need(pe, sem["hidden"], ALL_E * c + i)
            pe.matmul(share[:, 0:width], expert_rows[:, i - 1, :], comb_rows[p][:], start=True, stop=True).then_inc(sem["share"], 1)

        def down(pe, c, p, i):
            pe.wait_ge(sem["hi"], ALL_E * c + i + 1)
            if i == 0:
                need(pe, sem["out"], c)
            b = (p + i) % 2
            parts = ((0, 0), (1, 0), (0, 1))
            for j, (a, x) in enumerate(parts):
                if j == 2:
                    pe.wait_ge(sem["lo"], ALL_E * c + i + 1)
                for t in range(DT):
                    mm = pe.matmul(y[t][:, 0:width], down_parts[a][:, i, t * P:(t + 1) * P], hidden_parts[b][x][:],
                                   start=(i == 0 and j == 0), stop=(i == ALL_E - 1 and j == 2))
            mm.then_inc(sem["down"], 1)

        def normalise(dve, n, q):
            dve.wait_ge(sem["rstd"], n + 1)
            need(dve, sem["logits"], n)
            need(dve, sem["xnl"], n)
            for t in range(DT):
                last = dve.scalar_tensor_tensor(out=xn[:, t, :], in0=x2[q][:, t, :], scalar=w_ln[:, t:t + 1], in1=rstd[:],
                                                op0=ALU.mult, op1=ALU.mult)
            last.then_inc(sem["xn"], 1)

        def choose(dve, n):
            r = ROUTE * n
            route = sem["route"]
            dve.wait_ge(sem["logits"], n + 1)
            need(dve, sem["combT"], n)
            at = misc[:, 0:tiles * EXPERTS].rearrange("p (i e) -> p i e", e=EXPERTS)
            dve.tensor_tensor(logit[:], at, spread(gate_bias[:], 1, tiles), ALU.add).then_inc(route, 1)
            dve.wait_ge(route, r + 1)
            dve.tensor_reduce(top[:], logit[:], AX.X, ALU.max).then_inc(route, 1)
            dve.wait_ge(route, r + 2)
            dve.tensor_tensor(is_top[:], logit[:], spread(top[:], 2, EXPERTS), ALU.is_equal).then_inc(route, 1)
            dve.wait_ge(route, r + 3)
            dve.tensor_tensor(rank[:], is_top[:], spread(order[:], 1, tiles), ALU.mult).then_inc(route, 1)
            dve.wait_ge(route, r + 4)
            dve.tensor_reduce(best[:], rank[:], AX.X, ALU.max).then_inc(route, 1)
            dve.wait_ge(route, r + 5)
            dve.tensor_tensor(first[:], rank[:], spread(best[:], 2, EXPERTS), ALU.is_equal).then_inc(route, 1)
            dve.wait_ge(route, r + 6)
            dve.scalar_tensor_tensor(out=others[:], in0=first[:], scalar=NEG, in1=logit[:], op0=ALU.mult, op1=ALU.add).then_inc(route, 1)
            dve.wait_ge(route, r + 7)
            dve.tensor_reduce(top2[:], others[:], AX.X, ALU.max).then_inc(route, 1)
            dve.wait_ge(route, r + 8)
            dve.tensor_tensor(diff[:], top2[:], top[:], ALU.subtract).then_inc(sem["diff"], 1)
            dve.tensor_tensor(is_second[:], others[:], spread(top2[:], 2, EXPERTS), ALU.is_equal).then_inc(route, 1)
            dve.wait_ge(route, r + 9)
            dve.tensor_tensor(rank2[:], is_second[:], spread(order[:], 1, tiles), ALU.mult).then_inc(route, 1)
            dve.wait_ge(route, r + 10)
            dve.tensor_reduce(best2[:], rank2[:], AX.X, ALU.max).then_inc(route, 1)
            dve.wait_ge(route, r + 11)
            dve.tensor_tensor(second[:], rank2[:], spread(best2[:], 2, EXPERTS), ALU.is_equal).then_inc(route, 1)

        def shares(dve, n):
            r = ROUTE * n
            route = sem["route"]
            dve.wait_ge(sem["ratio"], n + 1)
            dve.tensor_scalar(total[:], ratio[:], 1.0, None, ALU.add).then_inc(route, 1)
            dve.wait_ge(route, r + 13)
            dve.reciprocal(weight1[:], total[:]).then_inc(route, 1)
            dve.wait_ge(route, r + 14)
            dve.tensor_tensor(weight2[:], ratio[:], weight1[:], ALU.mult).then_inc(route, 1)
            dve.tensor_tensor(share1[:], first[:], spread(weight1[:], 2, EXPERTS), ALU.mult).then_inc(route, 1)
            dve.wait_ge(route, r + 16)
            dve.tensor_tensor(share2[:], second[:], spread(weight2[:], 2, EXPERTS), ALU.mult).then_inc(route, 1)
            dve.wait_ge(route, r + 17)
            dve.tensor_tensor(comb[:], share1[:], share2[:], ALU.add).then_inc(route, 1)
            dve.wait_ge(route, r + 18)
            dve.tensor_copy(comb_parts[:, :, 0, :], comb[:]).then_inc(route, 1)
            dve.wait_ge(route, r + 19)
            dve.tensor_tensor(comb_parts[:, :, 1, :], comb[:], comb_parts[:, :, 0, :].bitcast(F32), ALU.subtract).then_inc(route, 1)

        def gate(dve, c, p, i):
            b = (p + i) % 2
            dve.wait_ge(sem["silu"], ALL_E * c + i + 1)
            need(dve, sem["lo"], ALL_E * c + i - 1)
            if i == 0:
                dve.tensor_tensor(hidden[b][:], gu[b][1][:, 0:width], silu[b][:], ALU.mult).then_inc(sem["hidden"], 1)
                return
            dve.tensor_tensor(gated[:], gu[b][1][:, 0:width], silu[b][:], ALU.mult).then_inc(sem["gated"], 1)
            dve.wait_ge(sem["gated"], EXPERTS * c + i)
            dve.wait_ge(sem["share"], EXPERTS * c + i)
            dve.tensor_tensor(hidden[b][:], gated[:], share[:, 0:width], ALU.mult).then_inc(sem["hidden"], 1)

        def finish(dve, c, p):
            dve.wait_ge(sem["down"], ALL_E * (c + 1))
            dve.wait_ge(sem["sum"], c + 1)
            need(dve, sem["store"], 16 * (c + 1))
            for t in range(DT):
                last = dve.tensor_tensor(out[p][:, t, :], y[t][:, 0:width], both[p][:, t, :], ALU.add)
            last.then_inc(sem["out"], 1)

        def square(act, n, q):
            act.wait_ge(sem["x2load"], 16 * (n + 1))
            act.activation(sq[:], x2[q][:], ACT.Square).then_inc(sem["sq"], 1)

        def inv_rms(act, n):
            act.wait_ge(sem["mean"], n + 1)
            act.activation(ln_sq[:], misc[:, 0:width], ACT.Ln, bias=eps[:]).then_inc(sem["lnsq"], 1)
            act.wait_ge(sem["lnsq"], n + 1)
            act.activation(rstd[:], ln_sq[:], ACT.Exp, scale=-0.5).then_inc(sem["rstd"], 1)

        def norm_high(act, n, q):
            act.wait_ge(sem["xn"], n + 1)
            need(act, sem["gu"], ALL_E * (n - 1))
            act.activation(xn_parts[q][0][:], xn[:], ACT.Copy).then_inc(sem["xnh"], 1)

        def share_ratio(act, n):
            act.wait_ge(sem["diff"], n + 1)
            act.activation(ratio[:], diff[:], ACT.Exp).then_inc(sem["ratio"], 1)

        def share_rows(act, n, q):
            act.wait_ge(sem["combT"], n + 1)
            need(act, sem["share"], EXPERTS * (n - 1))
            act.activation(comb_rows[q][:], misc[0:2 * EXPERTS, 0:width], ACT.Copy).then_inc(sem["rows"], 1)

        def silu_gate(act, c, p, i):
            b = (p + i) % 2
            act.wait_ge(sem["gu"], ALL_E * c + i + 1)
            act.activation(silu[b][:], gu[b][0][:, 0:width], ACT.Silu).then_inc(sem["silu"], 1)

        def hidden_high(act, c, p, i):
            b = (p + i) % 2
            act.wait_ge(sem["hidden"], ALL_E * c + i + 1)
            need(act, sem["down"], ALL_E * c + i - 1)
            act.activation(hidden_parts[b][0][:], hidden[b][:], ACT.Copy).then_inc(sem["hi"], 1)

        def add_squares(pool, n):
            pool.wait_ge(sem["sq"], n + 1)
            pool.tensor_tensor(sqs[:], sq[:, 0, :], sq[:, 1, :], ALU.add).then_inc(sem["sqs"], 1)

        def norm_low(pool, n, q):
            pool.wait_ge(sem["xnh"], n + 1)
            pool.tensor_tensor(xn_parts[q][1][:], xn[:], xn_parts[q][0][:].bitcast(F32), ALU.subtract).then_inc(sem["xnl"], 1)

        def add_residuals(pool, n, q):
            pool.wait_ge(sem["h1load"], 16 * (n + 1))
            pool.tensor_tensor(both[q][:], both[q][:], x2[q][:], ALU.add).then_inc(sem["sum"], 1)

        def hidden_low(pool, c, p, i):
            b = (p + i) % 2
            pool.wait_ge(sem["hi"], ALL_E * c + i + 1)
            pool.tensor_tensor(hidden_parts[b][1][:], hidden[b][:], hidden_parts[b][0][:].bitcast(F32),
                               ALU.subtract).then_inc(sem["lo"], 1)

        def each_step(engine, step):
            step(0, 0, True, False)
            if chunks > 2:
                with engine.Fori(0, (chunks - 2) // 2) as i:
                    step(i * 2 + 1, 1, False, False)
                    step(i * 2 + 2, 0, False, False)
            step(chunks - 1, 1, False, True)

        LOADS = 16 * 6
        with nc.Block() as block:

            @block.sync
            def _(sp):
                for dst, name in ((w_gate, "w_gate"), (gate_bias, "gate_bias"), (order, "order"), (w_ln, "w_ln2"),
                                  (ident, "ident"), (expert_rows_f, "expert_rows")):
                    sp.dma_start(dst[:], dram[name]).then_inc(sem["weights"], 16)
                load_x2(sp, 0, 0)
                load_h1(sp, 0, 0)
                for i in places:
                    need(sp, sem["split_lo"], i)
                    sp.dma_start(raw_up[:], dram["up"][:, i]).then_inc(sem["raw"], 16)
                    sp.dma_start(raw_down[:], dram["down"][:, i]).then_inc(sem["raw"], 16)

                def step(c, p, is_first, is_last):
                    if not is_last:
                        load_x2(sp, c + 1, 1 - p)
                        load_h1(sp, c + 1, 1 - p)
                    if not is_first:
                        store(sp, c - 1, 1 - p)
                each_step(sp, step)
                store(sp, chunks - 1, 1)
                sp.wait_ge(sem["store"], 16 * (chunks + 1))

            @block.tensor
            def _(pe):
                pe.wait_ge(sem["const"], 3)
                pe.wait_ge(sem["weights"], LOADS)
                mean_square(pe, 0)
                logits(pe, 0)
                turn_shares(pe, 0)
                pe.wait_ge(sem["split_lo"], ALL_E)

                def step(c, p, is_first, is_last):
                    for i in places:
                        gate_up(pe, c, p, i)
                        if i > 0:
                            spread_share(pe, c, p, i)
                        if i >= 2:
                            down(pe, c, p, i - 2)
                        elif not is_first:
                            down(pe, c - 1, 1 - p, ALL_E - 2 + i)
                        if not is_last:
                            if i == 1:
                                mean_square(pe, c + 1)
                            if i == 4:
                                logits(pe, c + 1)
                            if i == 6:
                                turn_shares(pe, c + 1)
                each_step(pe, step)
                for i in (ALL_E - 2, ALL_E - 1):
                    down(pe, chunks - 1, 1, i)

            @block.vector
            def _(dve):
                dve.memset(ones_avg[:], 1.0 / D).then_inc(sem["const"], 1)
                dve.memset(eps[:], EPS).then_inc(sem["const"], 1)
                dve.memset(ratio[:], 0.0).then_inc(sem["store"], 16)
                dve.wait_ge(sem["weights"], LOADS)
                dve.tensor_copy(expert_rows[:], expert_rows_f[:]).then_inc(sem["const"], 1)
                normalise(dve, 0, 0)
                choose(dve, 0)
                shares(dve, 0)
                for i in places:
                    dve.wait_ge(sem["split_hi"], i + 1)
                    dve.tensor_tensor(up_parts[1][:, i], raw_up[:], up_parts[0][:, i].bitcast(F32), ALU.subtract)
                    dve.tensor_tensor(down_parts[1][:, i], raw_down[:], down_parts[0][:, i].bitcast(F32),
                                      ALU.subtract).then_inc(sem["split_lo"], 1)

                def step(c, p, is_first, is_last):
                    for i in places:
                        gate(dve, c, p, i)
                        if i == 1 and not is_first:
                            finish(dve, c - 1, 1 - p)
                        if not is_last:
                            if i == 2:
                                normalise(dve, c + 1, 1 - p)
                            if i == 4:
                                choose(dve, c + 1)
                            if i == 5:
                                shares(dve, c + 1)
                each_step(dve, step)
                finish(dve, chunks - 1, 1)

            @block.scalar
            def _(act):
                act.preload_act_table_set("natural_log_exp_and_others")
                act.wait_ge(sem["const"], 2)
                square(act, 0, 0)
                inv_rms(act, 0)
                norm_high(act, 0, 0)
                share_ratio(act, 0)
                for i in places:
                    act.wait_ge(sem["raw"], 32 * (i + 1))
                    act.activation(up_parts[0][:, i], raw_up[:], ACT.Copy)
                    act.activation(down_parts[0][:, i], raw_down[:], ACT.Copy).then_inc(sem["split_hi"], 1)
                share_rows(act, 0, 0)
                act.preload_act_table_set("silu_and_others")

                def step(c, p, is_first, is_last):
                    if not is_last:
                        square(act, c + 1, 1 - p)
                    for i in places:
                        silu_gate(act, c, p, i)
                        hidden_high(act, c, p, i)
                        if not is_last:
                            if i == 1:
                                act.preload_act_table_set("natural_log_exp_and_others")
                                inv_rms(act, c + 1)
                                act.preload_act_table_set("silu_and_others")
                            if i == 3:
                                norm_high(act, c + 1, 1 - p)
                            if i == 4:
                                act.preload_act_table_set("natural_log_exp_and_others")
                                share_ratio(act, c + 1)
                                act.preload_act_table_set("silu_and_others")
                            if i == 6:
                                share_rows(act, c + 1, 1 - p)
                each_step(act, step)

            @block.gpsimd
            def _(pool):
                add_squares(pool, 0)
                norm_low(pool, 0, 0)
                add_residuals(pool, 0, 0)

                def step(c, p, is_first, is_last):
                    if not is_last:
                        add_squares(pool, c + 1)
                    for i in places:
                        hidden_low(pool, c, p, i)
                        if not is_last:
                            if i == 3:
                                norm_low(pool, c + 1, 1 - p)
                            if i == 5:
                                add_residuals(pool, c + 1, 1 - p)
                each_step(pool, step)


def host_layouts(a):
    f = {}
    seqs = a["x"].shape[0]

    def feature_tiles(w):
        return w.reshape(-1, P, w.shape[-1]).transpose(1, 0, 2)

    def column(v):
        return v.reshape(-1, P).T

    n = 4
    patches = a["x"].reshape(seqs, 3, n, 16, n, 16).transpose(1, 3, 5, 0, 2, 4).reshape(FEAT, seqs * n * n)
    f["patches"] = feature_tiles(patches)
    f["txt"] = a["txt"].transpose(2, 0, 1).reshape(DT, P, seqs, TXT_TOK).transpose(1, 2, 0, 3).reshape(P, -1)
    f["tok_w"] = feature_tiles(a["L0_tok_W"].T)
    f["tok_b"] = column(a["L0_tok_b"])
    f["pos"] = feature_tiles(a["L0_tok_pos_emb"].T)
    w = a["L0_attn_qkv_w"].T.reshape(D, HEADS, 3, HD1)
    b = a["L0_attn_qkv_b"].reshape(HEADS, 3, HD1)
    f["wqk"] = feature_tiles(w[:, :, 0:2].reshape(D, 2 * D)).reshape(P, DT, GROUPS, P)
    f["bqk"] = column(b[:, 0:2].ravel())
    f["wv"] = feature_tiles(w[:, :, 2].reshape(D, D))
    f["bv"] = np.broadcast_to(b[:, 2].reshape(1, D), (P, D))
    fcw = np.zeros((HPG, Q, GROUPS, D), np.float32)
    fcw[:, :HD1] = a["L0_attn_fc_w"].T.reshape(GROUPS, HPG, HD1, D).transpose(1, 2, 0, 3)
    f["fcw"] = fcw.reshape(P, GROUPS, D)
    f["fcb"] = column(a["L0_attn_fc_b"])
    f["w_ln1"] = column(a["L0_ffn_w_ln1"])
    wq = a["L0_ffn_Wq"].reshape(D, GROUPS, HPG, 2, NOPE)
    f["wqn_t"] = wq[:, :, :, 0].transpose(2, 3, 1, 0).reshape(P, GROUPS, D)
    f["wq_rope"] = feature_tiles(wq[:, :, :, 1].reshape(D, GROUPS * P)).reshape(P, DT, GROUPS, P)
    wkb = a["L0_ffn_Wkvb"].reshape(LAT, GROUPS, HPG, NOPE)
    f["wkb_t"] = wkb.transpose(2, 3, 1, 0).reshape(P, GROUPS, LAT)
    f["wo_n"] = a["L0_ffn_Wo"].reshape(GROUPS, HPG, 2, NOPE, D)[:, :, 0].transpose(1, 2, 0, 3).reshape(P, GROUPS, D)
    f["wkva"] = feature_tiles(np.concatenate([a["L0_ffn_Wkva"]] * 2, 1))
    f["w_ln2"] = column(a["L0_ffn_w_ln2"])
    f["w_gate"] = feature_tiles(a["L0_ffn_Wgate"])
    f["gate_bias"] = np.broadcast_to(a["L0_ffn_expert_bias"][None], (P, EXPERTS))
    up = np.stack([np.concatenate([a["L0_ffn_s" + w], a["L0_ffn_" + w]]) for w in ("Wg", "Wu")])
    f["up"] = up.reshape(2, ALL_E, DT, P, INNER).transpose(3, 1, 2, 0, 4)
    f["down"] = np.concatenate([a["L0_ffn_sWd"], a["L0_ffn_Wd"]]).transpose(1, 0, 2)
    f["order"] = np.broadcast_to(np.arange(EXPERTS, 0, -1, dtype=np.float32)[None], (P, EXPERTS))
    owner = np.arange(2 * EXPERTS)[:, None] % EXPERTS == np.arange(EXPERTS)[None]
    f["expert_rows"] = np.broadcast_to(owner.astype(np.float32)[:, :, None], (2 * EXPERTS, EXPERTS, P))
    half = np.arange(0, ROPE, 2, dtype=np.float32) / np.float32(ROPE)
    angle = np.outer(np.arange(T, dtype=np.float32), np.float32(1.0) / np.float32(100000.0) ** half).astype(np.float32)
    cos, sin = (np.repeat(c(angle).T, 2, 0).astype(np.float32) for c in (np.cos, np.sin))
    sin[0::2] *= -1
    cos_tiles, sin_tiles = np.ones((P, HPG + 1, T), np.float32), np.zeros((P, HPG + 1, T), np.float32)
    for quadrant in range(4):
        r = slice(Q * quadrant, Q * quadrant + Q)
        cos_tiles[r, :HPG], sin_tiles[r, :HPG] = cos[:, None], sin[:, None]
        if quadrant % 2:
            cos_tiles[r, HPG], sin_tiles[r, HPG] = cos, sin
    f["rope_cos"], f["rope_sin"] = cos_tiles, sin_tiles
    one, two = np.arange(P)[:, None], np.arange(P)[None, :]
    masks = np.zeros((P, 2 * P + T + REM), np.float32)
    masks[:, 0:P][two > one] = NEG
    masks[:, P:2 * P][one > two] = NEG
    last = np.where(one % Q < REM, P + one % Q, T)
    masks[:, 2 * P:2 * P + T][np.arange(T)[None, :] > last] = NEG
    masks[:REM, 2 * P + T:][one[:REM] > two[:, :REM]] = NEG
    f["masks"] = masks
    row, place = np.arange(2 * (HEADS + GROUPS))[:, None] % (HEADS + GROUPS), np.arange(HEADS + GROUPS)[None, :]
    f["onehot2"] = np.broadcast_to((row == place).astype(np.float32)[:, :, None], (40, HEADS + GROUPS, P))
    rows = np.arange(P)
    f["rem_mask"] = (rows % Q < REM).astype(np.float32)[:, None]
    f["ident"] = np.eye(P, dtype=np.float32)
    cols = np.arange(HEADS + GROUPS)
    owns = np.zeros((HEADS + GROUPS, HEADS), np.float32)
    for h in range(HEADS):
        owns[h, h] = owns[HEADS + h // HPG, h] = 1
    f["onehot1"] = np.broadcast_to(np.concatenate([owns, owns])[:, :, None], (40, HEADS, P))
    rem = np.zeros((41, HEADS, Q), np.float32)
    rem[:40, :, :REM] = np.concatenate([owns, owns])[:, :, None]
    rem[40, :, REM:] = NEG
    f["onehot1_rem"] = rem
    main = np.concatenate([cols < HEADS] * 2)
    f["nt_rows"] = np.stack([main, ~main], 1).astype(np.float32)
    return {k: np.ascontiguousarray(v) for k, v in f.items()}


def build(nc, dram, out, seqs):
    h1 = nc.dram_tensor("h1_scratch", [P, DT, seqs * T], F32).ap()
    x2 = nc.dram_tensor("x2_scratch", [P, DT, seqs * T], F32).ap()
    with nc.sbuf_tensor("embedded", [P, DT, seqs * IMG_TOK], F32) as embedded:
        embed_phase(nc, dram, embedded, seqs)
        attn1_phase(nc, dram, embedded, h1, seqs)
    attn2_phase(nc, dram, h1, x2, seqs)
    moe_phase(nc, dram, h1, x2, out, seqs * T, CHUNK)


def kernel(**inputs):
    import concourse.bacc as bacc
    from concourse.bass_utils import run_bass_kernel_spmd

    laid = host_layouts({name: np.asarray(value) for name, value in inputs.items()})
    nc = bacc.Bacc("TRN2", target_bir_lowering=False, num_devices=1)
    arrays = {f"in_{name}": value for name, value in laid.items()}
    dram = {name: nc.dram_tensor(f"in_{name}", value.shape, F32, kind="ExternalInput").ap() for name, value in laid.items()}
    out = nc.dram_tensor("out", [P, DT, SEQS * T], F32, kind="ExternalOutput").ap()
    build(nc, dram, out, SEQS)
    result = run_bass_kernel_spmd(nc, [arrays], core_ids=[0])
    got = np.asarray(result.results[0]["out"])
    return np.ascontiguousarray(got.reshape(P, DT, SEQS, T).transpose(2, 3, 1, 0)).reshape(SEQS, T, D)
```

```python
from contextlib import ExitStack

import numpy as np

import concourse.bass as bass
from concourse import mybir

F32 = mybir.dt.float32
F32R = mybir.dt.float32r
BF16 = mybir.dt.bfloat16
ALU = mybir.AluOpType
ACT = mybir.ActivationFunctionType
AX = mybir.AxisListType

P = 128
SEQS, IMG_TOK, TXT_TOK, D = 64, 16, 128, 256
T = IMG_TOK + TXT_TOK
DT = D // P
HEADS, GROUPS, HPG = 16, 4, 4
Q = 32
REM = T - P
PAD_T = P + Q
HD1 = D // HEADS
SPLIT = 6
PARTS = 3
FEAT = 768
KT_EMB = FEAT // P
EPS = 1e-5
NOPE = ROPE = LAT = 32
EXPERTS, ALL_E, TOPK, INNER = 8, 9, 2, 128
NEG = -1.0e30
CHUNK = 512


def need(engine, semaphore, value):
    if isinstance(value, int) and value <= 0:
        return
    engine.wait_ge(semaphore, value)


def in_register(engine, value):
    if isinstance(value, int):
        return value
    register = engine.alloc_register()
    engine.reg_mov(register, value)
    return register


def need_all(engine, *waits):
    waits = [(semaphore, in_register(engine, value)) for semaphore, value in waits]
    for semaphore, value in waits:
        need(engine, semaphore, value)


def spread(ap, axis, n):
    a = ap.unsqueeze(axis)
    shape = list(a.shape)
    shape[axis] = n
    return a.to_broadcast(shape)


def names(ctx, nc, prefix, words):
    return {w: ctx.enter_context(nc.semaphore(f"{prefix}_{w}")) for w in words.split()}


def embed_phase(nc, dram, embedded, seqs):
    tokens = seqs * IMG_TOK
    width = min(CHUNK, tokens)
    chunks = tokens // width
    with ExitStack() as ctx:
        sb = lambda name, shape, dt=F32: ctx.enter_context(nc.sbuf_tensor(name, shape, dt))
        weights = sb("e_weights", [P, KT_EMB, D])
        patches = sb("e_patches", [P, KT_EMB, width])
        bias = sb("e_bias", [P, DT])
        pos = sb("e_pos", [P, DT, IMG_TOK])
        out = [ctx.enter_context(nc.psum_tensor(f"e_out{t}", [P, width], F32)) for t in range(DT)]
        sem = names(ctx, nc, "e", "weights patches product embedded")
        with nc.Block() as block:

            @block.sync
            def _(sp):
                sp.dma_start(weights[:], dram["tok_w"]).then_inc(sem["weights"], 16)
                sp.dma_start(bias[:], dram["tok_b"]).then_inc(sem["weights"], 16)
                sp.dma_start(pos[:], dram["pos"]).then_inc(sem["weights"], 16)
                for c in range(chunks):
                    need(sp, sem["product"], c)
                    sp.dma_start(patches[:], dram["patches"][:, :, c * width:(c + 1) * width]).then_inc(sem["patches"], 16)

            @block.tensor
            def _(pe):
                pe.wait_ge(sem["weights"], 48)
                for c in range(chunks):
                    pe.wait_ge(sem["patches"], 16 * (c + 1))
                    need(pe, sem["embedded"], c)
                    for t in range(DT):
                        for k in range(KT_EMB):
                            mm = pe.matmul(out[t][:], weights[:, k, t * P:(t + 1) * P], patches[:, k, :],
                                           start=(k == 0), stop=(k == KT_EMB - 1))
                    mm.then_inc(sem["product"], 1)

            @block.vector
            def _(dve):
                n = width // IMG_TOK
                for c in range(chunks):
                    dve.wait_ge(sem["product"], c + 1)
                    for t in range(DT):
                        last = dve.scalar_tensor_tensor(
                            out=embedded[:, t, c * width:(c + 1) * width].rearrange("p (s n) -> p s n", n=IMG_TOK),
                            in0=out[t][:].rearrange("p (s n) -> p s n", n=IMG_TOK), scalar=bias[:, t:t + 1],
                            in1=spread(pos[:, t, :], 1, n), op0=ALU.add, op1=ALU.add)
                    last.then_inc(sem["embedded"], 1)


def attn1_phase(nc, dram, embedded, h1_scratch, seqs):
    with ExitStack() as ctx:
        sb = lambda name, shape, dt=F32: ctx.enter_context(nc.sbuf_tensor(name, shape, dt))
        wqk = sb("a_wqk", [P, DT, 4, P])
        bqk = sb("a_bqk", [P, 4])
        wv = sb("a_wv", [P, DT, D])
        bv = sb("a_bv", [P, D])
        bv_rem = sb("a_bv_rem", [P, D])
        fcw = sb("a_fcw", [P, GROUPS, D])
        fcb = sb("a_fcb", [P, DT])
        rem_mask = sb("a_rem_mask", [P, 1])
        ones_avg = sb("a_ones_avg", [P, P])
        ident_f = sb("a_ident_f", [P, P])
        ident = sb("a_ident", [P, P], BF16)
        onehot_f = sb("a_onehot_f", [40, HEADS, P])
        onehot_rem_f = sb("a_onehot_rem_f", [41, HEADS, Q])
        onehot = sb("a_onehot", [40, HEADS, P], BF16)
        onehot_rem = sb("a_onehot_rem", [41, HEADS, Q], BF16)
        nt_rows = sb("a_nt_rows", [40, 2])
        eps = sb("a_eps", [P, 1])
        waited = sb("a_waited", [1, 1])
        x = [sb(f"a_x{i}", [P, DT, T]) for i in range(2)]
        res = [sb(f"a_res{i}", [P, DT, T]) for i in range(2)]
        xs = sb("a_xs", [P, T])
        xc = sb("a_xc", [P, DT, T])
        sq = sb("a_sq", [P, DT, T])
        sqs = sb("a_sqs", [P, T])
        ln_var = sb("a_ln_var", [P, T])
        rstd = sb("a_rstd", [P, T])
        xn = sb("a_xn", [P, DT, T])
        xn_rem = sb("a_xn_rem", [P, DT, P])
        qk = sb("a_qk", [P, 2, 2, T])
        parts = [sb(f"a_part{i}", [P, 2, 2, T], BF16) for i in range(PARTS)]
        rest = sb("a_rest", [P, 2, 2, T])
        stacks = [sb(f"a_stacks{i}", [SPLIT * HD1, 2 * HEADS * T + Q - REM], BF16) for i in range(2)]
        spill = [nc.dram_tensor(f"a_spill{i}", [PARTS, P, GROUPS * T], BF16).ap() for i in range(2)]
        v_main = [sb(f"a_v{i}", [P, HEADS, Q]) for i in range(2)]
        v_rem = [sb(f"a_vrem{i}", [P, GROUPS, P]) for i in range(2)]
        nmax = sb("a_nmax", [P, HEADS + GROUPS])
        nmax_parts = sb("a_nmax_parts", [P, 2, HEADS + GROUPS], BF16)
        nt = sb("a_nt", [41, HPG, T], BF16)
        prob = [sb(f"a_prob{i}", [P, HPG, T]) for i in range(2)]
        prob_rem = [sb(f"a_probrem{i}", [P, T]) for i in range(2)]
        ou = sb("a_ou", [P, GROUPS, T])
        z = sb("a_z", [P, GROUPS, T])
        lnz = sb("a_lnz", [P, GROUPS, T])
        rz = sb("a_rz", [P, GROUPS, T])
        ot = sb("a_ot", [P, GROUPS, T])
        h1 = [sb(f"a_h1{i}", [P, DT, T]) for i in range(2)]
        ps = ctx.enter_context(nc.psum_tensor("a_psum", [P, 8, 512], F32))
        sem = names(ctx, nc, "a", "weights const xload xs mean xc sq sqs var lnv rstd xn xnr res q qk c1 r1 c2 c3 spill0 spill1 spill2 stack "
                    "v vout vr vrout s max nm1 nm2 nmt nt st exp pv ou z lnz rz ot fc h1 store")
        EV = sem
        heads = range(HPG)

        def stacked(p, which, h, a, b):
            at = ((h % HPG * 2 + which) * GROUPS + h // HPG) * T
            return stacks[p][:, at + a:at + b]

        def s_banks(g):
            return ps[:, 2 * (g % 2):2 * (g % 2) + 2, :]

        def st_banks(g):
            return ps[:, 2 + 2 * (g % 2):4 + 2 * (g % 2), :]

        def two_heads(banks):
            return banks[:, :, 0:2 * T]

        STACKS = 10
        OUT_BANK = (0, 1, 0, 6)

        def load_x(sp, n, q):
            text, patch = n * D, n * IMG_TOK
            need_all(sp, (EV["res"], n - 1), (EV["xload"], 32 * n))
            sp.dma_start(x[q][:, :, IMG_TOK:], dram["txt"][:, bass.ds(text, D)].rearrange("p (t j) -> p t j", t=DT)
                         ).then_inc(EV["xload"], 16)
            sp.dma_start(x[q][:, :, 0:IMG_TOK], embedded[:, :, bass.ds(patch, IMG_TOK)]).then_inc(EV["xload"], 16)

        def stack(sp, n, q):
            row, plane, src = GROUPS * T, P * GROUPS * T, spill[q]

            def write(part, made):
                if part == 0:
                    need_all(sp, (EV[made], 2 * n + 2), (EV["stack"], 16 * STACKS * (n - 1)))
                else:
                    sp.wait_ge(EV[made], 2 * n + 2)
                sp.dma_start(src[part], parts[part][:].rearrange("p a b j -> p (a b j)")).then_inc(EV[f"spill{part}"], 16)

            def read(slot, a, b):
                dst = stacks[q][slot * HD1:(slot + 1) * HD1, 0:2 * HEADS * T].rearrange("d (j w c) -> d j w c", w=2, j=HPG)
                if a == b:
                    sp.dma_start(dst.rearrange("d j w c -> d (j w) c"),
                                 bass.AP(tensor=src.tensor, offset=src.offset + a * plane,
                                         ap=[[row, HD1], [HD1 * row, 2 * HPG], [1, row]])).then_inc(EV["stack"], 16)
                else:
                    for w, part in enumerate((a, b)):
                        sp.dma_start(dst[:, :, w, :],
                                     bass.AP(tensor=src.tensor, offset=src.offset + part * plane + w * HD1 * row,
                                             ap=[[row, HD1], [Q * row, HPG], [1, row]])).then_inc(EV["stack"], 16)

            write(0, "c1")
            write(1, "c2")
            need_all(sp, (EV["spill0"], 16 * (n + 1)), (EV["st"], GROUPS * (n - 1)))
            read(0, 0, 0)
            write(2, "c3")
            sp.wait_ge(EV["spill1"], 16 * (n + 1))
            read(1, 0, 1)
            read(2, 1, 0)
            read(3, 1, 1)
            sp.wait_ge(EV["spill2"], 16 * (n + 1))
            read(4, 0, 2)
            read(5, 2, 0)

        def store_h1(sp, s, p):
            token = s * T
            need_all(sp, (EV["h1"], s + 1), (EV["store"], 16 * (s + 1)))
            sp.dma_start(h1_scratch[:, :, bass.ds(token, T)], h1[p][:]).then_inc(EV["store"], 16)

        def mean(pe, n):
            pe.wait_ge(EV["xs"], n + 1)
            need(pe, EV["nt"], n - 1)
            pe.matmul(ps[:, 7, 0:T], ones_avg[:], xs[:], start=True, stop=True).then_inc(EV["mean"], 1)

        def var(pe, n):
            pe.wait_ge(EV["sqs"], n + 1)
            pe.wait_ge(EV["xc"], n + 1)
            pe.matmul(ps[:, 7, 0:T], ones_avg[:], sqs[:], start=True, stop=True).then_inc(EV["var"], 1)

        def project_qk(pe, n, which):
            if which == 0:
                pe.wait_ge(EV["xn"], n + 1)
                need(pe, EV["exp"], GROUPS * (n - 1))
            for t in range(DT):
                for k in range(DT):
                    mm = pe.matmul(ps[:, 4 + which, t * T:(t + 1) * T], wqk[:, k, 2 * which + t, :], xn[:, k, :],
                                   start=(k == 0), stop=(k == DT - 1))
            mm.then_inc(EV["q"], 1)

        def project_v(pe, n):
            pe.wait_ge(EV["qk"], 2 * n + 1)
            for k in range(DT):
                mm = pe.matmul(ps[:, 4, 0:D], xn[:, k, 0:P], wv[:, k, :], start=(k == 0), stop=(k == DT - 1))
            mm.then_inc(EV["v"], 1)

        def project_v_rem(pe, n):
            pe.wait_ge(EV["qk"], 2 * n + 2)
            pe.wait_ge(EV["xnr"], n + 1)
            for k in range(DT):
                mm = pe.matmul(ps[:, 5, 0:D], xn_rem[:, k, :], wv[:, k, :],
                               start=(k == 0), stop=(k == DT - 1))
            mm.then_inc(EV["vr"], 1)

        def scores(pe, s, p, g):
            if g == 0:
                pe.wait_ge(EV["stack"], 16 * STACKS * (s + 1))
                need(pe, EV["ou"], GROUPS * s - 1)
            elif g == 1:
                need(pe, EV["exp"], GROUPS * (s - 1) + 3)
            else:
                need(pe, EV["max"], GROUPS * s + g - 1)
            b = s_banks(g)
            for j in heads:
                h = HPG * g + j
                pe.matmul(b[:, j // 2, (j % 2) * T:(j % 2 + 1) * T], stacked(p, 0, h, 0, P), stacked(p, 1, h, 0, T),
                          start=True, stop=True)
            for j in heads:
                h = HPG * g + j
                mm = pe.matmul(b[Q * j:Q * j + Q, 0, 2 * T:3 * T], stacked(p, 0, h, P, PAD_T), stacked(p, 1, h, 0, T),
                               start=True, stop=True)
            mm.then_inc(EV["s"], 1)

        def turn_max(pe, s, n_var):
            pe.wait_ge(EV["nm2"], s + 1)
            need(pe, EV["lnv"], n_var)
            pe.matmul(ps[0:40, 7, 0:P], nmax_parts[:].rearrange("p a c -> p (a c)"), ident[:],
                      start=True, stop=True).then_inc(EV["nmt"], 1)

        def scores_t(pe, s, p, g, v_read=None):
            if g == 0:
                pe.wait_ge(EV["nt"], s + 1)
                pe.wait_ge(EV["max"], GROUPS * s + 4)
            else:
                need(pe, EV["exp"], GROUPS * s + g - 1)
            if g == 1:
                pe.wait_ge(EV["vout"], v_read)
                pe.wait_ge(EV["vrout"], v_read)
            b = st_banks(g)
            for j in heads:
                h = HPG * g + j
                o = b[:, j // 2, (j % 2) * T:(j % 2 + 1) * T]
                pe.matmul(o, stacked(p, 1, h, 0, P), stacked(p, 0, h, 0, T), start=True, stop=False)
                pe.matmul(o, onehot[:, h, :], nt[0:40, j, :], start=False, stop=True)
            for j in heads:
                h = HPG * g + j
                o = b[Q * j:Q * j + Q, 0, 2 * T:3 * T]
                pe.matmul(o, stacked(p, 1, h, P, PAD_T), stacked(p, 0, h, 0, T), start=True, stop=False)
                mm = pe.matmul(o, onehot_rem[:, h, :], nt[:, j, :], start=False, stop=True)
            mm.then_inc(EV["st"], 1)

        def weigh(pe, s, p, g):
            pe.wait_ge(EV["exp"], GROUPS * s + g + 1)
            if g == 0:
                pe.wait_ge(EV["max"], GROUPS * s + 3)
            elif g == 2:
                pe.wait_ge(EV["ou"], GROUPS * s + 1)
            elif g == 3:
                need(pe, EV["h1"], s)
            b = ps[:, OUT_BANK[g], 0:T]
            pe.matmul(b, v_rem[p][:, g, :], prob_rem[g % 2][:], start=True, stop=False)
            for j in heads:
                mm = pe.matmul(b[Q * j:Q * j + Q], v_main[p][:, HPG * g + j, :], prob[g % 2][:, j, :],
                               start=False, stop=True)
            mm.then_inc(EV["pv"], 1)

        def fc(pe, s):
            pe.wait_ge(EV["ot"], s + 1)
            for t in range(DT):
                for g in range(GROUPS):
                    mm = pe.matmul(ps[:, 6, t * T:(t + 1) * T], fcw[:, g, t * P:(t + 1) * P], ot[:, g, :],
                                   start=(g == 0), stop=(g == GROUPS - 1))
            mm.then_inc(EV["fc"], 1)

        def centre(dve, n, q):
            dve.wait_ge(EV["mean"], n + 1)
            dve.tensor_tensor(xc[:], x[q][:], spread(ps[:, 7, 0:T], 1, DT), ALU.subtract).then_inc(EV["xc"], 1)

        def normalise(dve, n):
            dve.wait_ge(EV["rstd"], n + 1)
            need(dve, EV["vr"], n)
            need(dve, EV["res"], n)
            dve.tensor_tensor(xn[:], xc[:], spread(rstd[:], 1, DT), ALU.mult).then_inc(EV["xn"], 1)

        def qk_out(dve, n, which):
            dve.wait_ge(EV["q"], 2 * n + which + 1)
            need(dve, EV["r1"], 2 * (n - 1) + which + 1)
            dve.tensor_tensor(qk[:, which], ps[:, 4 + which, 0:2 * T].rearrange("p (t j) -> p t j", t=DT),
                              spread(bqk[:, 2 * which:2 * which + 2], 2, T), ALU.add).then_inc(EV["qk"], 1)

        def v_out(dve, n, q):
            dve.wait_ge(EV["v"], n + 1)
            dve.tensor_tensor(v_main[q][:, :, 0:HD1], ps[:, 4, 0:D].rearrange("p (h d) -> p h d", d=HD1),
                              bv[:].rearrange("p (h d) -> p h d", d=HD1), ALU.add).then_inc(EV["vout"], 1)

        def v_rem_out(dve, n, q):
            dve.wait_ge(EV["vr"], n + 1)
            for j in heads:
                r = slice(Q * j, Q * j + Q)
                last = dve.scalar_tensor_tensor(
                    out=v_rem[q][r, :, Q * j:Q * j + HD1],
                    in0=ps[r, 5, 0:D].rearrange("p (g j d) -> p g j d", g=GROUPS, j=HPG)[:, :, j, :],
                    scalar=rem_mask[r, :],
                    in1=bv_rem[r, :].rearrange("p (g j d) -> p g j d", g=GROUPS, j=HPG)[:, :, j, :],
                    op0=ALU.mult, op1=ALU.add)
            last.then_inc(EV["vrout"], 1)

        def maxima(dve, s, g):
            dve.wait_ge(EV["s"], GROUPS * s + g + 1)
            b = s_banks(g)
            dve.tensor_reduce(nmax[:, HPG * g:HPG * g + HPG].rearrange("p (b j) -> p b j", b=2),
                              two_heads(b).rearrange("p b (j k) -> p b j k", j=2), AX.X, ALU.max, negate=True)
            dve.tensor_reduce(nmax[:, HEADS + g:HEADS + g + 1], b[:, 0, 2 * T:3 * T], AX.X, ALU.max,
                              negate=True).then_inc(EV["max"], 1)

        def split_max(dve, s):
            dve.wait_ge(EV["max"], GROUPS * (s + 1))
            dve.tensor_copy(nmax_parts[:, 0, :], nmax[:]).then_inc(EV["nm1"], 1)
            dve.wait_ge(EV["nm1"], s + 1)
            dve.tensor_tensor(nmax_parts[:, 1, :], nmax[:], nmax_parts[:, 0, :], ALU.subtract).then_inc(EV["nm2"], 1)

        def weighed_out(dve, s, g):
            if g > 0:
                dve.wait_ge(EV["ou"], GROUPS * s + g)
            dve.wait_ge(EV["pv"], GROUPS * s + g + 1)
            dve.tensor_copy(ou[:, g, :], ps[:, OUT_BANK[g], 0:T]).then_inc(EV["ou"], 1)

        def sums(dve, s, g):
            if g == GROUPS - 1:
                dve.wait_ge(EV["ou"], GROUPS * (s + 1))
                dve.memset(waited[:], 0.0)
            dve.stream_shuffle(z[:, g, :], ou[:, g, :], [HD1 + i % HD1 for i in range(Q)]).then_inc(EV["z"], 1)

        def residual(dve, s, p):
            dve.wait_ge(EV["fc"], s + 1)
            need(dve, EV["store"], 16 * (s + 1))
            dve.wait_ge(EV["res"], s + 1)
            for t in range(DT):
                last = dve.scalar_tensor_tensor(out=h1[p][:, t, :], in0=ps[:, 6, t * T:(t + 1) * T],
                                                scalar=fcb[:, t:t + 1], in1=res[p][:, t, :], op0=ALU.add, op1=ALU.add)
            last.then_inc(EV["h1"], 1)

        def square(act, n):
            act.wait_ge(EV["xc"], n + 1)
            act.activation(sq[:], xc[:], ACT.Square).then_inc(EV["sq"], 1)

        def inv_std(act, n):
            act.wait_ge(EV["var"], n + 1)
            act.activation(ln_var[:], ps[:, 7, 0:T], ACT.Ln, bias=eps[:]).then_inc(EV["lnv"], 1)
            act.wait_ge(EV["lnv"], n + 1)
            act.activation(rstd[:], ln_var[:], ACT.Exp, scale=-0.5).then_inc(EV["rstd"], 1)

        def repeat_last(act, n):
            act.wait_ge(EV["xn"], n + 1)
            act.activation(xn_rem[:].rearrange("p t (r j) -> p t r j", j=REM), spread(xn[:, :, P:T], 2, P // REM),
                           ACT.Copy).then_inc(EV["xnr"], 1)

        def first_part(act, n, which):
            act.wait_ge(EV["qk"], 2 * n + which + 1)
            need(act, EV["stack"], 16 * STACKS * n)
            act.activation(parts[0][:, which], qk[:, which], ACT.Copy).then_inc(EV["c1"], 1)

        def second_part(act, n, which):
            act.wait_ge(EV["r1"], 2 * n + which + 1)
            act.activation(parts[1][:, which], rest[:, which], ACT.Copy).then_inc(EV["c2"], 1)

        def max_rows(act, s):
            act.wait_ge(EV["nmt"], s + 1)
            act.activation(nt[0:40, :, 0:P], spread(ps[0:40, 7, 0:P], 1, HPG), ACT.Copy, scale=nt_rows[:, 0:1])
            act.activation(nt[0:40, :, P:T], ps[0:40, 7, 0:P].rearrange("p (j q) -> p j q", q=Q)[:, :, 0:REM],
                           ACT.Copy, scale=nt_rows[:, 1:2]).then_inc(EV["nt"], 1)

        def exps(act, s, g):
            act.wait_ge(EV["st"], GROUPS * s + g + 1)
            need(act, EV["pv"], GROUPS * s + g - 1)
            b = st_banks(g)
            act.activation(prob[g % 2][:].rearrange("p (b j) q -> p b (j q)", b=2), two_heads(b), ACT.Exp, scale=HD1 ** -0.5)
            act.activation(prob_rem[g % 2][:], b[:, 0, 2 * T:3 * T], ACT.Exp, scale=HD1 ** -0.5).then_inc(EV["exp"], 1)

        def inv_sums(act, s):
            act.wait_ge(EV["z"], GROUPS * (s + 1))
            act.activation(lnz[:], z[:], ACT.Ln).then_inc(EV["lnz"], 1)
            act.wait_ge(EV["lnz"], s + 1)
            act.activation(rz[:], lnz[:], ACT.Exp, scale=-1.0).then_inc(EV["rz"], 1)

        def add_tiles(pool, n, q):
            pool.wait_ge(EV["xload"], 32 * (n + 1))
            need(pool, EV["mean"], n)
            pool.tensor_tensor(xs[:], x[q][:, 0, :], x[q][:, 1, :], ALU.add).then_inc(EV["xs"], 1)

        def add_squares(pool, n):
            pool.wait_ge(EV["sq"], n + 1)
            pool.tensor_tensor(sqs[:], sq[:, 0, :], sq[:, 1, :], ALU.add).then_inc(EV["sqs"], 1)

        def add_norm(pool, n, q):
            pool.wait_ge(EV["xn"], n + 1)
            need(pool, EV["h1"], n - 1)
            pool.tensor_tensor(res[q][:], x[q][:], xn[:], ALU.add).then_inc(EV["res"], 1)

        def rest_one(pool, n, which):
            pool.wait_ge(EV["c1"], 2 * n + which + 1)
            pool.tensor_tensor(rest[:, which], qk[:, which], parts[0][:, which], ALU.subtract).then_inc(EV["r1"], 1)

        def third_part(pool, n, which):
            pool.wait_ge(EV["c2"], 2 * n + which + 1)
            pool.tensor_tensor(parts[2][:, which], rest[:, which], parts[1][:, which], ALU.subtract).then_inc(EV["c3"], 1)

        def divide(pool, s):
            pool.wait_ge(EV["rz"], s + 1)
            if isinstance(s, int):
                need(pool, EV["fc"], s)
            pool.tensor_tensor(ot[:], ou[:], rz[:], ALU.mult).then_inc(EV["ot"], 1)

        def each_step(engine, step):
            step(0, 0, True, True, True)
            if seqs > 4:
                with engine.Fori(0, (seqs - 4) // 2) as i:
                    step(i * 2 + 1, 1, False, True, True)
                    step(i * 2 + 2, 0, False, True, True)
            step(seqs - 3, 1, False, True, True)
            step(seqs - 2, 0, False, True, False)
            step(seqs - 1, 1, False, False, False)

        with nc.Block() as block:

            @block.sync
            def _(sp):
                for dst, name in ((wqk, "wqk"), (bqk, "bqk"), (wv, "wv"), (bv, "bv"), (fcw, "fcw"), (fcb, "fcb"),
                                  (rem_mask, "rem_mask"), (onehot_f, "onehot1"), (onehot_rem_f, "onehot1_rem"), (nt_rows, "nt_rows"), (ident_f, "ident")):
                    sp.dma_start(dst[:], dram[name]).then_inc(sem["weights"], 16)
                load_x(sp, 0, 0)
                load_x(sp, 1, 1)
                stack(sp, 0, 0)

                def step(s, p, first, has_next, has_norm):
                    if has_norm:
                        load_x(sp, s + 2, p)
                    if has_next:
                        stack(sp, s + 1, 1 - p)
                    if not first:
                        store_h1(sp, s - 1, 1 - p)
                each_step(sp, step)
                store_h1(sp, seqs - 1, 1)
                sp.wait_ge(EV["store"], 16 * (seqs + 1))

            @block.tensor
            def _(pe):
                pe.wait_ge(sem["weights"], 176)
                pe.wait_ge(sem["const"], 9)
                mean(pe, 0)
                var(pe, 0)
                project_qk(pe, 0, 0)
                project_qk(pe, 0, 1)
                project_v(pe, 0)
                project_v_rem(pe, 0)
                mean(pe, 1)
                var(pe, 1)

                def step(s, p, first, has_next, has_norm):
                    n, m = s + 1, s + 2
                    if has_next:
                        project_qk(pe, n, 0)
                        project_qk(pe, n, 1)
                    scores(pe, s, p, 0)
                    scores(pe, s, p, 1)
                    scores(pe, s, p, 2)
                    scores(pe, s, p, 3)
                    if has_next:
                        project_v(pe, n)
                        project_v_rem(pe, n)
                    turn_max(pe, s, m if has_next else n)
                    if not first:
                        fc(pe, s - 1)
                    scores_t(pe, s, p, 0)
                    if has_norm:
                        mean(pe, m)
                    scores_t(pe, s, p, 1, m if has_next else n)
                    weigh(pe, s, p, 0)
                    scores_t(pe, s, p, 2)
                    if has_norm:
                        var(pe, m)
                    weigh(pe, s, p, 1)
                    scores_t(pe, s, p, 3)
                    weigh(pe, s, p, 2)
                    weigh(pe, s, p, 3)
                each_step(pe, step)
                fc(pe, seqs - 1)

            @block.vector
            def _(dve):
                dve.memset(ones_avg[:], 1.0 / D).then_inc(sem["const"], 1)
                for i in range(2):
                    dve.memset(v_main[i][:, :, HD1:], 1.0).then_inc(sem["const"], 1)
                dve.memset(eps[:], EPS).then_inc(sem["const"], 1)
                dve.memset(waited[:], 0.0).then_inc(sem["store"], 16)
                for i in range(2):
                    dve.memset(stacks[i][:, 2 * HEADS * T:], 0.0)
                dve.memset(nt[Q:], 1.0)
                dve.memset(nt[0:Q], 0.0).then_inc(sem["const"], 1)
                dve.wait_ge(sem["weights"], 176)
                dve.tensor_copy(ident[:], ident_f[:]).then_inc(sem["const"], 1)
                dve.tensor_copy(onehot[:], onehot_f[:]).then_inc(sem["const"], 1)
                dve.tensor_scalar(bv_rem[:], bv[:], rem_mask[:, 0:1], None, ALU.mult).then_inc(sem["const"], 1)
                dve.wait_ge(sem["const"], 8)
                dve.tensor_copy(onehot_rem[:], onehot_rem_f[:]).then_inc(sem["const"], 1)
                centre(dve, 0, 0)
                normalise(dve, 0)
                qk_out(dve, 0, 0)
                qk_out(dve, 0, 1)
                v_out(dve, 0, 0)
                for i in range(2):
                    dve.memset(v_rem[i][:], 0.0).then_inc(sem["const"], 1)
                dve.wait_ge(sem["const"], 11)
                for i in range(2):
                    for j in heads:
                        r = slice(Q * j, Q * j + Q)
                        last = dve.tensor_copy(v_rem[i][r, :, Q * j + HD1:Q * j + Q],
                                               spread(spread(rem_mask[r, 0], 1, GROUPS), 2, HD1))
                last.then_inc(sem["const"], 1)
                v_rem_out(dve, 0, 0)
                centre(dve, 1, 1)
                normalise(dve, 1)

                def step(s, p, first, has_next, has_norm):
                    n, m = s + 1, s + 2
                    if not first:
                        sums(dve, s - 1, GROUPS - 1)
                    if has_next:
                        qk_out(dve, n, 0)
                        qk_out(dve, n, 1)
                    maxima(dve, s, 0)
                    maxima(dve, s, 1)
                    maxima(dve, s, 2)
                    maxima(dve, s, 3)
                    split_max(dve, s)
                    if has_next:
                        v_out(dve, n, 1 - p)
                        v_rem_out(dve, n, 1 - p)
                    if not first:
                        residual(dve, s - 1, 1 - p)
                    if has_norm:
                        centre(dve, m, p)
                    weighed_out(dve, s, 0)
                    for g in range(1, GROUPS):
                        if g == 2 and has_norm:
                            normalise(dve, m)
                        weighed_out(dve, s, g)
                        sums(dve, s, g - 1)
                each_step(dve, step)
                sums(dve, seqs - 1, GROUPS - 1)
                residual(dve, seqs - 1, 1)

            @block.scalar
            def _(act):
                act.preload_act_table_set("natural_log_exp_and_others")
                act.wait_ge(sem["const"], 9)
                square(act, 0)
                inv_std(act, 0)
                repeat_last(act, 0)
                for which in range(2):
                    first_part(act, 0, which)
                    second_part(act, 0, which)
                square(act, 1)
                inv_std(act, 1)
                repeat_last(act, 1)

                def step(s, p, first, has_next, has_norm):
                    n, m = s + 1, s + 2
                    if not first:
                        inv_sums(act, s - 1)
                    if has_next:
                        first_part(act, n, 0)
                        first_part(act, n, 1)
                        second_part(act, n, 0)
                        second_part(act, n, 1)
                    max_rows(act, s)
                    exps(act, s, 0)
                    if has_norm:
                        square(act, m)
                    exps(act, s, 1)
                    exps(act, s, 2)
                    if has_norm:
                        inv_std(act, m)
                    exps(act, s, 3)
                    if has_norm:
                        repeat_last(act, m)
                each_step(act, step)
                inv_sums(act, seqs - 1)

            @block.gpsimd
            def _(pool):
                add_tiles(pool, 0, 0)
                add_squares(pool, 0)
                add_norm(pool, 0, 0)
                for which in range(2):
                    rest_one(pool, 0, which)
                for which in range(2):
                    third_part(pool, 0, which)
                add_tiles(pool, 1, 1)
                add_squares(pool, 1)

                def step(s, p, first, has_next, has_norm):
                    n, m = s + 1, s + 2
                    if not first:
                        divide(pool, s - 1)
                    if has_norm:
                        add_tiles(pool, m, p)
                    if has_next:
                        rest_one(pool, n, 0)
                        rest_one(pool, n, 1)
                        third_part(pool, n, 0)
                        third_part(pool, n, 1)
                        add_norm(pool, n, 1 - p)
                    if has_norm:
                        add_squares(pool, m)
                each_step(pool, step)
                divide(pool, seqs - 1)


def attn2_phase(nc, dram, h1_scratch, x2_scratch, seqs):
    with ExitStack() as ctx:
        sb = lambda name, shape, dt=F32: ctx.enter_context(nc.sbuf_tensor(name, shape, dt))
        RT = HPG + 1
        wqn_t = sb("b_wqn_t", [P, GROUPS, D])
        wkb_t = sb("b_wkb_t", [P, GROUPS, LAT])
        wo_n = sb("b_wo_n", [P, GROUPS, D])
        wq_nope = sb("b_wq_nope", [P, DT, GROUPS, P])
        wo = sb("b_wo", [P, GROUPS, D])
        wq_rope = sb("b_wq_rope", [P, DT, GROUPS, P])
        wkva = sb("b_wkva", [P, DT, P])
        w_ln = sb("b_w_ln", [P, DT])
        rope_cos = sb("b_rope_cos", [P, RT, T])
        rope_sin = sb("b_rope_sin", [P, RT, T])
        ones_avg = sb("b_ones_avg", [P, P])
        ones = sb("b_ones", [P, Q])
        eps = sb("b_eps", [P, 1])
        waited = sb("b_waited", [1, 1])
        masks_f = sb("b_masks_f", [P, 2 * P + T + REM])
        masks = sb("b_masks", [P, 2 * P + T + REM], BF16)
        mask_main, mask_main_t = masks[:, 0:P], masks[:, P:2 * P]
        mask_rem, mask_rem_t = masks[:, 2 * P:2 * P + T], masks[0:REM, 2 * P + T:]
        ident_f = sb("b_ident_f", [P, P])
        ident = sb("b_ident", [P, P], BF16)
        onehot_f = sb("b_onehot_f", [40, HEADS + GROUPS, P])
        onehot = sb("b_onehot", [40, HEADS + GROUPS, P], BF16)
        x = [sb(f"b_x{i}", [P, DT, T]) for i in range(2)]
        xs = sb("b_xs", [P, T])
        xc = sb("b_xc", [P, DT, T])
        sq = sb("b_sq", [P, DT, T])
        sqs = sb("b_sqs", [P, T])
        ln_var = sb("b_ln_var", [P, T])
        rstd = sb("b_rstd", [P, T])
        norm_a = sb("b_norm_a", [P, T])
        norm_b = sb("b_norm_b", [P, T])
        ln_rms = sb("b_ln_rms", [P, T])
        inv_rms = sb("b_inv_rms", [P, T])
        both = sb("b_both", [P, T])
        x1 = [sb(f"b_x1{i}", [P, DT, T]) for i in range(2)]
        xr = sb("b_xr", [P, DT, T])
        nope_b = sb("b_nope_b", [P, GROUPS, T], BF16)
        nope = [sb(f"b_nope{i}", [P, GROUPS, T], F32R) for i in range(2)]
        raw = sb("b_raw", [P, RT, T])
        swapped = sb("b_swapped", [P, RT, T])
        with_cos = sb("b_with_cos", [P, RT, T])
        with_sin = sb("b_with_sin", [P, RT, T])
        roped = [sb(f"b_roped{i}", [P, RT, T]) for i in range(2)]
        roped_b = [sb(f"b_roped_b{i}", [P, RT, T], BF16) for i in range(2)]
        keys_b = [sb(f"b_keys_b{i}", [P, T], BF16) for i in range(2)]
        roped_hi = [sb(f"b_roped_hi{i}", [P, RT, T], F32R) for i in range(2)]
        roped_lo = [sb(f"b_roped_lo{i}", [P, RT, T], F32R) for i in range(2)]
        stacks = [sb(f"b_stacks{i}", [P, HEADS * T + Q - REM], F32R) for i in range(2)]
        stack_b = sb("b_stack_b", [P, GROUPS, HPG * T + Q - REM], BF16)
        v_main = [sb(f"b_v{i}", [P, LAT]) for i in range(2)]
        v_rem = [sb(f"b_vrem{i}", [REM, LAT]) for i in range(2)]
        nmax = sb("b_nmax", [P, HEADS + GROUPS])
        nmax_parts = sb("b_nmax_parts", [P, 2, HEADS + GROUPS], BF16)
        nt = sb("b_nt", [40, P], BF16)
        prob = [sb(f"b_prob{i}", [P, HPG, P]) for i in range(2)]
        prob_q = sb("b_prob_q", [P, GROUPS, HPG, REM])
        prob_qq = sb("b_prob_qq", [REM, GROUPS, HPG, REM])
        ouz = sb("b_ouz", [P, 2, GROUPS, T])
        lnz = sb("b_lnz", [P, GROUPS, T])
        rz = sb("b_rz", [P, GROUPS, T])
        ot = sb("b_ot", [P, GROUPS, T])
        x2 = [sb(f"b_x2{i}", [P, DT, T]) for i in range(2)]
        ps = ctx.enter_context(nc.psum_tensor("b_psum", [P, 8, 512], F32))
        sem = names(ctx, nc, "b", "weights const absorb absorbed xload xs mean xc sq sqs var lnv rstd na nb lnr ir both x1 xr "
                    "qn qr qnh qnl raw cos swap sin rope rope_b rhi rlo kb stack cast nope_b v vout "
                    "s max nm1 nm2 nmt nt st exp expr_in expr pv pvr ou oz lnz rz ot wo x2 store")
        EV = sem
        members = range(HPG)

        def place_b(G, m, a, b):
            return stack_b[:, G, m * T + a:m * T + b]

        def places(p):
            return stacks[p][:, 0:HEADS * T].rearrange("p (h j) -> p h j", j=T)

        def load_x(sp, n, q):
            token = n * T
            need_all(sp, (EV["xc"], n - 1), (EV["xload"], 16 * n))
            sp.dma_start(x[q][:], h1_scratch[:, :, bass.ds(token, T)]).then_inc(EV["xload"], 16)

        def stack(sp, n, q):
            for slot, (made, src) in enumerate((("qnh", nope[0]), ("rhi", roped_hi[q]), ("qnl", nope[1]), ("rlo", roped_lo[q]))):
                if slot == 0:
                    need_all(sp, (EV["expr_in"], n - 1), (EV["st"], GROUPS * (n - 1)), (EV[made], n + 1))
                else:
                    sp.wait_ge(EV[made], n + 1)
                for j in range(HPG):
                    sp.dma_start(stacks[q][Q * slot:Q * slot + Q, j * GROUPS * T:(j + 1) * GROUPS * T].bitcast(F32),
                                 src[Q * j:Q * j + Q, 0:GROUPS, :].rearrange("p g j -> p (g j)").bitcast(F32)).then_inc(EV["stack"], 16)

        def store_x2(sp, s, p):
            token = s * T
            need_all(sp, (EV["x2"], s + 1), (EV["store"], 16 * (s + 1)))
            sp.dma_start(x2_scratch[:, :, bass.ds(token, T)], x2[p][:]).then_inc(EV["store"], 16)

        def mean(pe, n):
            pe.wait_ge(EV["xs"], n + 1)
            need(pe, EV["nt"], n - 1)
            pe.matmul(ps[:, 6, 0:T], ones_avg[:], xs[:], start=True, stop=True).then_inc(EV["mean"], 1)

        def var(pe, n):
            pe.wait_ge(EV["sqs"], n + 1)
            pe.wait_ge(EV["xc"], n + 1)
            pe.matmul(ps[:, 6, 0:T], ones_avg[:], sqs[:], start=True, stop=True).then_inc(EV["var"], 1)

        def project_nope(pe, n):
            pe.wait_ge(EV["raw"], n + 1)
            for g in range(GROUPS):
                for k in range(DT):
                    mm = pe.matmul(ps[:, 4 + g // 2, (g % 2) * T:(g % 2 + 1) * T], wq_nope[:, k, g, :], xr[:, k, :],
                                   start=(k == 0), stop=(k == DT - 1))
            mm.then_inc(EV["qn"], 1)

        def project_rope(pe, n):
            pe.wait_ge(EV["xr"], n + 1)
            need(pe, EV["exp"], GROUPS * (n - 1))
            for g in range(RT):
                for k in range(DT):
                    w = wq_rope[:, k, g, :] if g < GROUPS else wkva[:, k, :]
                    mm = pe.matmul(ps[:, 4 + g // 3, (g % 3) * T:(g % 3 + 1) * T], w, xr[:, k, :],
                                   start=(k == 0), stop=(k == DT - 1))
            mm.then_inc(EV["qr"], 1)

        def project_v(pe, n):
            pe.wait_ge(EV["qnl"], n + 1)
            for k in range(DT):
                pe.matmul(ps[:, 4, 0:LAT], xr[:, k, 0:P], wkva[:, k, 0:LAT], start=(k == 0), stop=(k == DT - 1))
            for k in range(DT):
                mm = pe.matmul(ps[0:REM, 4, LAT:2 * LAT], xr[:, k, P:T], wkva[:, k, 0:LAT], start=(k == 0), stop=(k == DT - 1))
            mm.then_inc(EV["v"], 1)

        def scores(pe, s, p, G):
            pe.wait_ge(EV["cast"], GROUPS * s + G + 1)
            if G == 0:
                pe.wait_ge(EV["kb"], s + 1)
                need(pe, EV["ou"], GROUPS * s - 1)
            elif G == 1:
                need(pe, EV["ou"], GROUPS * s)
            else:
                need(pe, EV["max"], GROUPS * s + G - 1)
            b, br = ps[:, G % 2, :], ps[:, 2 + G % 2, 0:T]
            keys = roped_b[p][:, GROUPS, :], keys_b[p][:]
            pe.matmul(b, ident[:], spread(mask_main, 1, HPG), start=True, stop=False)
            for m in members:
                for i in range(2):
                    pe.matmul(b[:, m * P:(m + 1) * P], place_b(G, m, 0, P), keys[i][:, 0:P], start=False,
                              stop=(m == HPG - 1 and i == 1))
            pe.matmul(br, ident[:], mask_rem, start=True, stop=False)
            for m in members:
                for i in range(2):
                    mm = pe.matmul(br[Q * m:Q * m + Q], place_b(G, m, P, PAD_T), keys[i], start=False, stop=(i == 1))
            mm.then_inc(EV["s"], 1)

        def turn_max(pe, s, n_var):
            pe.wait_ge(EV["nm2"], s + 1)
            need(pe, EV["nb"], n_var)
            pe.matmul(ps[0:40, 6, 0:P], nmax_parts[:].rearrange("p a c -> p (a c)"), ident[:],
                      start=True, stop=True).then_inc(EV["nmt"], 1)

        def scores_t(pe, s, p, G, v_read=None):
            if G == 0:
                pe.wait_ge(EV["vout"], v_read)
            need(pe, EV["exp"], GROUPS * s + G - 1)
            b = ps[:, 4 + G % 2, :]
            q = places(p)[:, HPG * G:HPG * G + HPG, 0:P]
            pe.matmul(b, ident[:], spread(mask_main_t, 1, HPG), start=True, stop=False)
            pe.matmul(b, roped_hi[p][:, GROUPS, 0:P], q, start=False, stop=False)
            pe.matmul(b, roped_lo[p][:, GROUPS, 0:P], q, start=False, stop=False)
            if G == 0:
                pe.wait_ge(EV["nt"], s + 1)
            for m in members:
                mm = pe.matmul(b[:, m * P:(m + 1) * P], onehot[:, HPG * G + m, :], nt[:], start=False, stop=(m == HPG - 1))
            mm.then_inc(EV["st"], 1)

        def scores_t_rem(pe, s, p, n_var):
            pe.wait_ge(EV["nt"], s + 1)
            pe.wait_ge(EV["nb"], n_var)
            b, bb = ps[:, 6, 0:2 * P], ps[0:REM, 6, 2 * P:4 * P]
            q = places(p)[:, :, P:T]
            rem_max = nt[:].rearrange("r (m q) -> r m q", q=Q)[:, :, 0:REM]
            w = HPG * REM
            pe.matmul(b, roped_hi[p][:, GROUPS, 0:P], q, start=True, stop=False)
            pe.matmul(b, roped_lo[p][:, GROUPS, 0:P], q, start=False, stop=False)
            for G in range(GROUPS):
                pe.matmul(b[:, G * w:(G + 1) * w], onehot[:, HEADS + G, :], rem_max, start=False, stop=(G == GROUPS - 1))
            pe.matmul(bb, roped[p][:, GROUPS, P:T], q.bitcast(F32), start=True, stop=False)
            pe.matmul(bb, ident[0:REM, 0:REM], spread(mask_rem_t, 1, HEADS), start=False, stop=False)
            for G in range(GROUPS):
                mm = pe.matmul(bb[:, G * w:(G + 1) * w], onehot[:, HEADS + G, 0:REM], rem_max, start=False, stop=(G == GROUPS - 1))
            mm.then_inc(EV["expr_in"], 1)

        def weigh(pe, s, p, G):
            pe.wait_ge(EV["exp"], GROUPS * s + G + 1)
            for m in members:
                pe.matmul(ps[Q * m:Q * m + Q, G, 0:P], v_main[p][:], prob[G % 2][:, m, :], start=True, stop=True)
            for m in members:
                mm = pe.matmul(ps[Q * m:Q * m + Q, G, P:2 * P], ones[:], prob[G % 2][:, m, :], start=True, stop=True)
            mm.then_inc(EV["pv"], 1)

        def weigh_rem(pe, s, p):
            pe.wait_ge(EV["expr"], s + 1)
            need(pe, EV["x2"], s)
            for m in members:
                for i, (v, vr) in enumerate(((v_main[p][:], v_rem[p][:]), (ones[:], ones[0:REM, :]))):
                    o = ps[Q * m:Q * m + Q, 7, i * HPG * REM:(i + 1) * HPG * REM]
                    pe.matmul(o, v, prob_q[:, :, m, :], start=True, stop=False)
                    mm = pe.matmul(o, vr, prob_qq[:, :, m, :], start=False, stop=True)
            mm.then_inc(EV["pvr"], 1)

        def project_out(pe, s):
            pe.wait_ge(EV["ot"], s + 1)
            pe.wait_ge(EV["oz"], s + 1)
            for t in range(DT):
                for G in range(GROUPS):
                    mm = pe.matmul(ps[:, 7, t * T:(t + 1) * T], wo[:, G, t * P:(t + 1) * P], ot[:, G, :],
                                   start=(G == 0), stop=(G == GROUPS - 1))
            mm.then_inc(EV["wo"], 1)

        def centre(dve, n, q):
            dve.wait_ge(EV["mean"], n + 1)
            need(dve, EV["x1"], n)
            dve.tensor_tensor(xc[:], x[q][:], spread(ps[:, 6, 0:T], 1, DT), ALU.subtract).then_inc(EV["xc"], 1)

        def rms_terms(dve, n):
            dve.wait_ge(EV["rstd"], n + 1)
            dve.tensor_tensor(norm_a[:], rstd[:], ps[:, 6, 0:T], ALU.mult).then_inc(EV["na"], 1)
            dve.wait_ge(EV["na"], n + 1)
            dve.tensor_tensor(norm_b[:], norm_a[:], rstd[:], ALU.mult).then_inc(EV["nb"], 1)

        def rms_norm(dve, n):
            dve.wait_ge(EV["ir"], n + 1)
            dve.tensor_tensor(both[:], rstd[:], inv_rms[:], ALU.mult).then_inc(EV["both"], 1)
            dve.wait_ge(EV["both"], n + 1)
            need(dve, EV["v"], n)
            for t in range(DT):
                last = dve.scalar_tensor_tensor(out=xr[:, t, :], in0=xc[:, t, :], scalar=w_ln[:, t:t + 1], in1=both[:],
                                                op0=ALU.mult, op1=ALU.mult)
            last.then_inc(EV["xr"], 1)

        def nope_low(dve, n):
            dve.wait_ge(EV["nope_b"], n + 1)
            for c in range(2):
                last = dve.tensor_tensor(nope[1][:, 2 * c:2 * c + 2, :], ps[:, 4 + c, 0:2 * T].rearrange("p (g j) -> p g j", g=2),
                                         nope_b[:, 2 * c:2 * c + 2, :], ALU.subtract)
            last.then_inc(EV["qnl"], 1)

        def turn(dve, n):
            dve.wait_ge(EV["raw"], n + 1)
            dve.memset(waited[:], 0.0)
            dve.stream_shuffle(swapped[:].rearrange("p a b -> p (a b)"), raw[:].rearrange("p a b -> p (a b)"),
                               [i ^ 1 for i in range(Q)]).then_inc(EV["swap"], 1)
            dve.wait_ge(EV["swap"], n + 1)
            dve.tensor_tensor(with_sin[:], swapped[:], rope_sin[:], ALU.mult).then_inc(EV["sin"], 1)

        def rotate(dve, n, q):
            dve.wait_ge(EV["sin"], n + 1)
            dve.wait_ge(EV["cos"], n + 1)
            dve.tensor_tensor(roped[q][:], with_sin[:], with_cos[:], ALU.add).then_inc(EV["rope"], 1)

        def v_out(dve, n, q):
            dve.wait_ge(EV["v"], n + 1)
            dve.tensor_copy(v_main[q][:], ps[:, 4, 0:LAT])
            dve.tensor_copy(v_rem[q][:], ps[0:REM, 4, LAT:2 * LAT]).then_inc(EV["vout"], 1)

        def maxima(dve, s, G):
            dve.wait_ge(EV["s"], GROUPS * s + G + 1)
            dve.tensor_reduce(nmax[:, HPG * G:HPG * G + HPG], ps[:, G % 2, :].rearrange("p (m k) -> p m k", m=HPG),
                              AX.X, ALU.max, negate=True)
            dve.tensor_reduce(nmax[:, HEADS + G:HEADS + G + 1], ps[:, 2 + G % 2, 0:T], AX.X, ALU.max,
                              negate=True).then_inc(EV["max"], 1)

        def split_max(dve, s):
            dve.wait_ge(EV["max"], GROUPS * (s + 1))
            dve.tensor_copy(nmax_parts[:, 0, :], nmax[:]).then_inc(EV["nm1"], 1)
            dve.wait_ge(EV["nm1"], s + 1)
            dve.tensor_tensor(nmax_parts[:, 1, :], nmax[:], nmax_parts[:, 0, :], ALU.subtract).then_inc(EV["nm2"], 1)

        def weighed_out(dve, s, G):
            dve.wait_ge(EV["pv"], GROUPS * s + G + 1)
            if G == 0:
                need(dve, EV["ot"], s)
            dve.tensor_copy(ouz[:, :, G, 0:P], ps[:, G, 0:2 * P].rearrange("p (a q) -> p a q", a=2)).then_inc(EV["ou"], 1)

        def weighed_rem_out(dve, s):
            dve.wait_ge(EV["pvr"], s + 1)
            w = HPG * REM
            for i in range(2):
                last = dve.tensor_copy(ouz[:, i, :, P:T], ps[:, 7, i * w:(i + 1) * w].rearrange("p (g q) -> p g q", q=REM))
            last.then_inc(EV["oz"], 1)

        def residual(dve, s, p):
            dve.wait_ge(EV["wo"], s + 1)
            need(dve, EV["store"], 16 * (s + 1))
            dve.wait_ge(EV["x1"], s + 1)
            dve.tensor_tensor(x2[p][:], ps[:, 7, 0:2 * T].rearrange("p (t j) -> p t j", t=DT), x1[p][:],
                              ALU.add).then_inc(EV["x2"], 1)

        def square(act, n):
            act.wait_ge(EV["xc"], n + 1)
            act.activation(sq[:], xc[:], ACT.Square).then_inc(EV["sq"], 1)

        def inv_std(act, n):
            act.wait_ge(EV["var"], n + 1)
            act.activation(ln_var[:], ps[:, 6, 0:T], ACT.Ln, bias=eps[:]).then_inc(EV["lnv"], 1)
            act.wait_ge(EV["lnv"], n + 1)
            act.activation(rstd[:], ln_var[:], ACT.Exp, scale=-0.5).then_inc(EV["rstd"], 1)

        def inv_mean_square(act, n):
            act.wait_ge(EV["nb"], n + 1)
            act.activation(ln_rms[:], norm_b[:], ACT.Ln, bias=eps[:]).then_inc(EV["lnr"], 1)
            act.wait_ge(EV["lnr"], n + 1)
            act.activation(inv_rms[:], ln_rms[:], ACT.Exp, scale=-0.5).then_inc(EV["ir"], 1)

        def nope_high(act, n):
            act.wait_ge(EV["qn"], n + 1)
            need(act, EV["stack"], 16 * 16 * n)
            for c in range(2):
                last = act.activation(nope_b[:, 2 * c:2 * c + 2, :], ps[:, 4 + c, 0:2 * T].rearrange("p (g j) -> p g j", g=2), ACT.Copy)
            last.then_inc(EV["nope_b"], 1)
            act.wait_ge(EV["nope_b"], n + 1)
            act.activation(nope[0][:], nope_b[:], ACT.Copy).then_inc(EV["qnh"], 1)

        def rope_raw(act, n):
            act.wait_ge(EV["qr"], n + 1)
            act.activation(raw[:, 0:3, :], ps[:, 4, 0:3 * T].rearrange("p (g j) -> p g j", g=3), ACT.Copy)
            act.activation(raw[:, 3:5, :], ps[:, 5, 0:2 * T].rearrange("p (g j) -> p g j", g=2), ACT.Copy).then_inc(EV["raw"], 1)

        def rope_short(act, n, q):
            act.wait_ge(EV["rope"], n + 1)
            act.activation(roped_b[q][:], roped[q][:], ACT.Copy).then_inc(EV["rope_b"], 1)

        def rope_high(act, n, q):
            act.wait_ge(EV["rope_b"], n + 1)
            act.activation(roped_hi[q][:], roped_b[q][:], ACT.Copy).then_inc(EV["rhi"], 1)

        def cast(act, s, p, G):
            if G == 0:
                act.wait_ge(EV["stack"], 16 * 16 * (s + 1))
                need(act, EV["s"], GROUPS * s)
            c = slice(G * HPG * T, (G + 1) * HPG * T + Q - REM)
            act.activation(stack_b[:, G], stacks[p][:, c].bitcast(F32), ACT.Copy).then_inc(EV["cast"], 1)

        def max_rows(act, s):
            act.wait_ge(EV["nmt"], s + 1)
            act.activation(nt[:], ps[0:40, 6, 0:P], ACT.Copy).then_inc(EV["nt"], 1)

        def exps(act, s, G):
            act.wait_ge(EV["st"], GROUPS * s + G + 1)
            need(act, EV["pv"], GROUPS * s + G - 1)
            act.activation(prob[G % 2][:], ps[:, 4 + G % 2, :].rearrange("p (m q) -> p m q", m=HPG), ACT.Exp,
                           scale=0.125).then_inc(EV["exp"], 1)

        def exps_rem(act, s):
            act.wait_ge(EV["expr_in"], s + 1)
            act.activation(prob_q[:].rearrange("p a b q -> p (a b q)"), ps[:, 6, 0:2 * P], ACT.Exp, scale=0.125)
            act.activation(prob_qq[:].rearrange("p a b q -> p (a b q)"), ps[0:REM, 6, 2 * P:4 * P], ACT.Exp,
                           scale=0.125).then_inc(EV["expr"], 1)

        def inv_sums(act, s):
            act.wait_ge(EV["oz"], s + 1)
            act.activation(lnz[:], ouz[:, 1], ACT.Ln).then_inc(EV["lnz"], 1)
            act.wait_ge(EV["lnz"], s + 1)
            act.activation(rz[:], lnz[:], ACT.Exp, scale=-1.0).then_inc(EV["rz"], 1)

        def add_tiles(pool, n, q):
            pool.wait_ge(EV["xload"], 16 * (n + 1))
            need(pool, EV["mean"], n)
            pool.tensor_tensor(xs[:], x[q][:, 0, :], x[q][:, 1, :], ALU.add).then_inc(EV["xs"], 1)

        def add_squares(pool, n):
            pool.wait_ge(EV["sq"], n + 1)
            pool.tensor_tensor(sqs[:], sq[:, 0, :], sq[:, 1, :], ALU.add).then_inc(EV["sqs"], 1)

        def layer_norm(pool, n, q):
            pool.wait_ge(EV["rstd"], n + 1)
            need(pool, EV["x2"], n - 1)
            pool.tensor_tensor(x1[q][:], xc[:], spread(rstd[:], 1, DT), ALU.mult).then_inc(EV["x1"], 1)

        def times_cos(pool, n):
            pool.wait_ge(EV["raw"], n + 1)
            pool.tensor_tensor(with_cos[:], raw[:], rope_cos[:], ALU.mult).then_inc(EV["cos"], 1)

        def rope_low(pool, n, q):
            pool.wait_ge(EV["rope_b"], n + 1)
            need(pool, EV["st"], GROUPS * (n - 1))
            pool.tensor_tensor(roped_lo[q][:], roped[q][:], roped_b[q][:], ALU.subtract).then_inc(EV["rlo"], 1)

        def keys_low(pool, n, q):
            pool.wait_ge(EV["rope_b"], n + 1)
            pool.tensor_tensor(keys_b[q][:], roped[q][:, GROUPS, :], roped_b[q][:, GROUPS, :], ALU.subtract).then_inc(EV["kb"], 1)

        def divide(pool, s):
            pool.wait_ge(EV["rz"], s + 1)
            if isinstance(s, int):
                need(pool, EV["wo"], s)
            pool.tensor_tensor(ot[:], ouz[:, 0], rz[:], ALU.mult).then_inc(EV["ot"], 1)

        def each_step(engine, step):
            step(0, 0, True, True, True)
            if seqs > 4:
                with engine.Fori(0, (seqs - 4) // 2) as i:
                    step(i * 2 + 1, 1, False, True, True)
                    step(i * 2 + 2, 0, False, True, True)
            step(seqs - 3, 1, False, True, True)
            step(seqs - 2, 0, False, True, False)
            step(seqs - 1, 1, False, False, False)

        with nc.Block() as block:

            @block.sync
            def _(sp):
                for dst, name in ((wqn_t, "wqn_t"), (wkb_t, "wkb_t"), (wo_n, "wo_n"), (wq_rope, "wq_rope"), (wkva, "wkva"),
                                  (w_ln, "w_ln1"), (rope_cos, "rope_cos"), (rope_sin, "rope_sin"), (masks_f, "masks"),
                                  (ident_f, "ident"), (onehot_f, "onehot2")):
                    sp.dma_start(dst[:], dram[name]).then_inc(sem["weights"], 16)
                load_x(sp, 0, 0)
                load_x(sp, 1, 1)
                stack(sp, 0, 0)

                def step(s, p, first, has_next, has_norm):
                    if has_norm:
                        load_x(sp, s + 2, p)
                    if has_next:
                        stack(sp, s + 1, 1 - p)
                    if not first:
                        store_x2(sp, s - 1, 1 - p)
                each_step(sp, step)
                store_x2(sp, seqs - 1, 1)
                sp.wait_ge(EV["store"], 16 * (seqs + 1))

            @block.tensor
            def _(pe):
                pe.wait_ge(sem["weights"], 176)
                for j in range(HPG):
                    for t in range(DT):
                        for g in range(GROUPS):
                            r = slice(Q * j, Q * j + Q)
                            pe.matmul(ps[:, j, (t * GROUPS + g) * LAT:(t * GROUPS + g + 1) * LAT],
                                      wqn_t[r, g, t * P:(t + 1) * P], wkb_t[r, g, :], start=True, stop=True)
                for j in range(HPG):
                    for g in range(GROUPS):
                        r = slice(Q * j, Q * j + Q)
                        mm = pe.matmul(ps[Q * g:Q * g + Q, 4 + j, 0:D], wkb_t[r, g, :], wo_n[r, g, :], start=True, stop=True)
                mm.then_inc(sem["absorb"], 1)
                pe.wait_ge(sem["absorbed"], 2)
                pe.wait_ge(sem["const"], 6)
                mean(pe, 0)
                var(pe, 0)
                project_rope(pe, 0)
                project_nope(pe, 0)
                project_v(pe, 0)
                mean(pe, 1)
                var(pe, 1)

                def step(s, p, first, has_next, has_norm):
                    n, m = s + 1, s + 2
                    if has_next:
                        project_rope(pe, n)
                    scores(pe, s, p, 0)
                    if has_next:
                        project_nope(pe, n)
                    scores(pe, s, p, 1)
                    scores(pe, s, p, 2)
                    scores(pe, s, p, 3)
                    if has_next:
                        project_v(pe, n)
                    if not first:
                        project_out(pe, s - 1)
                    turn_max(pe, s, m if has_next else n)
                    scores_t(pe, s, p, 0, m if has_next else n)
                    if has_norm:
                        mean(pe, m)
                    scores_t(pe, s, p, 1)
                    weigh(pe, s, p, 0)
                    scores_t(pe, s, p, 2)
                    if has_norm:
                        var(pe, m)
                    weigh(pe, s, p, 1)
                    scores_t(pe, s, p, 3)
                    scores_t_rem(pe, s, p, s + 3 if has_norm else seqs)
                    weigh(pe, s, p, 2)
                    weigh(pe, s, p, 3)
                    weigh_rem(pe, s, p)
                each_step(pe, step)
                project_out(pe, seqs - 1)

            @block.vector
            def _(dve):
                dve.memset(ones_avg[:], 1.0 / D).then_inc(sem["const"], 1)
                dve.memset(ones[:], 1.0).then_inc(sem["const"], 1)
                dve.memset(eps[:], EPS)
                dve.memset(waited[:], 0.0).then_inc(sem["store"], 16)
                for i in range(2):
                    dve.memset(stacks[i][:, HEADS * T:].bitcast(F32), 0.0)
                dve.wait_ge(sem["weights"], 176)
                dve.tensor_copy(masks[:], masks_f[:]).then_inc(sem["const"], 1)
                dve.tensor_copy(ident[:], ident_f[:]).then_inc(sem["const"], 1)
                dve.tensor_copy(onehot[:], onehot_f[:]).then_inc(sem["const"], 2)
                dve.wait_ge(sem["absorb"], 1)
                for j in range(HPG):
                    last = dve.tensor_copy(wq_nope[:].rearrange("p t g (j r) -> p j (t g) r", j=HPG)[:, j],
                                           ps[:, j, 0:D].rearrange("p (a r) -> p a r", r=LAT))
                last.then_inc(sem["absorbed"], 1)
                dve.tensor_copy(wo[:], ps[:, 4:8, 0:D]).then_inc(sem["absorbed"], 1)
                centre(dve, 0, 0)
                rms_terms(dve, 0)
                rms_norm(dve, 0)
                turn(dve, 0)
                rotate(dve, 0, 0)
                nope_low(dve, 0)
                v_out(dve, 0, 0)
                centre(dve, 1, 1)
                rms_terms(dve, 1)
                rms_norm(dve, 1)

                def step(s, p, first, has_next, has_norm):
                    n, m = s + 1, s + 2
                    if has_next:
                        turn(dve, n)
                    maxima(dve, s, 0)
                    if has_next:
                        rotate(dve, n, 1 - p)
                    maxima(dve, s, 1)
                    if has_next:
                        nope_low(dve, n)
                    maxima(dve, s, 2)
                    maxima(dve, s, 3)
                    split_max(dve, s)
                    if has_next:
                        v_out(dve, n, 1 - p)
                    if not first:
                        residual(dve, s - 1, 1 - p)
                    if has_norm:
                        centre(dve, m, p)
                    weighed_out(dve, s, 0)
                    if has_norm:
                        rms_terms(dve, m)
                    weighed_out(dve, s, 1)
                    if has_norm:
                        rms_norm(dve, m)
                    weighed_out(dve, s, 2)
                    weighed_out(dve, s, 3)
                    weighed_rem_out(dve, s)
                each_step(dve, step)
                residual(dve, seqs - 1, 1)

            @block.scalar
            def _(act):
                act.preload_act_table_set("natural_log_exp_and_others")
                act.wait_ge(sem["const"], 6)
                square(act, 0)
                inv_std(act, 0)
                inv_mean_square(act, 0)
                rope_raw(act, 0)
                nope_high(act, 0)
                rope_short(act, 0, 0)
                rope_high(act, 0, 0)
                square(act, 1)
                inv_std(act, 1)
                inv_mean_square(act, 1)

                def step(s, p, first, has_next, has_norm):
                    n, m = s + 1, s + 2
                    cast(act, s, p, 0)
                    cast(act, s, p, 1)
                    if not first:
                        inv_sums(act, s - 1)
                    if has_next:
                        rope_raw(act, n)
                    cast(act, s, p, 2)
                    cast(act, s, p, 3)
                    if has_next:
                        nope_high(act, n)
                        rope_short(act, n, 1 - p)
                        rope_high(act, n, 1 - p)
                    max_rows(act, s)
                    exps(act, s, 0)
                    if has_norm:
                        square(act, m)
                    exps(act, s, 1)
                    if has_norm:
                        inv_std(act, m)
                    exps(act, s, 2)
                    if has_norm:
                        inv_mean_square(act, m)
                    exps(act, s, 3)
                    exps_rem(act, s)
                each_step(act, step)
                inv_sums(act, seqs - 1)

            @block.gpsimd
            def _(pool):
                add_tiles(pool, 0, 0)
                add_squares(pool, 0)
                layer_norm(pool, 0, 0)
                times_cos(pool, 0)
                rope_low(pool, 0, 0)
                keys_low(pool, 0, 0)
                add_tiles(pool, 1, 1)
                add_squares(pool, 1)

                def step(s, p, first, has_next, has_norm):
                    n, m = s + 1, s + 2
                    if not first:
                        divide(pool, s - 1)
                    if has_norm:
                        add_tiles(pool, m, p)
                    if has_next:
                        times_cos(pool, n)
                        layer_norm(pool, n, 1 - p)
                        rope_low(pool, n, 1 - p)
                    if has_norm:
                        add_squares(pool, m)
                    if has_next:
                        keys_low(pool, n, 1 - p)
                each_step(pool, step)
                divide(pool, seqs - 1)


def moe_phase(nc, dram, h1_scratch, x2_scratch, out_dram, tokens, width):
    chunks = tokens // width
    tiles = width // P
    with ExitStack() as ctx:
        sb = lambda name, shape, dt=F32: ctx.enter_context(nc.sbuf_tensor(name, shape, dt))
        raw_up = [sb(f"m_raw_up{i}", [P, DT, 2, INNER]) for i in range(2)]
        raw_down = [sb(f"m_raw_down{i}", [P, D]) for i in range(2)]
        up_parts = [sb(f"m_up{i}", [P, ALL_E, DT, 2, INNER], F32R) for i in range(2)]
        down_parts = [sb(f"m_down{i}", [P, ALL_E, D], F32R) for i in range(2)]
        w_gate = sb("m_w_gate", [P, DT, EXPERTS])
        gate_bias = sb("m_gate_bias", [P, EXPERTS])
        order = sb("m_order", [P, EXPERTS])
        w_ln = sb("m_w_ln", [P, DT])
        ident = sb("m_ident", [P, P])
        expert_rows_f = sb("m_expert_rows_f", [2 * EXPERTS, EXPERTS, P])
        expert_rows = sb("m_expert_rows", [2 * EXPERTS, EXPERTS, P], F32R)
        ones_avg = sb("m_ones_avg", [P, P])
        eps = sb("m_eps", [P, 1])
        x2 = [sb(f"m_x2{i}", [P, DT, width]) for i in range(2)]
        both = [sb(f"m_both{i}", [P, DT, width]) for i in range(2)]
        sq = sb("m_sq", [P, DT, width])
        sqs = sb("m_sqs", [P, width])
        ln_sq = sb("m_ln_sq", [P, width])
        rstd = sb("m_rstd", [P, width])
        xn = sb("m_xn", [P, DT, width])
        xn_parts = [[sb(f"m_xn{i}_{k}", [P, DT, width], F32R) for k in range(2)] for i in range(2)]
        small = lambda name, *shape: sb(f"m_{name}", [P, tiles, *shape])
        logit, is_top, rank, first = (small(w, EXPERTS) for w in ("logit", "is_top", "rank", "first"))
        others, is_second, rank2, second = (small(w, EXPERTS) for w in ("others", "is_second", "rank2", "second"))
        share1, share2, comb = (small(w, EXPERTS) for w in ("share1", "share2", "comb"))
        top, best, top2, best2 = (small(w) for w in ("top", "best", "top2", "best2"))
        diff, ratio, total, weight1, weight2 = (small(w) for w in ("diff", "ratio", "total", "weight1", "weight2"))
        comb_parts = sb("m_comb_parts", [P, tiles, 2, EXPERTS], F32R)
        comb_rows = [sb(f"m_comb_rows{i}", [2 * EXPERTS, width], F32R) for i in range(2)]
        silu = [sb(f"m_silu{i}", [P, width]) for i in range(2)]
        gated = sb("m_gated", [P, width])
        hidden = [sb(f"m_hidden{i}", [P, width]) for i in range(2)]
        hidden_parts = [[sb(f"m_hidden{i}_{k}", [P, width], F32R) for k in range(2)] for i in range(2)]
        out = [sb(f"m_out{i}", [P, DT, width]) for i in range(2)]
        y = [ctx.enter_context(nc.psum_tensor(f"m_y{t}", [P, 512], F32)) for t in range(DT)]
        gu = [[ctx.enter_context(nc.psum_tensor(f"m_gu{i}_{w}", [P, 512], F32)) for w in range(2)] for i in range(2)]
        share = ctx.enter_context(nc.psum_tensor("m_share", [P, 512], F32))
        misc = ctx.enter_context(nc.psum_tensor("m_misc", [P, 512], F32))
        sem = names(ctx, nc, "m", "weights raw0 raw1 split_hi split_lo const x2load h1load sq sqs mean lnsq rstd xn xnh xnl logits route diff ratio "
                    "combT rows gu share silu gated hidden hi lo down sum out store")
        ROUTE = 20
        places = range(ALL_E)

        def load_x2(sp, n, q):
            token = n * width
            need_all(sp, (sem["xn"], n - 1), (sem["sum"], n - 1), (sem["x2load"], 16 * n))
            sp.dma_start(x2[q][:], x2_scratch[:, :, bass.ds(token, width)]).then_inc(sem["x2load"], 16)

        def load_h1(sp, n, q):
            token = n * width
            need_all(sp, (sem["out"], n - 1), (sem["h1load"], 16 * n))
            sp.dma_start(both[q][:], h1_scratch[:, :, bass.ds(token, width)]).then_inc(sem["h1load"], 16)

        def store(sp, c, p):
            token = c * width
            need_all(sp, (sem["out"], c + 1), (sem["store"], 16 * (c + 1)))
            sp.dma_start(out_dram[:, :, bass.ds(token, width)], out[p][:]).then_inc(sem["store"], 16)

        def mean_square(pe, n):
            pe.wait_ge(sem["sqs"], n + 1)
            need(pe, sem["rows"], n)
            pe.matmul(misc[:, 0:width], ones_avg[:], sqs[:], start=True, stop=True).then_inc(sem["mean"], 1)

        def logits(pe, n):
            pe.wait_ge(sem["xn"], n + 1)
            pe.wait_ge(sem["lnsq"], n + 1)
            for i in range(tiles):
                for k in range(DT):
                    mm = pe.matmul(misc[:, i * EXPERTS:(i + 1) * EXPERTS], xn[:, k, i * P:(i + 1) * P], w_gate[:, k, :],
                                   start=(k == 0), stop=(k == DT - 1))
            mm.then_inc(sem["logits"], 1)

        def turn_shares(pe, n):
            pe.wait_ge(sem["route"], ROUTE * (n + 1))
            for i in range(tiles):
                mm = pe.matmul(misc[0:2 * EXPERTS, i * P:(i + 1) * P],
                               comb_parts[:, i].rearrange("p a e -> p (a e)").bitcast(F32), ident[:], start=True, stop=True)
            mm.then_inc(sem["combT"], 1)

        def gate_up(pe, c, p, i):
            if i == 0:
                pe.wait_ge(sem["xnh"], c + 1)
                pe.wait_ge(sem["xnl"], c + 1)
            need(pe, sem["hidden"], ALL_E * c + i - 1)
            b = (p + i) % 2
            for w in range(2):
                for j, (a, x) in enumerate(((0, 0), (0, 1), (1, 0))):
                    for k in range(DT):
                        mm = pe.matmul(gu[b][w][:, 0:width], up_parts[a][:, i, k, w, :], xn_parts[p][x][:, k, :],
                                       start=(j == 0 and k == 0), stop=(j == 2 and k == DT - 1))
            mm.then_inc(sem["gu"], 1)

        def spread_share(pe, c, p, i):
            pe.wait_ge(sem["rows"], c + 1)
            need(pe, sem["hidden"], ALL_E * c + i)
            pe.matmul(share[:, 0:width], expert_rows[:, i - 1, :], comb_rows[p][:], start=True, stop=True).then_inc(sem["share"], 1)

        def down(pe, c, p, i):
            pe.wait_ge(sem["hi"], ALL_E * c + i + 1)
            if i == 0:
                need(pe, sem["out"], c)
            b = (p + i) % 2
            parts = ((0, 0), (1, 0), (0, 1))
            for j, (a, x) in enumerate(parts):
                if j == 2:
                    pe.wait_ge(sem["lo"], ALL_E * c + i + 1)
                for t in range(DT):
                    mm = pe.matmul(y[t][:, 0:width], down_parts[a][:, i, t * P:(t + 1) * P], hidden_parts[b][x][:],
                                   start=(i == 0 and j == 0), stop=(i == ALL_E - 1 and j == 2))
            mm.then_inc(sem["down"], 1)

        def normalise(dve, n, q):
            dve.wait_ge(sem["rstd"], n + 1)
            need(dve, sem["logits"], n)
            need(dve, sem["xnl"], n)
            for t in range(DT):
                last = dve.scalar_tensor_tensor(out=xn[:, t, :], in0=x2[q][:, t, :], scalar=w_ln[:, t:t + 1], in1=rstd[:],
                                                op0=ALU.mult, op1=ALU.mult)
            last.then_inc(sem["xn"], 1)

        def weights_low(dve, i):
            dve.wait_ge(sem["split_hi"], i + 1)
            dve.tensor_tensor(up_parts[1][:, i], raw_up[i % 2][:], up_parts[0][:, i].bitcast(F32), ALU.subtract)
            dve.tensor_tensor(down_parts[1][:, i], raw_down[i % 2][:], down_parts[0][:, i].bitcast(F32),
                              ALU.subtract).then_inc(sem["split_lo"], 1)

        def choose(dve, n):
            r = ROUTE * n
            route = sem["route"]
            dve.wait_ge(sem["logits"], n + 1)
            need(dve, sem["combT"], n)
            at = misc[:, 0:tiles * EXPERTS].rearrange("p (i e) -> p i e", e=EXPERTS)
            dve.tensor_tensor(logit[:], at, spread(gate_bias[:], 1, tiles), ALU.add).then_inc(route, 1)
            dve.wait_ge(route, r + 1)
            dve.tensor_reduce(top[:], logit[:], AX.X, ALU.max).then_inc(route, 1)
            dve.wait_ge(route, r + 2)
            dve.tensor_tensor(is_top[:], logit[:], spread(top[:], 2, EXPERTS), ALU.is_equal).then_inc(route, 1)
            dve.wait_ge(route, r + 3)
            dve.tensor_tensor(rank[:], is_top[:], spread(order[:], 1, tiles), ALU.mult).then_inc(route, 1)
            dve.wait_ge(route, r + 4)
            dve.tensor_reduce(best[:], rank[:], AX.X, ALU.max).then_inc(route, 1)
            dve.wait_ge(route, r + 5)
            dve.tensor_tensor(first[:], rank[:], spread(best[:], 2, EXPERTS), ALU.is_equal).then_inc(route, 1)
            dve.wait_ge(route, r + 6)
            dve.scalar_tensor_tensor(out=others[:], in0=first[:], scalar=NEG, in1=logit[:], op0=ALU.mult, op1=ALU.add).then_inc(route, 1)
            dve.wait_ge(route, r + 7)
            dve.tensor_reduce(top2[:], others[:], AX.X, ALU.max).then_inc(route, 1)
            dve.wait_ge(route, r + 8)
            dve.tensor_tensor(diff[:], top2[:], top[:], ALU.subtract).then_inc(sem["diff"], 1)
            dve.tensor_tensor(is_second[:], others[:], spread(top2[:], 2, EXPERTS), ALU.is_equal).then_inc(route, 1)
            dve.wait_ge(route, r + 9)
            dve.tensor_tensor(rank2[:], is_second[:], spread(order[:], 1, tiles), ALU.mult).then_inc(route, 1)
            dve.wait_ge(route, r + 10)
            dve.tensor_reduce(best2[:], rank2[:], AX.X, ALU.max).then_inc(route, 1)
            dve.wait_ge(route, r + 11)
            dve.tensor_tensor(second[:], rank2[:], spread(best2[:], 2, EXPERTS), ALU.is_equal).then_inc(route, 1)

        def shares(dve, n):
            r = ROUTE * n
            route = sem["route"]
            dve.wait_ge(sem["ratio"], n + 1)
            dve.tensor_scalar(total[:], ratio[:], 1.0, None, ALU.add).then_inc(route, 1)
            dve.wait_ge(route, r + 13)
            dve.reciprocal(weight1[:], total[:]).then_inc(route, 1)
            dve.wait_ge(route, r + 14)
            dve.tensor_tensor(weight2[:], ratio[:], weight1[:], ALU.mult).then_inc(route, 1)
            dve.tensor_tensor(share1[:], first[:], spread(weight1[:], 2, EXPERTS), ALU.mult).then_inc(route, 1)
            dve.wait_ge(route, r + 16)
            dve.tensor_tensor(share2[:], second[:], spread(weight2[:], 2, EXPERTS), ALU.mult).then_inc(route, 1)
            dve.wait_ge(route, r + 17)
            dve.tensor_tensor(comb[:], share1[:], share2[:], ALU.add).then_inc(route, 1)
            dve.wait_ge(route, r + 18)
            dve.tensor_copy(comb_parts[:, :, 0, :], comb[:]).then_inc(route, 1)
            dve.wait_ge(route, r + 19)
            dve.tensor_tensor(comb_parts[:, :, 1, :], comb[:], comb_parts[:, :, 0, :].bitcast(F32), ALU.subtract).then_inc(route, 1)

        def gate(dve, c, p, i):
            b = (p + i) % 2
            dve.wait_ge(sem["silu"], ALL_E * c + i + 1)
            need(dve, sem["lo"], ALL_E * c + i - 1)
            if i == 0:
                dve.tensor_tensor(hidden[b][:], gu[b][1][:, 0:width], silu[b][:], ALU.mult).then_inc(sem["hidden"], 1)
                return
            dve.tensor_tensor(gated[:], gu[b][1][:, 0:width], silu[b][:], ALU.mult).then_inc(sem["gated"], 1)
            dve.wait_ge(sem["gated"], EXPERTS * c + i)
            dve.wait_ge(sem["share"], EXPERTS * c + i)
            dve.tensor_tensor(hidden[b][:], gated[:], share[:, 0:width], ALU.mult).then_inc(sem["hidden"], 1)

        def finish(dve, c, p):
            dve.wait_ge(sem["down"], ALL_E * (c + 1))
            dve.wait_ge(sem["sum"], c + 1)
            need(dve, sem["store"], 16 * (c + 1))
            for t in range(DT):
                last = dve.tensor_tensor(out[p][:, t, :], y[t][:, 0:width], both[p][:, t, :], ALU.add)
            last.then_inc(sem["out"], 1)

        def square(act, n, q):
            act.wait_ge(sem["x2load"], 16 * (n + 1))
            act.activation(sq[:], x2[q][:], ACT.Square).then_inc(sem["sq"], 1)

        def inv_rms(act, n):
            act.wait_ge(sem["mean"], n + 1)
            act.activation(ln_sq[:], misc[:, 0:width], ACT.Ln, bias=eps[:]).then_inc(sem["lnsq"], 1)
            act.wait_ge(sem["lnsq"], n + 1)
            act.activation(rstd[:], ln_sq[:], ACT.Exp, scale=-0.5).then_inc(sem["rstd"], 1)

        def norm_high(act, n, q):
            act.wait_ge(sem["xn"], n + 1)
            need(act, sem["gu"], ALL_E * (n - 1))
            act.activation(xn_parts[q][0][:], xn[:], ACT.Copy).then_inc(sem["xnh"], 1)

        def weights_high(act, i):
            act.wait_ge(sem[f"raw{i % 2}"], 32 * (i // 2 + 1))
            act.activation(up_parts[0][:, i], raw_up[i % 2][:], ACT.Copy)
            act.activation(down_parts[0][:, i], raw_down[i % 2][:], ACT.Copy).then_inc(sem["split_hi"], 1)

        def share_ratio(act, n):
            act.wait_ge(sem["diff"], n + 1)
            act.activation(ratio[:], diff[:], ACT.Exp).then_inc(sem["ratio"], 1)

        def share_rows(act, n, q):
            act.wait_ge(sem["combT"], n + 1)
            need(act, sem["share"], EXPERTS * (n - 1))
            act.activation(comb_rows[q][:], misc[0:2 * EXPERTS, 0:width], ACT.Copy).then_inc(sem["rows"], 1)

        def silu_gate(act, c, p, i):
            b = (p + i) % 2
            act.wait_ge(sem["gu"], ALL_E * c + i + 1)
            act.activation(silu[b][:], gu[b][0][:, 0:width], ACT.Silu).then_inc(sem["silu"], 1)

        def hidden_high(act, c, p, i):
            b = (p + i) % 2
            act.wait_ge(sem["hidden"], ALL_E * c + i + 1)
            need(act, sem["down"], ALL_E * c + i - 1)
            act.activation(hidden_parts[b][0][:], hidden[b][:], ACT.Copy).then_inc(sem["hi"], 1)

        def add_squares(pool, n):
            pool.wait_ge(sem["sq"], n + 1)
            pool.tensor_tensor(sqs[:], sq[:, 0, :], sq[:, 1, :], ALU.add).then_inc(sem["sqs"], 1)

        def norm_low(pool, n, q):
            pool.wait_ge(sem["xnh"], n + 1)
            pool.tensor_tensor(xn_parts[q][1][:], xn[:], xn_parts[q][0][:].bitcast(F32), ALU.subtract).then_inc(sem["xnl"], 1)

        def add_residuals(pool, n, q):
            pool.wait_ge(sem["h1load"], 16 * (n + 1))
            pool.tensor_tensor(both[q][:], both[q][:], x2[q][:], ALU.add).then_inc(sem["sum"], 1)

        def hidden_low(pool, c, p, i):
            b = (p + i) % 2
            pool.wait_ge(sem["hi"], ALL_E * c + i + 1)
            pool.tensor_tensor(hidden_parts[b][1][:], hidden[b][:], hidden_parts[b][0][:].bitcast(F32),
                               ALU.subtract).then_inc(sem["lo"], 1)

        def each_step(engine, step):
            step(0, 0, True, False)
            if chunks > 2:
                with engine.Fori(0, (chunks - 2) // 2) as i:
                    step(i * 2 + 1, 1, False, False)
                    step(i * 2 + 2, 0, False, False)
            step(chunks - 1, 1, False, True)

        LOADS = 16 * 6
        with nc.Block() as block:

            @block.sync
            def _(sp):
                for dst, name in ((w_gate, "w_gate"), (gate_bias, "gate_bias"), (order, "order"), (w_ln, "w_ln2"),
                                  (ident, "ident"), (expert_rows_f, "expert_rows")):
                    sp.dma_start(dst[:], dram[name]).then_inc(sem["weights"], 16)
                load_x2(sp, 0, 0)
                for i in places:
                    need(sp, sem["split_lo"], i - 1)
                    sp.dma_start(raw_up[i % 2][:], dram["up"][:, i]).then_inc(sem[f"raw{i % 2}"], 16)
                    sp.dma_start(raw_down[i % 2][:], dram["down"][:, i]).then_inc(sem[f"raw{i % 2}"], 16)
                    if i == 1:
                        load_h1(sp, 0, 0)
                        load_x2(sp, 1, 1)
                        load_h1(sp, 1, 1)

                def step(c, p, is_first, is_last):
                    if not (is_first or is_last):
                        load_x2(sp, c + 1, 1 - p)
                        load_h1(sp, c + 1, 1 - p)
                    if not is_first:
                        store(sp, c - 1, 1 - p)
                each_step(sp, step)
                store(sp, chunks - 1, 1)
                sp.wait_ge(sem["store"], 16 * (chunks + 1))

            @block.tensor
            def _(pe):
                pe.wait_ge(sem["const"], 3)
                pe.wait_ge(sem["weights"], LOADS)
                mean_square(pe, 0)
                logits(pe, 0)
                turn_shares(pe, 0)

                def step(c, p, is_first, is_last):
                    for i in places:
                        if is_first:
                            pe.wait_ge(sem["split_lo"], i + 1)
                        gate_up(pe, c, p, i)
                        if i > 0:
                            spread_share(pe, c, p, i)
                        if i >= 2:
                            down(pe, c, p, i - 2)
                        elif not is_first:
                            down(pe, c - 1, 1 - p, ALL_E - 2 + i)
                        if not is_last:
                            if i == 1:
                                mean_square(pe, c + 1)
                            if i == 4:
                                logits(pe, c + 1)
                            if i == 6:
                                turn_shares(pe, c + 1)
                each_step(pe, step)
                for i in (ALL_E - 2, ALL_E - 1):
                    down(pe, chunks - 1, 1, i)

            @block.vector
            def _(dve):
                dve.memset(ones_avg[:], 1.0 / D).then_inc(sem["const"], 1)
                dve.memset(eps[:], EPS).then_inc(sem["const"], 1)
                dve.memset(ratio[:], 0.0).then_inc(sem["store"], 16)
                dve.wait_ge(sem["weights"], LOADS)
                dve.tensor_copy(expert_rows[:], expert_rows_f[:]).then_inc(sem["const"], 1)
                normalise(dve, 0, 0)
                weights_low(dve, 0)
                choose(dve, 0)
                shares(dve, 0)
                weights_low(dve, 1)

                def step(c, p, is_first, is_last):
                    for i in places:
                        gate(dve, c, p, i)
                        if is_first and i + 2 < ALL_E:
                            weights_low(dve, i + 2)
                        if i == 1 and not is_first:
                            finish(dve, c - 1, 1 - p)
                        if not is_last:
                            if i == 2:
                                normalise(dve, c + 1, 1 - p)
                            if i == 4:
                                choose(dve, c + 1)
                            if i == 5:
                                shares(dve, c + 1)
                each_step(dve, step)
                finish(dve, chunks - 1, 1)

            @block.scalar
            def _(act):
                act.preload_act_table_set("natural_log_exp_and_others")
                act.wait_ge(sem["const"], 2)
                square(act, 0, 0)
                inv_rms(act, 0)
                norm_high(act, 0, 0)
                weights_high(act, 0)
                share_ratio(act, 0)
                weights_high(act, 1)
                share_rows(act, 0, 0)
                act.preload_act_table_set("silu_and_others")

                def step(c, p, is_first, is_last):
                    if not is_last:
                        square(act, c + 1, 1 - p)
                    for i in places:
                        if is_first and i + 2 < ALL_E:
                            weights_high(act, i + 2)
                        silu_gate(act, c, p, i)
                        hidden_high(act, c, p, i)
                        if not is_last:
                            if i == 1:
                                act.preload_act_table_set("natural_log_exp_and_others")
                                inv_rms(act, c + 1)
                                act.preload_act_table_set("silu_and_others")
                            if i == 3:
                                norm_high(act, c + 1, 1 - p)
                            if i == 4:
                                act.preload_act_table_set("natural_log_exp_and_others")
                                share_ratio(act, c + 1)
                                act.preload_act_table_set("silu_and_others")
                            if i == 6:
                                share_rows(act, c + 1, 1 - p)
                each_step(act, step)

            @block.gpsimd
            def _(pool):
                add_squares(pool, 0)
                norm_low(pool, 0, 0)
                add_residuals(pool, 0, 0)

                def step(c, p, is_first, is_last):
                    if not is_last:
                        add_squares(pool, c + 1)
                    for i in places:
                        hidden_low(pool, c, p, i)
                        if not is_last:
                            if i == 3:
                                norm_low(pool, c + 1, 1 - p)
                            if i == 5:
                                add_residuals(pool, c + 1, 1 - p)
                each_step(pool, step)


def host_layouts(a):
    f = {}
    seqs = a["x"].shape[0]

    def feature_tiles(w):
        return w.reshape(-1, P, w.shape[-1]).transpose(1, 0, 2)

    def column(v):
        return v.reshape(-1, P).T

    n = 4
    patches = a["x"].reshape(seqs, 3, n, 16, n, 16).transpose(1, 3, 5, 0, 2, 4).reshape(FEAT, seqs * n * n)
    f["patches"] = feature_tiles(patches)
    f["txt"] = a["txt"].transpose(2, 0, 1).reshape(DT, P, seqs, TXT_TOK).transpose(1, 2, 0, 3).reshape(P, -1)
    f["tok_w"] = feature_tiles(a["L0_tok_W"].T)
    f["tok_b"] = column(a["L0_tok_b"])
    f["pos"] = feature_tiles(a["L0_tok_pos_emb"].T)
    w = a["L0_attn_qkv_w"].T.reshape(D, HEADS, 3, HD1)
    b = a["L0_attn_qkv_b"].reshape(HEADS, 3, HD1)
    f["wqk"] = feature_tiles(w[:, :, 0:2].reshape(D, 2 * D)).reshape(P, DT, GROUPS, P)
    f["bqk"] = column(b[:, 0:2].ravel())
    f["wv"] = feature_tiles(w[:, :, 2].reshape(D, D))
    f["bv"] = np.broadcast_to(b[:, 2].reshape(1, D), (P, D))
    fcw = np.zeros((HPG, Q, GROUPS, D), np.float32)
    fcw[:, :HD1] = a["L0_attn_fc_w"].T.reshape(GROUPS, HPG, HD1, D).transpose(1, 2, 0, 3)
    f["fcw"] = fcw.reshape(P, GROUPS, D)
    f["fcb"] = column(a["L0_attn_fc_b"])
    f["w_ln1"] = column(a["L0_ffn_w_ln1"])
    wq = a["L0_ffn_Wq"].reshape(D, GROUPS, HPG, 2, NOPE)
    f["wqn_t"] = wq[:, :, :, 0].transpose(2, 3, 1, 0).reshape(P, GROUPS, D)
    f["wq_rope"] = feature_tiles(wq[:, :, :, 1].reshape(D, GROUPS * P)).reshape(P, DT, GROUPS, P)
    wkb = a["L0_ffn_Wkvb"].reshape(LAT, GROUPS, HPG, NOPE)
    f["wkb_t"] = wkb.transpose(2, 3, 1, 0).reshape(P, GROUPS, LAT)
    f["wo_n"] = a["L0_ffn_Wo"].reshape(GROUPS, HPG, 2, NOPE, D)[:, :, 0].transpose(1, 2, 0, 3).reshape(P, GROUPS, D)
    f["wkva"] = feature_tiles(np.concatenate([a["L0_ffn_Wkva"]] * 2, 1))
    f["w_ln2"] = column(a["L0_ffn_w_ln2"])
    f["w_gate"] = feature_tiles(a["L0_ffn_Wgate"])
    f["gate_bias"] = np.broadcast_to(a["L0_ffn_expert_bias"][None], (P, EXPERTS))
    up = np.stack([np.concatenate([a["L0_ffn_s" + w], a["L0_ffn_" + w]]) for w in ("Wg", "Wu")])
    f["up"] = up.reshape(2, ALL_E, DT, P, INNER).transpose(3, 1, 2, 0, 4)
    f["down"] = np.concatenate([a["L0_ffn_sWd"], a["L0_ffn_Wd"]]).transpose(1, 0, 2)
    f["order"] = np.broadcast_to(np.arange(EXPERTS, 0, -1, dtype=np.float32)[None], (P, EXPERTS))
    owner = np.arange(2 * EXPERTS)[:, None] % EXPERTS == np.arange(EXPERTS)[None]
    f["expert_rows"] = np.broadcast_to(owner.astype(np.float32)[:, :, None], (2 * EXPERTS, EXPERTS, P))
    half = np.arange(0, ROPE, 2, dtype=np.float32) / np.float32(ROPE)
    angle = np.outer(np.arange(T, dtype=np.float32), np.float32(1.0) / np.float32(100000.0) ** half).astype(np.float32)
    cos, sin = (np.repeat(c(angle).T, 2, 0).astype(np.float32) for c in (np.cos, np.sin))
    sin[0::2] *= -1
    cos_tiles, sin_tiles = np.ones((P, HPG + 1, T), np.float32), np.zeros((P, HPG + 1, T), np.float32)
    for quadrant in range(4):
        r = slice(Q * quadrant, Q * quadrant + Q)
        cos_tiles[r, :HPG], sin_tiles[r, :HPG] = cos[:, None], sin[:, None]
        if quadrant % 2:
            cos_tiles[r, HPG], sin_tiles[r, HPG] = cos, sin
    f["rope_cos"], f["rope_sin"] = cos_tiles, sin_tiles
    one, two = np.arange(P)[:, None], np.arange(P)[None, :]
    masks = np.zeros((P, 2 * P + T + REM), np.float32)
    masks[:, 0:P][two > one] = NEG
    masks[:, P:2 * P][one > two] = NEG
    last = np.where(one % Q < REM, P + one % Q, T)
    masks[:, 2 * P:2 * P + T][np.arange(T)[None, :] > last] = NEG
    masks[:REM, 2 * P + T:][one[:REM] > two[:, :REM]] = NEG
    f["masks"] = masks
    row, place = np.arange(2 * (HEADS + GROUPS))[:, None] % (HEADS + GROUPS), np.arange(HEADS + GROUPS)[None, :]
    f["onehot2"] = np.broadcast_to((row == place).astype(np.float32)[:, :, None], (40, HEADS + GROUPS, P))
    rows = np.arange(P)
    f["rem_mask"] = (rows % Q < REM).astype(np.float32)[:, None]
    f["ident"] = np.eye(P, dtype=np.float32)
    cols = np.arange(HEADS + GROUPS)
    owns = np.zeros((HEADS + GROUPS, HEADS), np.float32)
    for h in range(HEADS):
        owns[h, h] = owns[HEADS + h // HPG, h] = 1
    f["onehot1"] = np.broadcast_to(np.concatenate([owns, owns])[:, :, None], (40, HEADS, P))
    rem = np.zeros((41, HEADS, Q), np.float32)
    rem[:40, :, :REM] = np.concatenate([owns, owns])[:, :, None]
    rem[40, :, REM:] = NEG
    f["onehot1_rem"] = rem
    main = np.concatenate([cols < HEADS] * 2)
    f["nt_rows"] = np.stack([main, ~main], 1).astype(np.float32)
    return {k: np.ascontiguousarray(v) for k, v in f.items()}


def build(nc, dram, out, seqs):
    h1 = nc.dram_tensor("h1_scratch", [P, DT, seqs * T], F32).ap()
    x2 = nc.dram_tensor("x2_scratch", [P, DT, seqs * T], F32).ap()
    with nc.sbuf_tensor("embedded", [P, DT, seqs * IMG_TOK], F32) as embedded:
        embed_phase(nc, dram, embedded, seqs)
        attn1_phase(nc, dram, embedded, h1, seqs)
    attn2_phase(nc, dram, h1, x2, seqs)
    moe_phase(nc, dram, h1, x2, out, seqs * T, CHUNK)


def kernel(**inputs):
    import concourse.bacc as bacc
    from concourse.bass_utils import run_bass_kernel_spmd

    laid = host_layouts({name: np.asarray(value) for name, value in inputs.items()})
    nc = bacc.Bacc("TRN2", target_bir_lowering=False, num_devices=1)
    arrays = {f"in_{name}": value for name, value in laid.items()}
    dram = {name: nc.dram_tensor(f"in_{name}", value.shape, F32, kind="ExternalInput").ap() for name, value in laid.items()}
    out = nc.dram_tensor("out", [P, DT, SEQS * T], F32, kind="ExternalOutput").ap()
    build(nc, dram, out, SEQS)
    result = run_bass_kernel_spmd(nc, [arrays], core_ids=[0])
    got = np.asarray(result.results[0]["out"])
    return np.ascontiguousarray(got.reshape(P, DT, SEQS, T).transpose(2, 3, 1, 0)).reshape(SEQS, T, D)
```

```python
from contextlib import ExitStack

import numpy as np

import concourse.bass as bass
from concourse import mybir

F32 = mybir.dt.float32
F32R = mybir.dt.float32r
BF16 = mybir.dt.bfloat16
ALU = mybir.AluOpType
ACT = mybir.ActivationFunctionType
AX = mybir.AxisListType

P = 128
SEQS, IMG_TOK, TXT_TOK, D = 64, 16, 128, 256
T = IMG_TOK + TXT_TOK
DT = D // P
HEADS, GROUPS, HPG = 16, 4, 4
Q = 32
REM = T - P
PAD_T = P + Q
HD1 = D // HEADS
SPLIT = 6
PARTS = 3
FEAT = 768
KT_EMB = FEAT // P
EPS = 1e-5
NOPE = ROPE = LAT = 32
EXPERTS, ALL_E, TOPK, INNER = 8, 9, 2, 128
NEG = -1.0e30
CHUNK = 512


def need(engine, semaphore, value):
    if isinstance(value, int) and value <= 0:
        return
    engine.wait_ge(semaphore, value)


def in_register(engine, value):
    if isinstance(value, int):
        return value
    register = engine.alloc_register()
    engine.reg_mov(register, value)
    return register


def need_all(engine, *waits):
    waits = [(semaphore, in_register(engine, value)) for semaphore, value in waits]
    for semaphore, value in waits:
        need(engine, semaphore, value)


def spread(ap, axis, n):
    a = ap.unsqueeze(axis)
    shape = list(a.shape)
    shape[axis] = n
    return a.to_broadcast(shape)


def names(ctx, nc, prefix, words):
    return {w: ctx.enter_context(nc.semaphore(f"{prefix}_{w}")) for w in words.split()}


def embed_phase(nc, dram, embedded, seqs):
    tokens = seqs * IMG_TOK
    width = min(CHUNK, tokens)
    chunks = tokens // width
    with ExitStack() as ctx:
        sb = lambda name, shape, dt=F32: ctx.enter_context(nc.sbuf_tensor(name, shape, dt))
        weights = sb("e_weights", [P, KT_EMB, D])
        patches = sb("e_patches", [P, chunks, KT_EMB, width])
        bias = sb("e_bias", [P, DT])
        pos = sb("e_pos", [P, DT, IMG_TOK])
        out = [[ctx.enter_context(nc.psum_tensor(f"e_out{i}_{t}", [P, width], F32)) for t in range(DT)] for i in range(2)]
        sem = names(ctx, nc, "e", "weights small patches product embedded")
        with nc.Block() as block:

            @block.sync
            def _(sp):
                sp.dma_start(weights[:], dram["tok_w"]).then_inc(sem["weights"], 16)
                for c in range(chunks):
                    need(sp, sem["patches"], 16 * c)
                    sp.dma_start(patches[:, c], dram["patches"][:, :, c * width:(c + 1) * width]).then_inc(sem["patches"], 16)
                    if c == 0:
                        sp.dma_start(bias[:], dram["tok_b"]).then_inc(sem["small"], 16)
                        sp.dma_start(pos[:], dram["pos"]).then_inc(sem["small"], 16)

            @block.tensor
            def _(pe):
                pe.wait_ge(sem["weights"], 16)
                for c in range(chunks):
                    pe.wait_ge(sem["patches"], 16 * (c + 1))
                    need(pe, sem["embedded"], c - 1)
                    for t in range(DT):
                        for k in range(KT_EMB):
                            mm = pe.matmul(out[c % 2][t][:], weights[:, k, t * P:(t + 1) * P], patches[:, c, k, :],
                                           start=(k == 0), stop=(k == KT_EMB - 1))
                    mm.then_inc(sem["product"], 1)

            @block.vector
            def _(dve):
                dve.wait_ge(sem["small"], 32)
                n = width // IMG_TOK
                for c in range(chunks):
                    dve.wait_ge(sem["product"], c + 1)
                    for t in range(DT):
                        last = dve.scalar_tensor_tensor(
                            out=embedded[:, t, c * width:(c + 1) * width].rearrange("p (s n) -> p s n", n=IMG_TOK),
                            in0=out[c % 2][t][:].rearrange("p (s n) -> p s n", n=IMG_TOK), scalar=bias[:, t:t + 1],
                            in1=spread(pos[:, t, :], 1, n), op0=ALU.add, op1=ALU.add)
                    last.then_inc(sem["embedded"], 1)


def attn1_phase(nc, dram, embedded, h1_scratch, seqs):
    with ExitStack() as ctx:
        sb = lambda name, shape, dt=F32: ctx.enter_context(nc.sbuf_tensor(name, shape, dt))
        wqk = sb("a_wqk", [P, DT, 4, P])
        bqk = sb("a_bqk", [P, 4])
        wv = sb("a_wv", [P, DT, D])
        bv = sb("a_bv", [P, D])
        bv_rem = sb("a_bv_rem", [P, D])
        fcw = sb("a_fcw", [P, GROUPS, D])
        fcb = sb("a_fcb", [P, DT])
        rem_mask = sb("a_rem_mask", [P, 1])
        ones_avg = sb("a_ones_avg", [P, P])
        ident_f = sb("a_ident_f", [P, P])
        ident = sb("a_ident", [P, P], BF16)
        onehot_f = sb("a_onehot_f", [40, HEADS, P])
        onehot_rem_f = sb("a_onehot_rem_f", [41, HEADS, Q])
        onehot = sb("a_onehot", [40, HEADS, P], BF16)
        onehot_rem = sb("a_onehot_rem", [41, HEADS, Q], BF16)
        nt_rows = sb("a_nt_rows", [40, 2])
        eps = sb("a_eps", [P, 1])
        waited = sb("a_waited", [1, 1])
        x = [sb(f"a_x{i}", [P, DT, T]) for i in range(2)]
        res = [sb(f"a_res{i}", [P, DT, T]) for i in range(2)]
        xs = sb("a_xs", [P, T])
        xc = sb("a_xc", [P, DT, T])
        sq = sb("a_sq", [P, DT, T])
        sqs = sb("a_sqs", [P, T])
        ln_var = sb("a_ln_var", [P, T])
        rstd = sb("a_rstd", [P, T])
        xn = sb("a_xn", [P, DT, T])
        xn_rem = sb("a_xn_rem", [P, DT, P])
        qk = sb("a_qk", [P, 2, 2, T])
        parts = [sb(f"a_part{i}", [P, 2, 2, T], BF16) for i in range(PARTS)]
        rest = sb("a_rest", [P, 2, 2, T])
        stacks = [sb(f"a_stacks{i}", [SPLIT * HD1, 2 * HEADS * T + Q - REM], BF16) for i in range(2)]
        spill = [nc.dram_tensor(f"a_spill{i}", [PARTS, P, GROUPS * T], BF16).ap() for i in range(2)]
        v_main = [sb(f"a_v{i}", [P, HEADS, Q]) for i in range(2)]
        v_rem = [sb(f"a_vrem{i}", [P, GROUPS, P]) for i in range(2)]
        nmax = sb("a_nmax", [P, HEADS + GROUPS])
        nmax_parts = sb("a_nmax_parts", [P, 2, HEADS + GROUPS], BF16)
        nt = sb("a_nt", [41, HPG, T], BF16)
        prob = [sb(f"a_prob{i}", [P, HPG, T]) for i in range(2)]
        prob_rem = [sb(f"a_probrem{i}", [P, T]) for i in range(2)]
        ou = sb("a_ou", [P, GROUPS, T])
        z = sb("a_z", [P, GROUPS, T])
        lnz = sb("a_lnz", [P, GROUPS, T])
        rz = sb("a_rz", [P, GROUPS, T])
        ot = sb("a_ot", [P, GROUPS, T])
        h1 = [sb(f"a_h1{i}", [P, DT, T]) for i in range(2)]
        ps = ctx.enter_context(nc.psum_tensor("a_psum", [P, 8, 512], F32))
        sem = names(ctx, nc, "a", "weights const xload xs mean xc sq sqs var lnv rstd xn xnr res q qk c1 r1 c2 c3 spill0 spill1 spill2 stack "
                    "v vout vr vrout s max nm1 nm2 nmt nt st exp pv ou z lnz rz ot fc h1 store")
        heads = range(HPG)

        def stacked(p, which, h, a, b):
            at = ((h % HPG * 2 + which) * GROUPS + h // HPG) * T
            return stacks[p][:, at + a:at + b]

        def s_banks(g):
            return ps[:, 2 * (g % 2):2 * (g % 2) + 2, :]

        def st_banks(g):
            return ps[:, 2 + 2 * (g % 2):4 + 2 * (g % 2), :]

        def two_heads(banks):
            return banks[:, :, 0:2 * T]

        STACKS = 10
        OUT_BANK = (0, 1, 0, 6)

        def load_x(sp, n, q):
            text, patch = n * D, n * IMG_TOK
            need_all(sp, (sem["res"], n - 1), (sem["xload"], 32 * n))
            sp.dma_start(x[q][:, :, IMG_TOK:], dram["txt"][:, bass.ds(text, D)].rearrange("p (t j) -> p t j", t=DT)
                         ).then_inc(sem["xload"], 16)
            sp.dma_start(x[q][:, :, 0:IMG_TOK], embedded[:, :, bass.ds(patch, IMG_TOK)]).then_inc(sem["xload"], 16)

        def stack(sp, n, q):
            row, plane, src = GROUPS * T, P * GROUPS * T, spill[q]

            def write(part, made):
                if part == 0:
                    need_all(sp, (sem[made], 2 * n + 2), (sem["stack"], 16 * STACKS * (n - 1)))
                else:
                    sp.wait_ge(sem[made], 2 * n + 2)
                sp.dma_start(src[part], parts[part][:].rearrange("p a b j -> p (a b j)")).then_inc(sem[f"spill{part}"], 16)

            def read(slot, a, b):
                dst = stacks[q][slot * HD1:(slot + 1) * HD1, 0:2 * HEADS * T].rearrange("d (j w c) -> d j w c", w=2, j=HPG)
                if a == b:
                    sp.dma_start(dst.rearrange("d j w c -> d (j w) c"),
                                 bass.AP(tensor=src.tensor, offset=src.offset + a * plane,
                                         ap=[[row, HD1], [HD1 * row, 2 * HPG], [1, row]])).then_inc(sem["stack"], 16)
                else:
                    for w, part in enumerate((a, b)):
                        sp.dma_start(dst[:, :, w, :],
                                     bass.AP(tensor=src.tensor, offset=src.offset + part * plane + w * HD1 * row,
                                             ap=[[row, HD1], [Q * row, HPG], [1, row]])).then_inc(sem["stack"], 16)

            write(0, "c1")
            write(1, "c2")
            need_all(sp, (sem["spill0"], 16 * (n + 1)), (sem["st"], GROUPS * (n - 1)))
            read(0, 0, 0)
            write(2, "c3")
            sp.wait_ge(sem["spill1"], 16 * (n + 1))
            read(1, 0, 1)
            read(2, 1, 0)
            read(3, 1, 1)
            sp.wait_ge(sem["spill2"], 16 * (n + 1))
            read(4, 0, 2)
            read(5, 2, 0)

        def store_h1(sp, s, p):
            token = s * T
            need_all(sp, (sem["h1"], s + 1), (sem["store"], 16 * (s + 1)))
            sp.dma_start(h1_scratch[:, :, bass.ds(token, T)], h1[p][:]).then_inc(sem["store"], 16)

        def mean(pe, n):
            pe.wait_ge(sem["xs"], n + 1)
            need(pe, sem["nt"], n - 1)
            pe.matmul(ps[:, 7, 0:T], ones_avg[:], xs[:], start=True, stop=True).then_inc(sem["mean"], 1)

        def var(pe, n):
            pe.wait_ge(sem["sqs"], n + 1)
            pe.wait_ge(sem["xc"], n + 1)
            pe.matmul(ps[:, 7, 0:T], ones_avg[:], sqs[:], start=True, stop=True).then_inc(sem["var"], 1)

        def project_qk(pe, n, which):
            if which == 0:
                pe.wait_ge(sem["xn"], n + 1)
                need(pe, sem["exp"], GROUPS * (n - 1))
            for t in range(DT):
                for k in range(DT):
                    mm = pe.matmul(ps[:, 4 + which, t * T:(t + 1) * T], wqk[:, k, 2 * which + t, :], xn[:, k, :],
                                   start=(k == 0), stop=(k == DT - 1))
            mm.then_inc(sem["q"], 1)

        def project_v(pe, n):
            pe.wait_ge(sem["qk"], 2 * n + 1)
            for k in range(DT):
                mm = pe.matmul(ps[:, 4, 0:D], xn[:, k, 0:P], wv[:, k, :], start=(k == 0), stop=(k == DT - 1))
            mm.then_inc(sem["v"], 1)

        def project_v_rem(pe, n):
            pe.wait_ge(sem["qk"], 2 * n + 2)
            pe.wait_ge(sem["xnr"], n + 1)
            for k in range(DT):
                mm = pe.matmul(ps[:, 5, 0:D], xn_rem[:, k, :], wv[:, k, :],
                               start=(k == 0), stop=(k == DT - 1))
            mm.then_inc(sem["vr"], 1)

        def scores(pe, s, p, g):
            if g == 0:
                pe.wait_ge(sem["stack"], 16 * STACKS * (s + 1))
                need(pe, sem["ou"], GROUPS * s - 1)
            elif g == 1:
                need(pe, sem["exp"], GROUPS * (s - 1) + 3)
            else:
                need(pe, sem["max"], GROUPS * s + g - 1)
            b = s_banks(g)
            for j in heads:
                h = HPG * g + j
                pe.matmul(b[:, j // 2, (j % 2) * T:(j % 2 + 1) * T], stacked(p, 0, h, 0, P), stacked(p, 1, h, 0, T),
                          start=True, stop=True)
            for j in heads:
                h = HPG * g + j
                mm = pe.matmul(b[Q * j:Q * j + Q, 0, 2 * T:3 * T], stacked(p, 0, h, P, PAD_T), stacked(p, 1, h, 0, T),
                               start=True, stop=True)
            mm.then_inc(sem["s"], 1)

        def turn_max(pe, s, n_var):
            pe.wait_ge(sem["nm2"], s + 1)
            need(pe, sem["lnv"], n_var)
            pe.matmul(ps[0:40, 7, 0:P], nmax_parts[:].rearrange("p a c -> p (a c)"), ident[:],
                      start=True, stop=True).then_inc(sem["nmt"], 1)

        def scores_t(pe, s, p, g, v_read=None):
            if g == 0:
                pe.wait_ge(sem["nt"], s + 1)
                pe.wait_ge(sem["max"], GROUPS * s + 4)
            else:
                need(pe, sem["exp"], GROUPS * s + g - 1)
            if g == 1:
                pe.wait_ge(sem["vout"], v_read)
                pe.wait_ge(sem["vrout"], v_read)
            b = st_banks(g)
            for j in heads:
                h = HPG * g + j
                o = b[:, j // 2, (j % 2) * T:(j % 2 + 1) * T]
                pe.matmul(o, stacked(p, 1, h, 0, P), stacked(p, 0, h, 0, T), start=True, stop=False)
                pe.matmul(o, onehot[:, h, :], nt[0:40, j, :], start=False, stop=True)
            for j in heads:
                h = HPG * g + j
                o = b[Q * j:Q * j + Q, 0, 2 * T:3 * T]
                pe.matmul(o, stacked(p, 1, h, P, PAD_T), stacked(p, 0, h, 0, T), start=True, stop=False)
                mm = pe.matmul(o, onehot_rem[:, h, :], nt[:, j, :], start=False, stop=True)
            mm.then_inc(sem["st"], 1)

        def weigh(pe, s, p, g):
            pe.wait_ge(sem["exp"], GROUPS * s + g + 1)
            if g == 0:
                pe.wait_ge(sem["max"], GROUPS * s + 3)
            elif g == 2:
                pe.wait_ge(sem["ou"], GROUPS * s + 1)
            elif g == 3:
                need(pe, sem["h1"], s)
            b = ps[:, OUT_BANK[g], 0:T]
            pe.matmul(b, v_rem[p][:, g, :], prob_rem[g % 2][:], start=True, stop=False)
            for j in heads:
                mm = pe.matmul(b[Q * j:Q * j + Q], v_main[p][:, HPG * g + j, :], prob[g % 2][:, j, :],
                               start=False, stop=True)
            mm.then_inc(sem["pv"], 1)

        def fc(pe, s):
            pe.wait_ge(sem["ot"], s + 1)
            for t in range(DT):
                for g in range(GROUPS):
                    mm = pe.matmul(ps[:, 6, t * T:(t + 1) * T], fcw[:, g, t * P:(t + 1) * P], ot[:, g, :],
                                   start=(g == 0), stop=(g == GROUPS - 1))
            mm.then_inc(sem["fc"], 1)

        def centre(dve, n, q):
            dve.wait_ge(sem["mean"], n + 1)
            dve.tensor_tensor(xc[:], x[q][:], spread(ps[:, 7, 0:T], 1, DT), ALU.subtract).then_inc(sem["xc"], 1)

        def normalise(dve, n):
            dve.wait_ge(sem["rstd"], n + 1)
            need(dve, sem["vr"], n)
            need(dve, sem["res"], n)
            dve.tensor_tensor(xn[:], xc[:], spread(rstd[:], 1, DT), ALU.mult).then_inc(sem["xn"], 1)

        def v_out(dve, n, q):
            dve.wait_ge(sem["v"], n + 1)
            dve.tensor_tensor(v_main[q][:, :, 0:HD1], ps[:, 4, 0:D].rearrange("p (h d) -> p h d", d=HD1),
                              bv[:].rearrange("p (h d) -> p h d", d=HD1), ALU.add).then_inc(sem["vout"], 1)

        def v_rem_out(dve, n, q):
            dve.wait_ge(sem["vr"], n + 1)
            for j in heads:
                r = slice(Q * j, Q * j + Q)
                last = dve.scalar_tensor_tensor(
                    out=v_rem[q][r, :, Q * j:Q * j + HD1],
                    in0=ps[r, 5, 0:D].rearrange("p (g j d) -> p g j d", g=GROUPS, j=HPG)[:, :, j, :],
                    scalar=rem_mask[r, :],
                    in1=bv_rem[r, :].rearrange("p (g j d) -> p g j d", g=GROUPS, j=HPG)[:, :, j, :],
                    op0=ALU.mult, op1=ALU.add)
            last.then_inc(sem["vrout"], 1)

        def maxima(dve, s, g):
            dve.wait_ge(sem["s"], GROUPS * s + g + 1)
            b = s_banks(g)
            dve.tensor_reduce(nmax[:, HPG * g:HPG * g + HPG].rearrange("p (b j) -> p b j", b=2),
                              two_heads(b).rearrange("p b (j k) -> p b j k", j=2), AX.X, ALU.max, negate=True)
            dve.tensor_reduce(nmax[:, HEADS + g:HEADS + g + 1], b[:, 0, 2 * T:3 * T], AX.X, ALU.max,
                              negate=True).then_inc(sem["max"], 1)

        def split_max(dve, s):
            dve.wait_ge(sem["max"], GROUPS * (s + 1))
            dve.tensor_copy(nmax_parts[:, 0, :], nmax[:]).then_inc(sem["nm1"], 1)
            dve.wait_ge(sem["nm1"], s + 1)
            dve.tensor_tensor(nmax_parts[:, 1, :], nmax[:], nmax_parts[:, 0, :], ALU.subtract).then_inc(sem["nm2"], 1)

        def weighed_out(dve, s, g):
            if g > 0:
                dve.wait_ge(sem["ou"], GROUPS * s + g)
            dve.wait_ge(sem["pv"], GROUPS * s + g + 1)
            dve.tensor_copy(ou[:, g, :], ps[:, OUT_BANK[g], 0:T]).then_inc(sem["ou"], 1)

        def sums(dve, s, g):
            if g == GROUPS - 1:
                dve.wait_ge(sem["ou"], GROUPS * (s + 1))
                dve.memset(waited[:], 0.0)
            dve.stream_shuffle(z[:, g, :], ou[:, g, :], [HD1 + i % HD1 for i in range(Q)]).then_inc(sem["z"], 1)

        def residual(dve, s, p):
            dve.wait_ge(sem["fc"], s + 1)
            need(dve, sem["store"], 16 * (s + 1))
            dve.wait_ge(sem["res"], s + 1)
            for t in range(DT):
                last = dve.scalar_tensor_tensor(out=h1[p][:, t, :], in0=ps[:, 6, t * T:(t + 1) * T],
                                                scalar=fcb[:, t:t + 1], in1=res[p][:, t, :], op0=ALU.add, op1=ALU.add)
            last.then_inc(sem["h1"], 1)

        def square(act, n):
            act.wait_ge(sem["xc"], n + 1)
            act.activation(sq[:], xc[:], ACT.Square).then_inc(sem["sq"], 1)

        def inv_std(act, n):
            act.wait_ge(sem["var"], n + 1)
            act.activation(ln_var[:], ps[:, 7, 0:T], ACT.Ln, bias=eps[:]).then_inc(sem["lnv"], 1)
            act.wait_ge(sem["lnv"], n + 1)
            act.activation(rstd[:], ln_var[:], ACT.Exp, scale=-0.5).then_inc(sem["rstd"], 1)

        def repeat_last(act, n):
            act.wait_ge(sem["xn"], n + 1)
            act.activation(xn_rem[:].rearrange("p t (r j) -> p t r j", j=REM), spread(xn[:, :, P:T], 2, P // REM),
                           ACT.Copy).then_inc(sem["xnr"], 1)

        def qk_out(act, n, which):
            act.wait_ge(sem["q"], 2 * n + which + 1)
            need(act, sem["r1"], 2 * (n - 1) + which + 1)
            for t in range(DT):
                last = act.activation(qk[:, which, t, :], ps[:, 4 + which, t * T:(t + 1) * T], ACT.Identity,
                                      bias=bqk[:, 2 * which + t:2 * which + t + 1])
            last.then_inc(sem["qk"], 1)

        def first_part(act, n, which):
            act.wait_ge(sem["qk"], 2 * n + which + 1)
            need(act, sem["stack"], 16 * STACKS * n)
            act.activation(parts[0][:, which], qk[:, which], ACT.Copy).then_inc(sem["c1"], 1)

        def second_part(act, n, which):
            act.wait_ge(sem["r1"], 2 * n + which + 1)
            act.activation(parts[1][:, which], rest[:, which], ACT.Copy).then_inc(sem["c2"], 1)

        def max_rows(act, s):
            act.wait_ge(sem["nmt"], s + 1)
            act.activation(nt[0:40, :, 0:P], spread(ps[0:40, 7, 0:P], 1, HPG), ACT.Copy, scale=nt_rows[:, 0:1])
            act.activation(nt[0:40, :, P:T], ps[0:40, 7, 0:P].rearrange("p (j q) -> p j q", q=Q)[:, :, 0:REM],
                           ACT.Copy, scale=nt_rows[:, 1:2]).then_inc(sem["nt"], 1)

        def exps(act, s, g):
            act.wait_ge(sem["st"], GROUPS * s + g + 1)
            need(act, sem["pv"], GROUPS * s + g - 1)
            b = st_banks(g)
            act.activation(prob[g % 2][:].rearrange("p (b j) q -> p b (j q)", b=2), two_heads(b), ACT.Exp, scale=HD1 ** -0.5)
            act.activation(prob_rem[g % 2][:], b[:, 0, 2 * T:3 * T], ACT.Exp, scale=HD1 ** -0.5).then_inc(sem["exp"], 1)

        def inv_sums(act, s):
            act.wait_ge(sem["z"], GROUPS * (s + 1))
            act.activation(lnz[:], z[:], ACT.Ln).then_inc(sem["lnz"], 1)
            act.wait_ge(sem["lnz"], s + 1)
            act.activation(rz[:], lnz[:], ACT.Exp, scale=-1.0).then_inc(sem["rz"], 1)

        def add_tiles(pool, n, q):
            pool.wait_ge(sem["xload"], 32 * (n + 1))
            need(pool, sem["mean"], n)
            pool.tensor_tensor(xs[:], x[q][:, 0, :], x[q][:, 1, :], ALU.add).then_inc(sem["xs"], 1)

        def add_squares(pool, n):
            pool.wait_ge(sem["sq"], n + 1)
            pool.tensor_tensor(sqs[:], sq[:, 0, :], sq[:, 1, :], ALU.add).then_inc(sem["sqs"], 1)

        def add_norm(pool, n, q):
            pool.wait_ge(sem["xn"], n + 1)
            need(pool, sem["h1"], n - 1)
            pool.tensor_tensor(res[q][:], x[q][:], xn[:], ALU.add).then_inc(sem["res"], 1)

        def rest_one(pool, n, which):
            pool.wait_ge(sem["c1"], 2 * n + which + 1)
            pool.tensor_tensor(rest[:, which], qk[:, which], parts[0][:, which], ALU.subtract).then_inc(sem["r1"], 1)

        def third_part(pool, n, which):
            pool.wait_ge(sem["c2"], 2 * n + which + 1)
            pool.tensor_tensor(parts[2][:, which], rest[:, which], parts[1][:, which], ALU.subtract).then_inc(sem["c3"], 1)

        def divide(pool, s):
            pool.wait_ge(sem["rz"], s + 1)
            if isinstance(s, int):
                need(pool, sem["fc"], s)
            pool.tensor_tensor(ot[:], ou[:], rz[:], ALU.mult).then_inc(sem["ot"], 1)

        def each_step(engine, step):
            step(0, 0, True, True, True)
            if seqs > 4:
                with engine.Fori(0, (seqs - 4) // 2) as i:
                    step(i * 2 + 1, 1, False, True, True)
                    step(i * 2 + 2, 0, False, True, True)
            step(seqs - 3, 1, False, True, True)
            step(seqs - 2, 0, False, True, False)
            step(seqs - 1, 1, False, False, False)

        with nc.Block() as block:

            @block.sync
            def _(sp):
                for dst, name in ((wqk, "wqk"), (bqk, "bqk"), (wv, "wv"), (bv, "bv"), (fcw, "fcw"), (fcb, "fcb"),
                                  (rem_mask, "rem_mask"), (onehot_f, "onehot1"), (onehot_rem_f, "onehot1_rem"), (nt_rows, "nt_rows"), (ident_f, "ident")):
                    sp.dma_start(dst[:], dram[name]).then_inc(sem["weights"], 16)
                load_x(sp, 0, 0)
                load_x(sp, 1, 1)
                stack(sp, 0, 0)

                def step(s, p, first, has_next, has_norm):
                    if has_norm:
                        load_x(sp, s + 2, p)
                    if has_next:
                        stack(sp, s + 1, 1 - p)
                    if not first:
                        store_h1(sp, s - 1, 1 - p)
                each_step(sp, step)
                store_h1(sp, seqs - 1, 1)
                sp.wait_ge(sem["store"], 16 * (seqs + 1))

            @block.tensor
            def _(pe):
                pe.wait_ge(sem["weights"], 176)
                pe.wait_ge(sem["const"], 9)
                mean(pe, 0)
                var(pe, 0)
                project_qk(pe, 0, 0)
                project_qk(pe, 0, 1)
                project_v(pe, 0)
                project_v_rem(pe, 0)
                mean(pe, 1)
                var(pe, 1)

                def step(s, p, first, has_next, has_norm):
                    n, m = s + 1, s + 2
                    if has_next:
                        project_qk(pe, n, 0)
                    scores(pe, s, p, 0)
                    scores(pe, s, p, 1)
                    if has_next:
                        project_qk(pe, n, 1)
                    scores(pe, s, p, 2)
                    scores(pe, s, p, 3)
                    if has_next:
                        project_v(pe, n)
                        project_v_rem(pe, n)
                    turn_max(pe, s, m if has_next else n)
                    if not first:
                        fc(pe, s - 1)
                    scores_t(pe, s, p, 0)
                    if has_norm:
                        mean(pe, m)
                    scores_t(pe, s, p, 1, m if has_next else n)
                    weigh(pe, s, p, 0)
                    scores_t(pe, s, p, 2)
                    if has_norm:
                        var(pe, m)
                    weigh(pe, s, p, 1)
                    scores_t(pe, s, p, 3)
                    weigh(pe, s, p, 2)
                    weigh(pe, s, p, 3)
                each_step(pe, step)
                fc(pe, seqs - 1)

            @block.vector
            def _(dve):
                dve.memset(ones_avg[:], 1.0 / D).then_inc(sem["const"], 1)
                for i in range(2):
                    dve.memset(v_main[i][:, :, HD1:], 1.0).then_inc(sem["const"], 1)
                dve.memset(eps[:], EPS).then_inc(sem["const"], 1)
                dve.memset(waited[:], 0.0).then_inc(sem["store"], 16)
                for i in range(2):
                    dve.memset(stacks[i][:, 2 * HEADS * T:], 0.0)
                dve.memset(nt[Q:], 1.0)
                dve.memset(nt[0:Q], 0.0).then_inc(sem["const"], 1)
                dve.wait_ge(sem["weights"], 176)
                dve.tensor_copy(ident[:], ident_f[:]).then_inc(sem["const"], 1)
                dve.tensor_copy(onehot[:], onehot_f[:]).then_inc(sem["const"], 1)
                dve.tensor_scalar(bv_rem[:], bv[:], rem_mask[:, 0:1], None, ALU.mult).then_inc(sem["const"], 1)
                dve.wait_ge(sem["const"], 8)
                dve.tensor_copy(onehot_rem[:], onehot_rem_f[:]).then_inc(sem["const"], 1)
                centre(dve, 0, 0)
                normalise(dve, 0)
                v_out(dve, 0, 0)
                for i in range(2):
                    dve.memset(v_rem[i][:], 0.0).then_inc(sem["const"], 1)
                dve.wait_ge(sem["const"], 11)
                for i in range(2):
                    for j in heads:
                        r = slice(Q * j, Q * j + Q)
                        last = dve.tensor_copy(v_rem[i][r, :, Q * j + HD1:Q * j + Q],
                                               spread(spread(rem_mask[r, 0], 1, GROUPS), 2, HD1))
                last.then_inc(sem["const"], 1)
                v_rem_out(dve, 0, 0)
                centre(dve, 1, 1)
                normalise(dve, 1)

                def step(s, p, first, has_next, has_norm):
                    n, m = s + 1, s + 2
                    if not first:
                        sums(dve, s - 1, GROUPS - 1)
                    maxima(dve, s, 0)
                    maxima(dve, s, 1)
                    maxima(dve, s, 2)
                    maxima(dve, s, 3)
                    split_max(dve, s)
                    if has_next:
                        v_out(dve, n, 1 - p)
                        v_rem_out(dve, n, 1 - p)
                    if not first:
                        residual(dve, s - 1, 1 - p)
                    if has_norm:
                        centre(dve, m, p)
                    weighed_out(dve, s, 0)
                    for g in range(1, GROUPS):
                        if g == 2 and has_norm:
                            normalise(dve, m)
                        weighed_out(dve, s, g)
                        sums(dve, s, g - 1)
                each_step(dve, step)
                sums(dve, seqs - 1, GROUPS - 1)
                residual(dve, seqs - 1, 1)

            @block.scalar
            def _(act):
                act.preload_act_table_set("natural_log_exp_and_others")
                act.wait_ge(sem["const"], 9)
                square(act, 0)
                inv_std(act, 0)
                repeat_last(act, 0)
                for which in range(2):
                    qk_out(act, 0, which)
                    first_part(act, 0, which)
                    second_part(act, 0, which)
                square(act, 1)
                inv_std(act, 1)
                repeat_last(act, 1)

                def step(s, p, first, has_next, has_norm):
                    n, m = s + 1, s + 2
                    if not first:
                        inv_sums(act, s - 1)
                    if has_next:
                        qk_out(act, n, 0)
                        first_part(act, n, 0)
                        qk_out(act, n, 1)
                        first_part(act, n, 1)
                        second_part(act, n, 0)
                        second_part(act, n, 1)
                    max_rows(act, s)
                    exps(act, s, 0)
                    if has_norm:
                        square(act, m)
                    exps(act, s, 1)
                    exps(act, s, 2)
                    if has_norm:
                        inv_std(act, m)
                    exps(act, s, 3)
                    if has_norm:
                        repeat_last(act, m)
                each_step(act, step)
                inv_sums(act, seqs - 1)

            @block.gpsimd
            def _(pool):
                add_tiles(pool, 0, 0)
                add_squares(pool, 0)
                add_norm(pool, 0, 0)
                for which in range(2):
                    rest_one(pool, 0, which)
                for which in range(2):
                    third_part(pool, 0, which)
                add_tiles(pool, 1, 1)
                add_squares(pool, 1)

                def step(s, p, first, has_next, has_norm):
                    n, m = s + 1, s + 2
                    if not first:
                        divide(pool, s - 1)
                    if has_norm:
                        add_tiles(pool, m, p)
                    if has_next:
                        rest_one(pool, n, 0)
                        rest_one(pool, n, 1)
                        third_part(pool, n, 0)
                        third_part(pool, n, 1)
                        add_norm(pool, n, 1 - p)
                    if has_norm:
                        add_squares(pool, m)
                each_step(pool, step)
                divide(pool, seqs - 1)


def attn2_phase(nc, dram, h1_scratch, x2_scratch, seqs):
    with ExitStack() as ctx:
        sb = lambda name, shape, dt=F32: ctx.enter_context(nc.sbuf_tensor(name, shape, dt))
        RT = HPG + 1
        wqn_t = sb("b_wqn_t", [P, GROUPS, D])
        wkb_t = sb("b_wkb_t", [P, GROUPS, LAT])
        wo_n = sb("b_wo_n", [P, GROUPS, D])
        wq_nope = sb("b_wq_nope", [P, DT, GROUPS, P])
        wo = sb("b_wo", [P, GROUPS, D])
        wq_rope = sb("b_wq_rope", [P, DT, GROUPS, P])
        wkva = sb("b_wkva", [P, DT, P])
        w_ln = sb("b_w_ln", [P, DT])
        rope_cos = sb("b_rope_cos", [P, RT, T])
        rope_sin = sb("b_rope_sin", [P, RT, T])
        ones_avg = sb("b_ones_avg", [P, P])
        ones = sb("b_ones", [P, Q])
        eps = sb("b_eps", [P, 1])
        waited = sb("b_waited", [1, 1])
        masks_f = sb("b_masks_f", [P, 2 * P + T + REM])
        masks = sb("b_masks", [P, 2 * P + T + REM], BF16)
        mask_main, mask_main_t = masks[:, 0:P], masks[:, P:2 * P]
        mask_rem, mask_rem_t = masks[:, 2 * P:2 * P + T], masks[0:REM, 2 * P + T:]
        ident_f = sb("b_ident_f", [P, P])
        ident = sb("b_ident", [P, P], BF16)
        onehot_f = sb("b_onehot_f", [40, HEADS + GROUPS, P])
        onehot = sb("b_onehot", [40, HEADS + GROUPS, P], BF16)
        x = [sb(f"b_x{i}", [P, DT, T]) for i in range(2)]
        xs = sb("b_xs", [P, T])
        xc = sb("b_xc", [P, DT, T])
        sq = sb("b_sq", [P, DT, T])
        sqs = sb("b_sqs", [P, T])
        ln_var = sb("b_ln_var", [P, T])
        rstd = sb("b_rstd", [P, T])
        norm_a = sb("b_norm_a", [P, T])
        norm_b = sb("b_norm_b", [P, T])
        ln_rms = sb("b_ln_rms", [P, T])
        inv_rms = sb("b_inv_rms", [P, T])
        both = sb("b_both", [P, T])
        x1 = [sb(f"b_x1{i}", [P, DT, T]) for i in range(2)]
        xr = sb("b_xr", [P, DT, T])
        nope_b = sb("b_nope_b", [P, GROUPS, T], BF16)
        nope = [sb(f"b_nope{i}", [P, GROUPS, T], F32R) for i in range(2)]
        raw = sb("b_raw", [P, RT, T])
        swapped = sb("b_swapped", [P, RT, T])
        with_cos = sb("b_with_cos", [P, RT, T])
        with_sin = sb("b_with_sin", [P, RT, T])
        roped = [sb(f"b_roped{i}", [P, RT, T]) for i in range(2)]
        roped_b = [sb(f"b_roped_b{i}", [P, RT, T], BF16) for i in range(2)]
        keys_b = [sb(f"b_keys_b{i}", [P, T], BF16) for i in range(2)]
        roped_hi = [sb(f"b_roped_hi{i}", [P, RT, T], F32R) for i in range(2)]
        roped_lo = [sb(f"b_roped_lo{i}", [P, RT, T], F32R) for i in range(2)]
        stacks = [sb(f"b_stacks{i}", [P, HEADS * T + Q - REM], F32R) for i in range(2)]
        stack_b = sb("b_stack_b", [P, GROUPS, HPG * T + Q - REM], BF16)
        v_main = [sb(f"b_v{i}", [P, LAT]) for i in range(2)]
        v_rem = [sb(f"b_vrem{i}", [REM, LAT]) for i in range(2)]
        nmax = sb("b_nmax", [P, HEADS + GROUPS])
        nmax_parts = sb("b_nmax_parts", [P, 2, HEADS + GROUPS], BF16)
        nt = sb("b_nt", [40, P], BF16)
        prob = [sb(f"b_prob{i}", [P, HPG, P]) for i in range(2)]
        prob_q = sb("b_prob_q", [P, GROUPS, HPG, REM])
        prob_qq = sb("b_prob_qq", [REM, GROUPS, HPG, REM])
        ouz = sb("b_ouz", [P, 2, GROUPS, T])
        lnz = sb("b_lnz", [P, GROUPS, T])
        rz = sb("b_rz", [P, GROUPS, T])
        ot = sb("b_ot", [P, GROUPS, T])
        x2 = [sb(f"b_x2{i}", [P, DT, T]) for i in range(2)]
        ps = ctx.enter_context(nc.psum_tensor("b_psum", [P, 8, 512], F32))
        sem = names(ctx, nc, "b", "weights const absorb absorbed xload xs mean xc sq sqs var lnv rstd na nb lnr ir both x1 xr "
                    "qn qr qnh qnl raw cos swap sin rope rope_b rhi rlo kb stack cast nope_b v vout "
                    "s max nm1 nm2 nmt nt st exp expr_in expr pv pvr ou oz lnz rz ot wo x2 store")
        members = range(HPG)

        def place_b(G, m, a, b):
            return stack_b[:, G, m * T + a:m * T + b]

        def places(p):
            return stacks[p][:, 0:HEADS * T].rearrange("p (h j) -> p h j", j=T)

        def load_x(sp, n, q):
            token = n * T
            need_all(sp, (sem["xc"], n - 1), (sem["xload"], 16 * n))
            sp.dma_start(x[q][:], h1_scratch[:, :, bass.ds(token, T)]).then_inc(sem["xload"], 16)

        def stack(sp, n, q):
            for slot, (made, src) in enumerate((("qnh", nope[0]), ("rhi", roped_hi[q]), ("qnl", nope[1]), ("rlo", roped_lo[q]))):
                if slot == 0:
                    need_all(sp, (sem["expr_in"], n - 1), (sem["st"], GROUPS * (n - 1)), (sem[made], n + 1))
                else:
                    sp.wait_ge(sem[made], n + 1)
                for j in range(HPG):
                    sp.dma_start(stacks[q][Q * slot:Q * slot + Q, j * GROUPS * T:(j + 1) * GROUPS * T].bitcast(F32),
                                 src[Q * j:Q * j + Q, 0:GROUPS, :].rearrange("p g j -> p (g j)").bitcast(F32)).then_inc(sem["stack"], 16)

        def store_x2(sp, s, p):
            token = s * T
            need_all(sp, (sem["x2"], s + 1), (sem["store"], 16 * (s + 1)))
            sp.dma_start(x2_scratch[:, :, bass.ds(token, T)], x2[p][:]).then_inc(sem["store"], 16)

        def mean(pe, n):
            pe.wait_ge(sem["xs"], n + 1)
            need(pe, sem["nt"], n - 1)
            pe.matmul(ps[:, 6, 0:T], ones_avg[:], xs[:], start=True, stop=True).then_inc(sem["mean"], 1)

        def var(pe, n):
            pe.wait_ge(sem["sqs"], n + 1)
            pe.wait_ge(sem["xc"], n + 1)
            pe.matmul(ps[:, 6, 0:T], ones_avg[:], sqs[:], start=True, stop=True).then_inc(sem["var"], 1)

        def project_nope(pe, n):
            pe.wait_ge(sem["raw"], n + 1)
            for g in range(GROUPS):
                for k in range(DT):
                    mm = pe.matmul(ps[:, 4 + g // 2, (g % 2) * T:(g % 2 + 1) * T], wq_nope[:, k, g, :], xr[:, k, :],
                                   start=(k == 0), stop=(k == DT - 1))
            mm.then_inc(sem["qn"], 1)

        def project_rope(pe, n):
            pe.wait_ge(sem["xr"], n + 1)
            need(pe, sem["exp"], GROUPS * (n - 1))
            for g in range(RT):
                for k in range(DT):
                    w = wq_rope[:, k, g, :] if g < GROUPS else wkva[:, k, :]
                    mm = pe.matmul(ps[:, 4 + g // 3, (g % 3) * T:(g % 3 + 1) * T], w, xr[:, k, :],
                                   start=(k == 0), stop=(k == DT - 1))
            mm.then_inc(sem["qr"], 1)

        def project_v(pe, n):
            pe.wait_ge(sem["qnl"], n + 1)
            for k in range(DT):
                pe.matmul(ps[:, 4, 0:LAT], xr[:, k, 0:P], wkva[:, k, 0:LAT], start=(k == 0), stop=(k == DT - 1))
            for k in range(DT):
                mm = pe.matmul(ps[0:REM, 4, LAT:2 * LAT], xr[:, k, P:T], wkva[:, k, 0:LAT], start=(k == 0), stop=(k == DT - 1))
            mm.then_inc(sem["v"], 1)

        def scores(pe, s, p, G):
            pe.wait_ge(sem["cast"], GROUPS * s + G + 1)
            if G == 0:
                pe.wait_ge(sem["kb"], s + 1)
                need(pe, sem["ou"], GROUPS * s - 1)
            elif G == 1:
                need(pe, sem["ou"], GROUPS * s)
            else:
                need(pe, sem["max"], GROUPS * s + G - 1)
            b, br = ps[:, G % 2, :], ps[:, 2 + G % 2, 0:T]
            keys = roped_b[p][:, GROUPS, :], keys_b[p][:]
            pe.matmul(b, ident[:], spread(mask_main, 1, HPG), start=True, stop=False)
            for m in members:
                for i in range(2):
                    pe.matmul(b[:, m * P:(m + 1) * P], place_b(G, m, 0, P), keys[i][:, 0:P], start=False,
                              stop=(m == HPG - 1 and i == 1))
            pe.matmul(br, ident[:], mask_rem, start=True, stop=False)
            for m in members:
                for i in range(2):
                    mm = pe.matmul(br[Q * m:Q * m + Q], place_b(G, m, P, PAD_T), keys[i], start=False, stop=(i == 1))
            mm.then_inc(sem["s"], 1)

        def turn_max(pe, s, n_var):
            pe.wait_ge(sem["nm2"], s + 1)
            need(pe, sem["nb"], n_var)
            pe.matmul(ps[0:40, 6, 0:P], nmax_parts[:].rearrange("p a c -> p (a c)"), ident[:],
                      start=True, stop=True).then_inc(sem["nmt"], 1)

        def scores_t(pe, s, p, G, v_read=None):
            if G == 0:
                pe.wait_ge(sem["vout"], v_read)
            need(pe, sem["exp"], GROUPS * s + G - 1)
            b = ps[:, 4 + G % 2, :]
            q = places(p)[:, HPG * G:HPG * G + HPG, 0:P]
            pe.matmul(b, ident[:], spread(mask_main_t, 1, HPG), start=True, stop=False)
            pe.matmul(b, roped_hi[p][:, GROUPS, 0:P], q, start=False, stop=False)
            pe.matmul(b, roped_lo[p][:, GROUPS, 0:P], q, start=False, stop=False)
            if G == 0:
                pe.wait_ge(sem["nt"], s + 1)
            for m in members:
                mm = pe.matmul(b[:, m * P:(m + 1) * P], onehot[:, HPG * G + m, :], nt[:], start=False, stop=(m == HPG - 1))
            mm.then_inc(sem["st"], 1)

        def scores_t_rem(pe, s, p, n_var):
            pe.wait_ge(sem["nt"], s + 1)
            pe.wait_ge(sem["nb"], n_var)
            b, bb = ps[:, 6, 0:2 * P], ps[0:REM, 6, 2 * P:4 * P]
            q = places(p)[:, :, P:T]
            rem_max = nt[:].rearrange("r (m q) -> r m q", q=Q)[:, :, 0:REM]
            w = HPG * REM
            pe.matmul(b, roped_hi[p][:, GROUPS, 0:P], q, start=True, stop=False)
            pe.matmul(b, roped_lo[p][:, GROUPS, 0:P], q, start=False, stop=False)
            for G in range(GROUPS):
                pe.matmul(b[:, G * w:(G + 1) * w], onehot[:, HEADS + G, :], rem_max, start=False, stop=(G == GROUPS - 1))
            pe.matmul(bb, roped[p][:, GROUPS, P:T], q.bitcast(F32), start=True, stop=False)
            pe.matmul(bb, ident[0:REM, 0:REM], spread(mask_rem_t, 1, HEADS), start=False, stop=False)
            for G in range(GROUPS):
                mm = pe.matmul(bb[:, G * w:(G + 1) * w], onehot[:, HEADS + G, 0:REM], rem_max, start=False, stop=(G == GROUPS - 1))
            mm.then_inc(sem["expr_in"], 1)

        def weigh(pe, s, p, G):
            pe.wait_ge(sem["exp"], GROUPS * s + G + 1)
            for m in members:
                pe.matmul(ps[Q * m:Q * m + Q, G, 0:P], v_main[p][:], prob[G % 2][:, m, :], start=True, stop=True)
            for m in members:
                mm = pe.matmul(ps[Q * m:Q * m + Q, G, P:2 * P], ones[:], prob[G % 2][:, m, :], start=True, stop=True)
            mm.then_inc(sem["pv"], 1)

        def weigh_rem(pe, s, p):
            pe.wait_ge(sem["expr"], s + 1)
            need(pe, sem["x2"], s)
            for m in members:
                for i, (v, vr) in enumerate(((v_main[p][:], v_rem[p][:]), (ones[:], ones[0:REM, :]))):
                    o = ps[Q * m:Q * m + Q, 7, i * HPG * REM:(i + 1) * HPG * REM]
                    pe.matmul(o, v, prob_q[:, :, m, :], start=True, stop=False)
                    mm = pe.matmul(o, vr, prob_qq[:, :, m, :], start=False, stop=True)
            mm.then_inc(sem["pvr"], 1)

        def project_out(pe, s):
            pe.wait_ge(sem["ot"], s + 1)
            pe.wait_ge(sem["oz"], s + 1)
            for t in range(DT):
                for G in range(GROUPS):
                    mm = pe.matmul(ps[:, 7, t * T:(t + 1) * T], wo[:, G, t * P:(t + 1) * P], ot[:, G, :],
                                   start=(G == 0), stop=(G == GROUPS - 1))
            mm.then_inc(sem["wo"], 1)

        def centre(dve, n, q):
            dve.wait_ge(sem["mean"], n + 1)
            need(dve, sem["x1"], n)
            dve.tensor_tensor(xc[:], x[q][:], spread(ps[:, 6, 0:T], 1, DT), ALU.subtract).then_inc(sem["xc"], 1)

        def rms_terms(dve, n):
            dve.wait_ge(sem["rstd"], n + 1)
            dve.tensor_tensor(norm_a[:], rstd[:], ps[:, 6, 0:T], ALU.mult).then_inc(sem["na"], 1)
            dve.wait_ge(sem["na"], n + 1)
            dve.tensor_tensor(norm_b[:], norm_a[:], rstd[:], ALU.mult).then_inc(sem["nb"], 1)

        def rms_norm(dve, n):
            dve.wait_ge(sem["ir"], n + 1)
            dve.tensor_tensor(both[:], rstd[:], inv_rms[:], ALU.mult).then_inc(sem["both"], 1)
            dve.wait_ge(sem["both"], n + 1)
            need(dve, sem["v"], n)
            for t in range(DT):
                last = dve.scalar_tensor_tensor(out=xr[:, t, :], in0=xc[:, t, :], scalar=w_ln[:, t:t + 1], in1=both[:],
                                                op0=ALU.mult, op1=ALU.mult)
            last.then_inc(sem["xr"], 1)

        def nope_low(dve, n):
            dve.wait_ge(sem["nope_b"], n + 1)
            for c in range(2):
                last = dve.tensor_tensor(nope[1][:, 2 * c:2 * c + 2, :], ps[:, 4 + c, 0:2 * T].rearrange("p (g j) -> p g j", g=2),
                                         nope_b[:, 2 * c:2 * c + 2, :], ALU.subtract)
            last.then_inc(sem["qnl"], 1)

        def turn(dve, n):
            dve.wait_ge(sem["raw"], n + 1)
            dve.memset(waited[:], 0.0)
            dve.stream_shuffle(swapped[:].rearrange("p a b -> p (a b)"), raw[:].rearrange("p a b -> p (a b)"),
                               [i ^ 1 for i in range(Q)]).then_inc(sem["swap"], 1)
            dve.wait_ge(sem["swap"], n + 1)
            dve.tensor_tensor(with_sin[:], swapped[:], rope_sin[:], ALU.mult).then_inc(sem["sin"], 1)

        def rotate(dve, n, q):
            dve.wait_ge(sem["sin"], n + 1)
            dve.wait_ge(sem["cos"], n + 1)
            dve.tensor_tensor(roped[q][:], with_sin[:], with_cos[:], ALU.add).then_inc(sem["rope"], 1)

        def v_out(dve, n, q):
            dve.wait_ge(sem["v"], n + 1)
            dve.tensor_copy(v_main[q][:], ps[:, 4, 0:LAT])
            dve.tensor_copy(v_rem[q][:], ps[0:REM, 4, LAT:2 * LAT]).then_inc(sem["vout"], 1)

        def maxima(dve, s, G):
            dve.wait_ge(sem["s"], GROUPS * s + G + 1)
            dve.tensor_reduce(nmax[:, HPG * G:HPG * G + HPG], ps[:, G % 2, :].rearrange("p (m k) -> p m k", m=HPG),
                              AX.X, ALU.max, negate=True)
            dve.tensor_reduce(nmax[:, HEADS + G:HEADS + G + 1], ps[:, 2 + G % 2, 0:T], AX.X, ALU.max,
                              negate=True).then_inc(sem["max"], 1)

        def split_max(dve, s):
            dve.wait_ge(sem["max"], GROUPS * (s + 1))
            dve.tensor_copy(nmax_parts[:, 0, :], nmax[:]).then_inc(sem["nm1"], 1)
            dve.wait_ge(sem["nm1"], s + 1)
            dve.tensor_tensor(nmax_parts[:, 1, :], nmax[:], nmax_parts[:, 0, :], ALU.subtract).then_inc(sem["nm2"], 1)

        def weighed_out(dve, s, G):
            dve.wait_ge(sem["pv"], GROUPS * s + G + 1)
            if G == 0:
                need(dve, sem["ot"], s)
            dve.tensor_copy(ouz[:, :, G, 0:P], ps[:, G, 0:2 * P].rearrange("p (a q) -> p a q", a=2)).then_inc(sem["ou"], 1)

        def weighed_rem_out(dve, s):
            dve.wait_ge(sem["pvr"], s + 1)
            w = HPG * REM
            for i in range(2):
                last = dve.tensor_copy(ouz[:, i, :, P:T], ps[:, 7, i * w:(i + 1) * w].rearrange("p (g q) -> p g q", q=REM))
            last.then_inc(sem["oz"], 1)

        def residual(dve, s, p):
            dve.wait_ge(sem["wo"], s + 1)
            need(dve, sem["store"], 16 * (s + 1))
            dve.wait_ge(sem["x1"], s + 1)
            dve.tensor_tensor(x2[p][:], ps[:, 7, 0:2 * T].rearrange("p (t j) -> p t j", t=DT), x1[p][:],
                              ALU.add).then_inc(sem["x2"], 1)

        def square(act, n):
            act.wait_ge(sem["xc"], n + 1)
            act.activation(sq[:], xc[:], ACT.Square).then_inc(sem["sq"], 1)

        def inv_std(act, n):
            act.wait_ge(sem["var"], n + 1)
            act.activation(ln_var[:], ps[:, 6, 0:T], ACT.Ln, bias=eps[:]).then_inc(sem["lnv"], 1)
            act.wait_ge(sem["lnv"], n + 1)
            act.activation(rstd[:], ln_var[:], ACT.Exp, scale=-0.5).then_inc(sem["rstd"], 1)

        def inv_mean_square(act, n):
            act.wait_ge(sem["nb"], n + 1)
            act.activation(ln_rms[:], norm_b[:], ACT.Ln, bias=eps[:]).then_inc(sem["lnr"], 1)
            act.wait_ge(sem["lnr"], n + 1)
            act.activation(inv_rms[:], ln_rms[:], ACT.Exp, scale=-0.5).then_inc(sem["ir"], 1)

        def nope_high(act, n):
            act.wait_ge(sem["qn"], n + 1)
            need(act, sem["stack"], 16 * 16 * n)
            for c in range(2):
                last = act.activation(nope_b[:, 2 * c:2 * c + 2, :], ps[:, 4 + c, 0:2 * T].rearrange("p (g j) -> p g j", g=2), ACT.Copy)
            last.then_inc(sem["nope_b"], 1)
            act.wait_ge(sem["nope_b"], n + 1)
            act.activation(nope[0][:], nope_b[:], ACT.Copy).then_inc(sem["qnh"], 1)

        def rope_raw(act, n):
            act.wait_ge(sem["qr"], n + 1)
            act.activation(raw[:, 0:3, :], ps[:, 4, 0:3 * T].rearrange("p (g j) -> p g j", g=3), ACT.Copy)
            act.activation(raw[:, 3:5, :], ps[:, 5, 0:2 * T].rearrange("p (g j) -> p g j", g=2), ACT.Copy).then_inc(sem["raw"], 1)

        def rope_short(act, n, q):
            act.wait_ge(sem["rope"], n + 1)
            act.activation(roped_b[q][:], roped[q][:], ACT.Copy).then_inc(sem["rope_b"], 1)

        def rope_high(act, n, q):
            act.wait_ge(sem["rope_b"], n + 1)
            act.activation(roped_hi[q][:], roped_b[q][:], ACT.Copy).then_inc(sem["rhi"], 1)

        def cast(act, s, p, G):
            if G == 0:
                act.wait_ge(sem["stack"], 16 * 16 * (s + 1))
                need(act, sem["s"], GROUPS * s)
            c = slice(G * HPG * T, (G + 1) * HPG * T + Q - REM)
            act.activation(stack_b[:, G], stacks[p][:, c].bitcast(F32), ACT.Copy).then_inc(sem["cast"], 1)

        def max_rows(act, s):
            act.wait_ge(sem["nmt"], s + 1)
            act.activation(nt[:], ps[0:40, 6, 0:P], ACT.Copy).then_inc(sem["nt"], 1)

        def exps(act, s, G):
            act.wait_ge(sem["st"], GROUPS * s + G + 1)
            need(act, sem["pv"], GROUPS * s + G - 1)
            act.activation(prob[G % 2][:], ps[:, 4 + G % 2, :].rearrange("p (m q) -> p m q", m=HPG), ACT.Exp,
                           scale=0.125).then_inc(sem["exp"], 1)

        def exps_rem(act, s):
            act.wait_ge(sem["expr_in"], s + 1)
            act.activation(prob_q[:].rearrange("p a b q -> p (a b q)"), ps[:, 6, 0:2 * P], ACT.Exp, scale=0.125)
            act.activation(prob_qq[:].rearrange("p a b q -> p (a b q)"), ps[0:REM, 6, 2 * P:4 * P], ACT.Exp,
                           scale=0.125).then_inc(sem["expr"], 1)

        def inv_sums(act, s):
            act.wait_ge(sem["oz"], s + 1)
            act.activation(lnz[:], ouz[:, 1], ACT.Ln).then_inc(sem["lnz"], 1)
            act.wait_ge(sem["lnz"], s + 1)
            act.activation(rz[:], lnz[:], ACT.Exp, scale=-1.0).then_inc(sem["rz"], 1)

        def add_tiles(pool, n, q):
            pool.wait_ge(sem["xload"], 16 * (n + 1))
            need(pool, sem["mean"], n)
            pool.tensor_tensor(xs[:], x[q][:, 0, :], x[q][:, 1, :], ALU.add).then_inc(sem["xs"], 1)

        def add_squares(pool, n):
            pool.wait_ge(sem["sq"], n + 1)
            pool.tensor_tensor(sqs[:], sq[:, 0, :], sq[:, 1, :], ALU.add).then_inc(sem["sqs"], 1)

        def layer_norm(pool, n, q):
            pool.wait_ge(sem["rstd"], n + 1)
            need(pool, sem["x2"], n - 1)
            pool.tensor_tensor(x1[q][:], xc[:], spread(rstd[:], 1, DT), ALU.mult).then_inc(sem["x1"], 1)

        def times_cos(pool, n):
            pool.wait_ge(sem["raw"], n + 1)
            pool.tensor_tensor(with_cos[:], raw[:], rope_cos[:], ALU.mult).then_inc(sem["cos"], 1)

        def rope_low(pool, n, q):
            pool.wait_ge(sem["rope_b"], n + 1)
            need(pool, sem["st"], GROUPS * (n - 1))
            pool.tensor_tensor(roped_lo[q][:], roped[q][:], roped_b[q][:], ALU.subtract).then_inc(sem["rlo"], 1)

        def keys_low(pool, n, q):
            pool.wait_ge(sem["rope_b"], n + 1)
            pool.tensor_tensor(keys_b[q][:], roped[q][:, GROUPS, :], roped_b[q][:, GROUPS, :], ALU.subtract).then_inc(sem["kb"], 1)

        def divide(pool, s):
            pool.wait_ge(sem["rz"], s + 1)
            if isinstance(s, int):
                need(pool, sem["wo"], s)
            pool.tensor_tensor(ot[:], ouz[:, 0], rz[:], ALU.mult).then_inc(sem["ot"], 1)

        def each_step(engine, step):
            step(0, 0, True, True, True)
            if seqs > 4:
                with engine.Fori(0, (seqs - 4) // 2) as i:
                    step(i * 2 + 1, 1, False, True, True)
                    step(i * 2 + 2, 0, False, True, True)
            step(seqs - 3, 1, False, True, True)
            step(seqs - 2, 0, False, True, False)
            step(seqs - 1, 1, False, False, False)

        with nc.Block() as block:

            @block.sync
            def _(sp):
                for dst, name in ((wqn_t, "wqn_t"), (wkb_t, "wkb_t"), (wo_n, "wo_n"), (wq_rope, "wq_rope"), (wkva, "wkva"),
                                  (w_ln, "w_ln1"), (rope_cos, "rope_cos"), (rope_sin, "rope_sin"), (masks_f, "masks"),
                                  (ident_f, "ident"), (onehot_f, "onehot2")):
                    sp.dma_start(dst[:], dram[name]).then_inc(sem["weights"], 16)
                load_x(sp, 0, 0)
                load_x(sp, 1, 1)
                stack(sp, 0, 0)

                def step(s, p, first, has_next, has_norm):
                    if has_norm:
                        load_x(sp, s + 2, p)
                    if has_next:
                        stack(sp, s + 1, 1 - p)
                    if not first:
                        store_x2(sp, s - 1, 1 - p)
                each_step(sp, step)
                store_x2(sp, seqs - 1, 1)
                sp.wait_ge(sem["store"], 16 * (seqs + 1))

            @block.tensor
            def _(pe):
                pe.wait_ge(sem["weights"], 176)
                for j in range(HPG):
                    for t in range(DT):
                        for g in range(GROUPS):
                            r = slice(Q * j, Q * j + Q)
                            pe.matmul(ps[:, j, (t * GROUPS + g) * LAT:(t * GROUPS + g + 1) * LAT],
                                      wqn_t[r, g, t * P:(t + 1) * P], wkb_t[r, g, :], start=True, stop=True)
                for j in range(HPG):
                    for g in range(GROUPS):
                        r = slice(Q * j, Q * j + Q)
                        mm = pe.matmul(ps[Q * g:Q * g + Q, 4 + j, 0:D], wkb_t[r, g, :], wo_n[r, g, :], start=True, stop=True)
                mm.then_inc(sem["absorb"], 1)
                pe.wait_ge(sem["absorbed"], 2)
                pe.wait_ge(sem["const"], 6)
                mean(pe, 0)
                var(pe, 0)
                project_rope(pe, 0)
                project_nope(pe, 0)
                project_v(pe, 0)
                mean(pe, 1)
                var(pe, 1)

                def step(s, p, first, has_next, has_norm):
                    n, m = s + 1, s + 2
                    if has_next:
                        project_rope(pe, n)
                    scores(pe, s, p, 0)
                    if has_next:
                        project_nope(pe, n)
                    scores(pe, s, p, 1)
                    scores(pe, s, p, 2)
                    scores(pe, s, p, 3)
                    if has_next:
                        project_v(pe, n)
                    if not first:
                        project_out(pe, s - 1)
                    turn_max(pe, s, m if has_next else n)
                    scores_t(pe, s, p, 0, m if has_next else n)
                    if has_norm:
                        mean(pe, m)
                    scores_t(pe, s, p, 1)
                    weigh(pe, s, p, 0)
                    scores_t(pe, s, p, 2)
                    if has_norm:
                        var(pe, m)
                    weigh(pe, s, p, 1)
                    scores_t(pe, s, p, 3)
                    scores_t_rem(pe, s, p, s + 3 if has_norm else seqs)
                    weigh(pe, s, p, 2)
                    weigh(pe, s, p, 3)
                    weigh_rem(pe, s, p)
                each_step(pe, step)
                project_out(pe, seqs - 1)

            @block.vector
            def _(dve):
                dve.memset(ones_avg[:], 1.0 / D).then_inc(sem["const"], 1)
                dve.memset(ones[:], 1.0).then_inc(sem["const"], 1)
                dve.memset(eps[:], EPS)
                dve.memset(waited[:], 0.0).then_inc(sem["store"], 16)
                for i in range(2):
                    dve.memset(stacks[i][:, HEADS * T:].bitcast(F32), 0.0)
                dve.wait_ge(sem["weights"], 176)
                dve.tensor_copy(masks[:], masks_f[:]).then_inc(sem["const"], 1)
                dve.tensor_copy(ident[:], ident_f[:]).then_inc(sem["const"], 1)
                dve.tensor_copy(onehot[:], onehot_f[:]).then_inc(sem["const"], 2)
                dve.wait_ge(sem["absorb"], 1)
                for j in range(HPG):
                    last = dve.tensor_copy(wq_nope[:].rearrange("p t g (j r) -> p j (t g) r", j=HPG)[:, j],
                                           ps[:, j, 0:D].rearrange("p (a r) -> p a r", r=LAT))
                last.then_inc(sem["absorbed"], 1)
                dve.tensor_copy(wo[:], ps[:, 4:8, 0:D]).then_inc(sem["absorbed"], 1)
                centre(dve, 0, 0)
                rms_terms(dve, 0)
                rms_norm(dve, 0)
                turn(dve, 0)
                rotate(dve, 0, 0)
                nope_low(dve, 0)
                v_out(dve, 0, 0)
                centre(dve, 1, 1)
                rms_terms(dve, 1)
                rms_norm(dve, 1)

                def step(s, p, first, has_next, has_norm):
                    n, m = s + 1, s + 2
                    if has_next:
                        turn(dve, n)
                    maxima(dve, s, 0)
                    if has_next:
                        rotate(dve, n, 1 - p)
                    maxima(dve, s, 1)
                    if has_next:
                        nope_low(dve, n)
                    maxima(dve, s, 2)
                    maxima(dve, s, 3)
                    split_max(dve, s)
                    if has_next:
                        v_out(dve, n, 1 - p)
                    if not first:
                        residual(dve, s - 1, 1 - p)
                    if has_norm:
                        centre(dve, m, p)
                    weighed_out(dve, s, 0)
                    if has_norm:
                        rms_terms(dve, m)
                    weighed_out(dve, s, 1)
                    if has_norm:
                        rms_norm(dve, m)
                    weighed_out(dve, s, 2)
                    weighed_out(dve, s, 3)
                    weighed_rem_out(dve, s)
                each_step(dve, step)
                residual(dve, seqs - 1, 1)

            @block.scalar
            def _(act):
                act.preload_act_table_set("natural_log_exp_and_others")
                act.wait_ge(sem["const"], 6)
                square(act, 0)
                inv_std(act, 0)
                inv_mean_square(act, 0)
                rope_raw(act, 0)
                nope_high(act, 0)
                rope_short(act, 0, 0)
                rope_high(act, 0, 0)
                square(act, 1)
                inv_std(act, 1)
                inv_mean_square(act, 1)

                def step(s, p, first, has_next, has_norm):
                    n, m = s + 1, s + 2
                    cast(act, s, p, 0)
                    cast(act, s, p, 1)
                    if not first:
                        inv_sums(act, s - 1)
                    if has_next:
                        rope_raw(act, n)
                    cast(act, s, p, 2)
                    cast(act, s, p, 3)
                    if has_next:
                        nope_high(act, n)
                        rope_short(act, n, 1 - p)
                        rope_high(act, n, 1 - p)
                    max_rows(act, s)
                    exps(act, s, 0)
                    if has_norm:
                        square(act, m)
                    exps(act, s, 1)
                    if has_norm:
                        inv_std(act, m)
                    exps(act, s, 2)
                    if has_norm:
                        inv_mean_square(act, m)
                    exps(act, s, 3)
                    exps_rem(act, s)
                each_step(act, step)
                inv_sums(act, seqs - 1)

            @block.gpsimd
            def _(pool):
                add_tiles(pool, 0, 0)
                add_squares(pool, 0)
                layer_norm(pool, 0, 0)
                times_cos(pool, 0)
                rope_low(pool, 0, 0)
                keys_low(pool, 0, 0)
                add_tiles(pool, 1, 1)
                add_squares(pool, 1)

                def step(s, p, first, has_next, has_norm):
                    n, m = s + 1, s + 2
                    if not first:
                        divide(pool, s - 1)
                    if has_norm:
                        add_tiles(pool, m, p)
                    if has_next:
                        times_cos(pool, n)
                        layer_norm(pool, n, 1 - p)
                        rope_low(pool, n, 1 - p)
                    if has_norm:
                        add_squares(pool, m)
                    if has_next:
                        keys_low(pool, n, 1 - p)
                each_step(pool, step)
                divide(pool, seqs - 1)


def moe_phase(nc, dram, h1_scratch, x2_scratch, out_dram, tokens, width):
    chunks = tokens // width
    tiles = width // P
    with ExitStack() as ctx:
        sb = lambda name, shape, dt=F32: ctx.enter_context(nc.sbuf_tensor(name, shape, dt))
        raw_up = [sb(f"m_raw_up{i}", [P, DT, 2, INNER]) for i in range(2)]
        raw_down = [sb(f"m_raw_down{i}", [P, D]) for i in range(2)]
        up_parts = [sb(f"m_up{i}", [P, ALL_E, DT, 2, INNER], F32R) for i in range(2)]
        down_parts = [sb(f"m_down{i}", [P, ALL_E, D], F32R) for i in range(2)]
        w_gate = sb("m_w_gate", [P, DT, EXPERTS])
        gate_bias = sb("m_gate_bias", [P, EXPERTS])
        order = sb("m_order", [P, EXPERTS])
        w_ln = sb("m_w_ln", [P, DT])
        ident = sb("m_ident", [P, P])
        expert_rows_f = sb("m_expert_rows_f", [2 * EXPERTS, EXPERTS, P])
        expert_rows = sb("m_expert_rows", [2 * EXPERTS, EXPERTS, P], F32R)
        ones_avg = sb("m_ones_avg", [P, P])
        eps = sb("m_eps", [P, 1])
        x2 = [sb(f"m_x2{i}", [P, DT, width]) for i in range(2)]
        both = [sb(f"m_both{i}", [P, DT, width]) for i in range(2)]
        sq = sb("m_sq", [P, DT, width])
        sqs = sb("m_sqs", [P, width])
        ln_sq = sb("m_ln_sq", [P, width])
        rstd = sb("m_rstd", [P, width])
        xn = sb("m_xn", [P, DT, width])
        xn_parts = [[sb(f"m_xn{i}_{k}", [P, DT, width], F32R) for k in range(2)] for i in range(2)]
        small = lambda name, *shape: sb(f"m_{name}", [P, tiles, *shape])
        logit, is_top, rank, first = (small(w, EXPERTS) for w in ("logit", "is_top", "rank", "first"))
        others, is_second, rank2, second = (small(w, EXPERTS) for w in ("others", "is_second", "rank2", "second"))
        share1, share2, comb = (small(w, EXPERTS) for w in ("share1", "share2", "comb"))
        top, best, top2, best2 = (small(w) for w in ("top", "best", "top2", "best2"))
        diff, ratio, total, weight1, weight2 = (small(w) for w in ("diff", "ratio", "total", "weight1", "weight2"))
        comb_parts = sb("m_comb_parts", [P, tiles, 2, EXPERTS], F32R)
        comb_rows = [sb(f"m_comb_rows{i}", [2 * EXPERTS, width], F32R) for i in range(2)]
        silu = [sb(f"m_silu{i}", [P, width]) for i in range(2)]
        gated = sb("m_gated", [P, width])
        hidden = [sb(f"m_hidden{i}", [P, width]) for i in range(2)]
        hidden_parts = [[sb(f"m_hidden{i}_{k}", [P, width], F32R) for k in range(2)] for i in range(2)]
        out = [sb(f"m_out{i}", [P, DT, width]) for i in range(2)]
        y = [ctx.enter_context(nc.psum_tensor(f"m_y{t}", [P, 512], F32)) for t in range(DT)]
        gu = [[ctx.enter_context(nc.psum_tensor(f"m_gu{i}_{w}", [P, 512], F32)) for w in range(2)] for i in range(2)]
        share = ctx.enter_context(nc.psum_tensor("m_share", [P, 512], F32))
        misc = ctx.enter_context(nc.psum_tensor("m_misc", [P, 512], F32))
        sem = names(ctx, nc, "m", "weights raw0 raw1 split_hi split_lo const x2load h1load sq sqs mean lnsq rstd xn xnh xnl logits route diff ratio "
                    "combT rows gu share silu gated hidden hi lo down sum out store")
        ROUTE = 20
        places = range(ALL_E)

        def load_x2(sp, n, q):
            token = n * width
            need_all(sp, (sem["xn"], n - 1), (sem["sum"], n - 1), (sem["x2load"], 16 * n))
            sp.dma_start(x2[q][:], x2_scratch[:, :, bass.ds(token, width)]).then_inc(sem["x2load"], 16)

        def load_h1(sp, n, q):
            token = n * width
            need_all(sp, (sem["out"], n - 1), (sem["h1load"], 16 * n))
            sp.dma_start(both[q][:], h1_scratch[:, :, bass.ds(token, width)]).then_inc(sem["h1load"], 16)

        def store(sp, c, p):
            token = c * width
            need_all(sp, (sem["out"], c + 1), (sem["store"], 16 * (c + 1)))
            sp.dma_start(out_dram[:, :, bass.ds(token, width)], out[p][:]).then_inc(sem["store"], 16)

        def mean_square(pe, n):
            pe.wait_ge(sem["sqs"], n + 1)
            need(pe, sem["rows"], n)
            pe.matmul(misc[:, 0:width], ones_avg[:], sqs[:], start=True, stop=True).then_inc(sem["mean"], 1)

        def logits(pe, n):
            pe.wait_ge(sem["xn"], n + 1)
            pe.wait_ge(sem["lnsq"], n + 1)
            for i in range(tiles):
                for k in range(DT):
                    mm = pe.matmul(misc[:, i * EXPERTS:(i + 1) * EXPERTS], xn[:, k, i * P:(i + 1) * P], w_gate[:, k, :],
                                   start=(k == 0), stop=(k == DT - 1))
            mm.then_inc(sem["logits"], 1)

        def turn_shares(pe, n):
            pe.wait_ge(sem["route"], ROUTE * (n + 1))
            for i in range(tiles):
                mm = pe.matmul(misc[0:2 * EXPERTS, i * P:(i + 1) * P],
                               comb_parts[:, i].rearrange("p a e -> p (a e)").bitcast(F32), ident[:], start=True, stop=True)
            mm.then_inc(sem["combT"], 1)

        def gate_up(pe, c, p, i):
            if i == 0:
                pe.wait_ge(sem["xnh"], c + 1)
                pe.wait_ge(sem["xnl"], c + 1)
            need(pe, sem["hidden"], ALL_E * c + i - 1)
            b = (p + i) % 2
            for w in range(2):
                for j, (a, x) in enumerate(((0, 0), (0, 1), (1, 0))):
                    for k in range(DT):
                        mm = pe.matmul(gu[b][w][:, 0:width], up_parts[a][:, i, k, w, :], xn_parts[p][x][:, k, :],
                                       start=(j == 0 and k == 0), stop=(j == 2 and k == DT - 1))
            mm.then_inc(sem["gu"], 1)

        def spread_share(pe, c, p, i):
            pe.wait_ge(sem["rows"], c + 1)
            need(pe, sem["hidden"], ALL_E * c + i)
            pe.matmul(share[:, 0:width], expert_rows[:, i - 1, :], comb_rows[p][:], start=True, stop=True).then_inc(sem["share"], 1)

        def down(pe, c, p, i):
            pe.wait_ge(sem["hi"], ALL_E * c + i + 1)
            if i == 0:
                need(pe, sem["out"], c)
            b = (p + i) % 2
            parts = ((0, 0), (1, 0), (0, 1))
            for j, (a, x) in enumerate(parts):
                if j == 2:
                    pe.wait_ge(sem["lo"], ALL_E * c + i + 1)
                for t in range(DT):
                    mm = pe.matmul(y[t][:, 0:width], down_parts[a][:, i, t * P:(t + 1) * P], hidden_parts[b][x][:],
                                   start=(i == 0 and j == 0), stop=(i == ALL_E - 1 and j == 2))
            mm.then_inc(sem["down"], 1)

        def normalise(dve, n, q):
            dve.wait_ge(sem["rstd"], n + 1)
            need(dve, sem["logits"], n)
            need(dve, sem["xnl"], n)
            for t in range(DT):
                last = dve.scalar_tensor_tensor(out=xn[:, t, :], in0=x2[q][:, t, :], scalar=w_ln[:, t:t + 1], in1=rstd[:],
                                                op0=ALU.mult, op1=ALU.mult)
            last.then_inc(sem["xn"], 1)

        def weights_low(dve, i):
            dve.wait_ge(sem["split_hi"], i + 1)
            dve.tensor_tensor(up_parts[1][:, i], raw_up[i % 2][:], up_parts[0][:, i].bitcast(F32), ALU.subtract)
            dve.tensor_tensor(down_parts[1][:, i], raw_down[i % 2][:], down_parts[0][:, i].bitcast(F32),
                              ALU.subtract).then_inc(sem["split_lo"], 1)

        def choose(dve, n):
            r = ROUTE * n
            route = sem["route"]
            dve.wait_ge(sem["logits"], n + 1)
            need(dve, sem["combT"], n)
            at = misc[:, 0:tiles * EXPERTS].rearrange("p (i e) -> p i e", e=EXPERTS)
            dve.tensor_tensor(logit[:], at, spread(gate_bias[:], 1, tiles), ALU.add).then_inc(route, 1)
            dve.wait_ge(route, r + 1)
            dve.tensor_reduce(top[:], logit[:], AX.X, ALU.max).then_inc(route, 1)
            dve.wait_ge(route, r + 2)
            dve.tensor_tensor(is_top[:], logit[:], spread(top[:], 2, EXPERTS), ALU.is_equal).then_inc(route, 1)
            dve.wait_ge(route, r + 3)
            dve.tensor_tensor(rank[:], is_top[:], spread(order[:], 1, tiles), ALU.mult).then_inc(route, 1)
            dve.wait_ge(route, r + 4)
            dve.tensor_reduce(best[:], rank[:], AX.X, ALU.max).then_inc(route, 1)
            dve.wait_ge(route, r + 5)
            dve.tensor_tensor(first[:], rank[:], spread(best[:], 2, EXPERTS), ALU.is_equal).then_inc(route, 1)
            dve.wait_ge(route, r + 6)
            dve.scalar_tensor_tensor(out=others[:], in0=first[:], scalar=NEG, in1=logit[:], op0=ALU.mult, op1=ALU.add).then_inc(route, 1)
            dve.wait_ge(route, r + 7)
            dve.tensor_reduce(top2[:], others[:], AX.X, ALU.max).then_inc(route, 1)
            dve.wait_ge(route, r + 8)
            dve.tensor_tensor(diff[:], top2[:], top[:], ALU.subtract).then_inc(sem["diff"], 1)
            dve.tensor_tensor(is_second[:], others[:], spread(top2[:], 2, EXPERTS), ALU.is_equal).then_inc(route, 1)
            dve.wait_ge(route, r + 9)
            dve.tensor_tensor(rank2[:], is_second[:], spread(order[:], 1, tiles), ALU.mult).then_inc(route, 1)
            dve.wait_ge(route, r + 10)
            dve.tensor_reduce(best2[:], rank2[:], AX.X, ALU.max).then_inc(route, 1)
            dve.wait_ge(route, r + 11)
            dve.tensor_tensor(second[:], rank2[:], spread(best2[:], 2, EXPERTS), ALU.is_equal).then_inc(route, 1)

        def shares(dve, n):
            r = ROUTE * n
            route = sem["route"]
            dve.wait_ge(sem["ratio"], n + 1)
            dve.tensor_scalar(total[:], ratio[:], 1.0, None, ALU.add).then_inc(route, 1)
            dve.wait_ge(route, r + 13)
            dve.reciprocal(weight1[:], total[:]).then_inc(route, 1)
            dve.wait_ge(route, r + 14)
            dve.tensor_tensor(weight2[:], ratio[:], weight1[:], ALU.mult).then_inc(route, 1)
            dve.tensor_tensor(share1[:], first[:], spread(weight1[:], 2, EXPERTS), ALU.mult).then_inc(route, 1)
            dve.wait_ge(route, r + 16)
            dve.tensor_tensor(share2[:], second[:], spread(weight2[:], 2, EXPERTS), ALU.mult).then_inc(route, 1)
            dve.wait_ge(route, r + 17)
            dve.tensor_tensor(comb[:], share1[:], share2[:], ALU.add).then_inc(route, 1)
            dve.wait_ge(route, r + 18)
            dve.tensor_copy(comb_parts[:, :, 0, :], comb[:]).then_inc(route, 1)
            dve.wait_ge(route, r + 19)
            dve.tensor_tensor(comb_parts[:, :, 1, :], comb[:], comb_parts[:, :, 0, :].bitcast(F32), ALU.subtract).then_inc(route, 1)

        def gate(dve, c, p, i):
            b = (p + i) % 2
            dve.wait_ge(sem["silu"], ALL_E * c + i + 1)
            need(dve, sem["lo"], ALL_E * c + i - 1)
            if i == 0:
                dve.tensor_tensor(hidden[b][:], gu[b][1][:, 0:width], silu[b][:], ALU.mult).then_inc(sem["hidden"], 1)
                return
            dve.tensor_tensor(gated[:], gu[b][1][:, 0:width], silu[b][:], ALU.mult).then_inc(sem["gated"], 1)
            dve.wait_ge(sem["gated"], EXPERTS * c + i)
            dve.wait_ge(sem["share"], EXPERTS * c + i)
            dve.tensor_tensor(hidden[b][:], gated[:], share[:, 0:width], ALU.mult).then_inc(sem["hidden"], 1)

        def finish(dve, c, p):
            dve.wait_ge(sem["down"], ALL_E * (c + 1))
            dve.wait_ge(sem["sum"], c + 1)
            need(dve, sem["store"], 16 * (c + 1))
            for t in range(DT):
                last = dve.tensor_tensor(out[p][:, t, :], y[t][:, 0:width], both[p][:, t, :], ALU.add)
            last.then_inc(sem["out"], 1)

        def square(act, n, q):
            act.wait_ge(sem["x2load"], 16 * (n + 1))
            act.activation(sq[:], x2[q][:], ACT.Square).then_inc(sem["sq"], 1)

        def inv_rms(act, n):
            act.wait_ge(sem["mean"], n + 1)
            act.activation(ln_sq[:], misc[:, 0:width], ACT.Ln, bias=eps[:]).then_inc(sem["lnsq"], 1)
            act.wait_ge(sem["lnsq"], n + 1)
            act.activation(rstd[:], ln_sq[:], ACT.Exp, scale=-0.5).then_inc(sem["rstd"], 1)

        def norm_high(act, n, q):
            act.wait_ge(sem["xn"], n + 1)
            need(act, sem["gu"], ALL_E * (n - 1))
            act.activation(xn_parts[q][0][:], xn[:], ACT.Copy).then_inc(sem["xnh"], 1)

        def weights_high(act, i):
            act.wait_ge(sem[f"raw{i % 2}"], 32 * (i // 2 + 1))
            act.activation(up_parts[0][:, i], raw_up[i % 2][:], ACT.Copy)
            act.activation(down_parts[0][:, i], raw_down[i % 2][:], ACT.Copy).then_inc(sem["split_hi"], 1)

        def share_ratio(act, n):
            act.wait_ge(sem["diff"], n + 1)
            act.activation(ratio[:], diff[:], ACT.Exp).then_inc(sem["ratio"], 1)

        def share_rows(act, n, q):
            act.wait_ge(sem["combT"], n + 1)
            need(act, sem["share"], EXPERTS * (n - 1))
            act.activation(comb_rows[q][:], misc[0:2 * EXPERTS, 0:width], ACT.Copy).then_inc(sem["rows"], 1)

        def silu_gate(act, c, p, i):
            b = (p + i) % 2
            act.wait_ge(sem["gu"], ALL_E * c + i + 1)
            act.activation(silu[b][:], gu[b][0][:, 0:width], ACT.Silu).then_inc(sem["silu"], 1)

        def hidden_high(act, c, p, i):
            b = (p + i) % 2
            act.wait_ge(sem["hidden"], ALL_E * c + i + 1)
            need(act, sem["down"], ALL_E * c + i - 1)
            act.activation(hidden_parts[b][0][:], hidden[b][:], ACT.Copy).then_inc(sem["hi"], 1)

        def add_squares(pool, n):
            pool.wait_ge(sem["sq"], n + 1)
            pool.tensor_tensor(sqs[:], sq[:, 0, :], sq[:, 1, :], ALU.add).then_inc(sem["sqs"], 1)

        def norm_low(pool, n, q):
            pool.wait_ge(sem["xnh"], n + 1)
            pool.tensor_tensor(xn_parts[q][1][:], xn[:], xn_parts[q][0][:].bitcast(F32), ALU.subtract).then_inc(sem["xnl"], 1)

        def add_residuals(pool, n, q):
            pool.wait_ge(sem["h1load"], 16 * (n + 1))
            pool.tensor_tensor(both[q][:], both[q][:], x2[q][:], ALU.add).then_inc(sem["sum"], 1)

        def hidden_low(pool, c, p, i):
            b = (p + i) % 2
            pool.wait_ge(sem["hi"], ALL_E * c + i + 1)
            pool.tensor_tensor(hidden_parts[b][1][:], hidden[b][:], hidden_parts[b][0][:].bitcast(F32),
                               ALU.subtract).then_inc(sem["lo"], 1)

        def each_step(engine, step):
            step(0, 0, True, False)
            if chunks > 2:
                with engine.Fori(0, (chunks - 2) // 2) as i:
                    step(i * 2 + 1, 1, False, False)
                    step(i * 2 + 2, 0, False, False)
            step(chunks - 1, 1, False, True)

        LOADS = 16 * 6
        with nc.Block() as block:

            @block.sync
            def _(sp):
                for dst, name in ((w_gate, "w_gate"), (gate_bias, "gate_bias"), (order, "order"), (w_ln, "w_ln2"),
                                  (ident, "ident"), (expert_rows_f, "expert_rows")):
                    sp.dma_start(dst[:], dram[name]).then_inc(sem["weights"], 16)
                load_x2(sp, 0, 0)
                for i in places:
                    need(sp, sem["split_lo"], i - 1)
                    sp.dma_start(raw_up[i % 2][:], dram["up"][:, i]).then_inc(sem[f"raw{i % 2}"], 16)
                    sp.dma_start(raw_down[i % 2][:], dram["down"][:, i]).then_inc(sem[f"raw{i % 2}"], 16)
                    if i == 1:
                        load_h1(sp, 0, 0)
                        load_x2(sp, 1, 1)
                        load_h1(sp, 1, 1)

                def step(c, p, is_first, is_last):
                    if not (is_first or is_last):
                        load_x2(sp, c + 1, 1 - p)
                        load_h1(sp, c + 1, 1 - p)
                    if not is_first:
                        store(sp, c - 1, 1 - p)
                each_step(sp, step)
                store(sp, chunks - 1, 1)
                sp.wait_ge(sem["store"], 16 * (chunks + 1))

            @block.tensor
            def _(pe):
                pe.wait_ge(sem["const"], 3)
                pe.wait_ge(sem["weights"], LOADS)
                mean_square(pe, 0)
                logits(pe, 0)
                turn_shares(pe, 0)

                def step(c, p, is_first, is_last):
                    for i in places:
                        if is_first:
                            pe.wait_ge(sem["split_lo"], i + 1)
                        gate_up(pe, c, p, i)
                        if i > 0:
                            spread_share(pe, c, p, i)
                        if i >= 2:
                            down(pe, c, p, i - 2)
                        elif not is_first:
                            down(pe, c - 1, 1 - p, ALL_E - 2 + i)
                        if not is_last:
                            if i == 1:
                                mean_square(pe, c + 1)
                            if i == 4:
                                logits(pe, c + 1)
                            if i == 6:
                                turn_shares(pe, c + 1)
                each_step(pe, step)
                for i in (ALL_E - 2, ALL_E - 1):
                    down(pe, chunks - 1, 1, i)

            @block.vector
            def _(dve):
                dve.memset(ones_avg[:], 1.0 / D).then_inc(sem["const"], 1)
                dve.memset(eps[:], EPS).then_inc(sem["const"], 1)
                dve.memset(ratio[:], 0.0).then_inc(sem["store"], 16)
                dve.wait_ge(sem["weights"], LOADS)
                dve.tensor_copy(expert_rows[:], expert_rows_f[:]).then_inc(sem["const"], 1)
                normalise(dve, 0, 0)
                weights_low(dve, 0)
                choose(dve, 0)
                shares(dve, 0)
                weights_low(dve, 1)

                def step(c, p, is_first, is_last):
                    for i in places:
                        gate(dve, c, p, i)
                        if is_first and i + 2 < ALL_E:
                            weights_low(dve, i + 2)
                        if i == 1 and not is_first:
                            finish(dve, c - 1, 1 - p)
                        if not is_last:
                            if i == 2:
                                normalise(dve, c + 1, 1 - p)
                            if i == 4:
                                choose(dve, c + 1)
                            if i == 5:
                                shares(dve, c + 1)
                each_step(dve, step)
                finish(dve, chunks - 1, 1)

            @block.scalar
            def _(act):
                act.preload_act_table_set("natural_log_exp_and_others")
                act.wait_ge(sem["const"], 2)
                square(act, 0, 0)
                inv_rms(act, 0)
                norm_high(act, 0, 0)
                weights_high(act, 0)
                share_ratio(act, 0)
                weights_high(act, 1)
                share_rows(act, 0, 0)
                act.preload_act_table_set("silu_and_others")

                def step(c, p, is_first, is_last):
                    if not is_last:
                        square(act, c + 1, 1 - p)
                    for i in places:
                        if is_first and i + 2 < ALL_E:
                            weights_high(act, i + 2)
                        silu_gate(act, c, p, i)
                        hidden_high(act, c, p, i)
                        if not is_last:
                            if i == 1:
                                act.preload_act_table_set("natural_log_exp_and_others")
                                inv_rms(act, c + 1)
                                act.preload_act_table_set("silu_and_others")
                            if i == 3:
                                norm_high(act, c + 1, 1 - p)
                            if i == 4:
                                act.preload_act_table_set("natural_log_exp_and_others")
                                share_ratio(act, c + 1)
                                act.preload_act_table_set("silu_and_others")
                            if i == 6:
                                share_rows(act, c + 1, 1 - p)
                each_step(act, step)

            @block.gpsimd
            def _(pool):
                add_squares(pool, 0)
                norm_low(pool, 0, 0)
                add_residuals(pool, 0, 0)

                def step(c, p, is_first, is_last):
                    if not is_last:
                        add_squares(pool, c + 1)
                    for i in places:
                        hidden_low(pool, c, p, i)
                        if not is_last:
                            if i == 3:
                                norm_low(pool, c + 1, 1 - p)
                            if i == 5:
                                add_residuals(pool, c + 1, 1 - p)
                each_step(pool, step)


def host_layouts(a):
    f = {}
    seqs = a["x"].shape[0]

    def feature_tiles(w):
        return w.reshape(-1, P, w.shape[-1]).transpose(1, 0, 2)

    def column(v):
        return v.reshape(-1, P).T

    n = 4
    patches = a["x"].reshape(seqs, 3, n, 16, n, 16).transpose(1, 3, 5, 0, 2, 4).reshape(FEAT, seqs * n * n)
    f["patches"] = feature_tiles(patches)
    f["txt"] = a["txt"].transpose(2, 0, 1).reshape(DT, P, seqs, TXT_TOK).transpose(1, 2, 0, 3).reshape(P, -1)
    f["tok_w"] = feature_tiles(a["L0_tok_W"].T)
    f["tok_b"] = column(a["L0_tok_b"])
    f["pos"] = feature_tiles(a["L0_tok_pos_emb"].T)
    w = a["L0_attn_qkv_w"].T.reshape(D, HEADS, 3, HD1)
    b = a["L0_attn_qkv_b"].reshape(HEADS, 3, HD1)
    f["wqk"] = feature_tiles(w[:, :, 0:2].reshape(D, 2 * D)).reshape(P, DT, GROUPS, P)
    f["bqk"] = column(b[:, 0:2].ravel())
    f["wv"] = feature_tiles(w[:, :, 2].reshape(D, D))
    f["bv"] = np.broadcast_to(b[:, 2].reshape(1, D), (P, D))
    fcw = np.zeros((HPG, Q, GROUPS, D), np.float32)
    fcw[:, :HD1] = a["L0_attn_fc_w"].T.reshape(GROUPS, HPG, HD1, D).transpose(1, 2, 0, 3)
    f["fcw"] = fcw.reshape(P, GROUPS, D)
    f["fcb"] = column(a["L0_attn_fc_b"])
    f["w_ln1"] = column(a["L0_ffn_w_ln1"])
    wq = a["L0_ffn_Wq"].reshape(D, GROUPS, HPG, 2, NOPE)
    f["wqn_t"] = wq[:, :, :, 0].transpose(2, 3, 1, 0).reshape(P, GROUPS, D)
    f["wq_rope"] = feature_tiles(wq[:, :, :, 1].reshape(D, GROUPS * P)).reshape(P, DT, GROUPS, P)
    wkb = a["L0_ffn_Wkvb"].reshape(LAT, GROUPS, HPG, NOPE)
    f["wkb_t"] = wkb.transpose(2, 3, 1, 0).reshape(P, GROUPS, LAT)
    f["wo_n"] = a["L0_ffn_Wo"].reshape(GROUPS, HPG, 2, NOPE, D)[:, :, 0].transpose(1, 2, 0, 3).reshape(P, GROUPS, D)
    f["wkva"] = feature_tiles(np.concatenate([a["L0_ffn_Wkva"]] * 2, 1))
    f["w_ln2"] = column(a["L0_ffn_w_ln2"])
    f["w_gate"] = feature_tiles(a["L0_ffn_Wgate"])
    f["gate_bias"] = np.broadcast_to(a["L0_ffn_expert_bias"][None], (P, EXPERTS))
    up = np.stack([np.concatenate([a["L0_ffn_s" + w], a["L0_ffn_" + w]]) for w in ("Wg", "Wu")])
    f["up"] = up.reshape(2, ALL_E, DT, P, INNER).transpose(3, 1, 2, 0, 4)
    f["down"] = np.concatenate([a["L0_ffn_sWd"], a["L0_ffn_Wd"]]).transpose(1, 0, 2)
    f["order"] = np.broadcast_to(np.arange(EXPERTS, 0, -1, dtype=np.float32)[None], (P, EXPERTS))
    owner = np.arange(2 * EXPERTS)[:, None] % EXPERTS == np.arange(EXPERTS)[None]
    f["expert_rows"] = np.broadcast_to(owner.astype(np.float32)[:, :, None], (2 * EXPERTS, EXPERTS, P))
    half = np.arange(0, ROPE, 2, dtype=np.float32) / np.float32(ROPE)
    angle = np.outer(np.arange(T, dtype=np.float32), np.float32(1.0) / np.float32(100000.0) ** half).astype(np.float32)
    cos, sin = (np.repeat(c(angle).T, 2, 0).astype(np.float32) for c in (np.cos, np.sin))
    sin[0::2] *= -1
    cos_tiles, sin_tiles = np.ones((P, HPG + 1, T), np.float32), np.zeros((P, HPG + 1, T), np.float32)
    for quadrant in range(4):
        r = slice(Q * quadrant, Q * quadrant + Q)
        cos_tiles[r, :HPG], sin_tiles[r, :HPG] = cos[:, None], sin[:, None]
        if quadrant % 2:
            cos_tiles[r, HPG], sin_tiles[r, HPG] = cos, sin
    f["rope_cos"], f["rope_sin"] = cos_tiles, sin_tiles
    one, two = np.arange(P)[:, None], np.arange(P)[None, :]
    masks = np.zeros((P, 2 * P + T + REM), np.float32)
    masks[:, 0:P][two > one] = NEG
    masks[:, P:2 * P][one > two] = NEG
    last = np.where(one % Q < REM, P + one % Q, T)
    masks[:, 2 * P:2 * P + T][np.arange(T)[None, :] > last] = NEG
    masks[:REM, 2 * P + T:][one[:REM] > two[:, :REM]] = NEG
    f["masks"] = masks
    row, place = np.arange(2 * (HEADS + GROUPS))[:, None] % (HEADS + GROUPS), np.arange(HEADS + GROUPS)[None, :]
    f["onehot2"] = np.broadcast_to((row == place).astype(np.float32)[:, :, None], (40, HEADS + GROUPS, P))
    rows = np.arange(P)
    f["rem_mask"] = (rows % Q < REM).astype(np.float32)[:, None]
    f["ident"] = np.eye(P, dtype=np.float32)
    cols = np.arange(HEADS + GROUPS)
    owns = np.zeros((HEADS + GROUPS, HEADS), np.float32)
    for h in range(HEADS):
        owns[h, h] = owns[HEADS + h // HPG, h] = 1
    f["onehot1"] = np.broadcast_to(np.concatenate([owns, owns])[:, :, None], (40, HEADS, P))
    rem = np.zeros((41, HEADS, Q), np.float32)
    rem[:40, :, :REM] = np.concatenate([owns, owns])[:, :, None]
    rem[40, :, REM:] = NEG
    f["onehot1_rem"] = rem
    main = np.concatenate([cols < HEADS] * 2)
    f["nt_rows"] = np.stack([main, ~main], 1).astype(np.float32)
    return {k: np.ascontiguousarray(v) for k, v in f.items()}


def build(nc, dram, out, seqs):
    h1 = nc.dram_tensor("h1_scratch", [P, DT, seqs * T], F32).ap()
    x2 = nc.dram_tensor("x2_scratch", [P, DT, seqs * T], F32).ap()
    with nc.sbuf_tensor("embedded", [P, DT, seqs * IMG_TOK], F32) as embedded:
        embed_phase(nc, dram, embedded, seqs)
        attn1_phase(nc, dram, embedded, h1, seqs)
    attn2_phase(nc, dram, h1, x2, seqs)
    moe_phase(nc, dram, h1, x2, out, seqs * T, CHUNK)


def kernel(**inputs):
    import concourse.bacc as bacc
    from concourse.bass_utils import run_bass_kernel_spmd

    laid = host_layouts({name: np.asarray(value) for name, value in inputs.items()})
    nc = bacc.Bacc("TRN2", target_bir_lowering=False, num_devices=1)
    arrays = {f"in_{name}": value for name, value in laid.items()}
    dram = {name: nc.dram_tensor(f"in_{name}", value.shape, F32, kind="ExternalInput").ap() for name, value in laid.items()}
    out = nc.dram_tensor("out", [P, DT, SEQS * T], F32, kind="ExternalOutput").ap()
    build(nc, dram, out, SEQS)
    result = run_bass_kernel_spmd(nc, [arrays], core_ids=[0])
    got = np.asarray(result.results[0]["out"])
    return np.ascontiguousarray(got.reshape(P, DT, SEQS, T).transpose(2, 3, 1, 0)).reshape(SEQS, T, D)
```
